# Optimizing a Trainium2 kernel written in Bass

```python
import numpy as np
import jax
import jax.numpy as jnp

def _softmax(x, axis=-1):
    return jax.nn.softmax(x, axis=axis)

def _gelu(x):
    return jax.nn.gelu(x, approximate=True)

def _silu(x):
    return jax.nn.silu(x)

def _sigmoid(x):
    return jax.nn.sigmoid(x)

def _layernorm(x, axis=-1, eps=1e-05):
    m = jnp.mean(x, axis=axis, keepdims=True)
    v = jnp.var(x, axis=axis, keepdims=True)
    return (x - m) / jnp.sqrt(v + eps)

def _scatter_add(tgt, idx, src, axis=0):
    return tgt.at[idx].add(src)

def _segment_sum(src, seg, n):
    return jax.ops.segment_sum(src, seg, n)
kernel_name = 'mk_gnn_ffn_d2_gnn_r16_4626be'

def setup_inputs(seed: int=0):
    np.random.seed(seed)
    _w = jnp.asarray

    def _rec_inputs():
        import jax
        import jax.numpy as jnp
        _gk = jax.random.key(seed)
        x = -0.0003713 + 1 * jax.random.normal(jax.random.fold_in(_gk, 1), (3125, 256), jnp.float32)
        _s = jax.random.randint(jax.random.fold_in(_gk, 2), (25000,), 0, 3125, jnp.int32)
        _d = jax.random.randint(jax.random.fold_in(_gk, 3), (25000,), 0, 3125, jnp.int32)
        _loop = jnp.arange(3125, dtype=jnp.int32)
        src = jnp.concatenate([_s, _d, _loop])
        dst = jnp.concatenate([_d, _s, _loop])
        _o = jnp.argsort(dst, stable=True)
        src = src[_o]
        dst = dst[_o]
        return (x, src, dst)
    x, src, dst = _rec_inputs()

    def _L0_gnn_setup():
        import jax, jax.numpy as jnp
        import numpy as np
        N, E, D_IN, D_OUT = (3125, 100000, 256, 256)
        key = jax.random.key(seed)
        k1, k2, k3, k4, k5, k6 = jax.random.split(key, 6)
        x = jax.random.normal(k1, (N, D_IN), dtype=jnp.float32)
        edge_index = jax.random.randint(k2, (2, E), 0, N, dtype=jnp.int64)
        s = 1.0 / np.sqrt(D_IN)
        W1 = jax.random.uniform(k3, (D_OUT, D_IN), minval=-s, maxval=s, dtype=jnp.float32)
        b1 = jax.random.uniform(k4, (D_OUT,), minval=-s, maxval=s, dtype=jnp.float32)
        W2 = jax.random.uniform(k5, (D_OUT, D_IN), minval=-s, maxval=s, dtype=jnp.float32)
        b2 = jax.random.uniform(k6, (D_OUT,), minval=-s, maxval=s, dtype=jnp.float32)
        return {'x': x, 'W1': W1, 'b1': b1, 'W2': W2, 'b2': b2, 'edge_index': edge_index}
    _L0_gnn_all = _L0_gnn_setup()
    _L0_gnn_in = {k: v for k, v in _L0_gnn_all.items() if k in ('W1', 'b1', 'W2', 'b2')}
    del _L0_gnn_all

    def _L0_ffn_setup():
        import jax, jax.numpy as jnp
        import numpy as np
        TOP_K = 2
        LN_EPS = 1e-05
        key = jax.random.key(seed)
        ks = jax.random.split(key, 8)
        B, S, D, E, H = (16, 1024, 256, 8, 1024)
        x = jax.random.normal(ks[0], (B, S, D), dtype=jnp.float32)
        Wr = jax.random.normal(ks[1], (D, E), dtype=jnp.float32) * 0.1
        br = jnp.zeros((E,), dtype=jnp.float32)
        ln_g = jnp.ones((E, D), dtype=jnp.float32)
        ln_b = jnp.zeros((E, D), dtype=jnp.float32)
        W1 = jax.random.normal(ks[2], (E, D, H), dtype=jnp.float32) * (1.0 / np.sqrt(D))
        b1 = jnp.zeros((E, H), dtype=jnp.float32)
        W2 = jax.random.normal(ks[3], (E, H, D), dtype=jnp.float32) * (1.0 / np.sqrt(H))
        b2 = jnp.zeros((E, D), dtype=jnp.float32)
        return {'x': x, 'Wr': Wr, 'br': br, 'ln_g': ln_g, 'ln_b': ln_b, 'W1': W1, 'b1': b1, 'W2': W2, 'b2': b2}
    _L0_ffn_all = _L0_ffn_setup()
    _L0_ffn_in = {k: v for k, v in _L0_ffn_all.items() if k in ('Wr', 'br', 'ln_g', 'ln_b', 'W1', 'b1', 'W2', 'b2')}
    del _L0_ffn_all

    def _L1_gnn_setup():
        import jax, jax.numpy as jnp
        import numpy as np
        N_NODES = 3125
        N_EDGES = 50000
        IN_F = 256
        HEADS = 8
        D = 32
        ALPHA_SLOPE = 0.2
        EPS = 1e-16
        key = jax.random.key(seed)
        k1, k2, k3, k4, k5 = jax.random.split(key, 5)
        x = jax.random.normal(k1, (N_NODES, IN_F), dtype=jnp.float32)
        W = jax.random.normal(k2, (HEADS, IN_F, D), dtype=jnp.float32) * 0.05
        a = jax.random.normal(k3, (HEADS, 5 * D), dtype=jnp.float32) * 0.05
        src = jax.random.randint(k4, (N_EDGES,), 0, N_NODES, dtype=jnp.int32)
        dst = jax.random.randint(k5, (N_EDGES,), 0, N_NODES, dtype=jnp.int32)
        return {'x': x, 'W': W, 'a': a, 'src': src, 'dst': dst}
    _L1_gnn_all = _L1_gnn_setup()
    _L1_gnn_in = {k: v for k, v in _L1_gnn_all.items() if k in ('W', 'a')}
    del _L1_gnn_all

    def _L1_ffn_setup():
        import jax, jax.numpy as jnp
        import numpy as np
        B, S, H, F, E, K = (8, 256, 256, 512, 16, 2)
        EPS = 1e-05
        key = jax.random.key(seed)
        ks = jax.random.split(key, 9)
        sc = 0.02
        return {'x': jax.random.normal(ks[0], (B, S, H), dtype=jnp.float32), 'gate_w': jax.random.normal(ks[1], (H, E), dtype=jnp.float32) * sc, 'gate_b': jnp.zeros((E,), dtype=jnp.float32), 'w1': jax.random.normal(ks[2], (E, H, F), dtype=jnp.float32) * sc, 'b1': jnp.zeros((E, F), dtype=jnp.float32), 'w2': jax.random.normal(ks[3], (E, F, H), dtype=jnp.float32) * sc, 'b2': jnp.zeros((E, H), dtype=jnp.float32), 'gamma': jnp.ones((H,), dtype=jnp.float32), 'beta': jnp.zeros((H,), dtype=jnp.float32)}
    _L1_ffn_all = _L1_ffn_setup()
    _L1_ffn_in = {k: v for k, v in _L1_ffn_all.items() if k in ('gate_w', 'gate_b', 'w1', 'b1', 'w2', 'b2', 'gamma', 'beta')}
    del _L1_ffn_all
    return {'x': x, 'src': src, 'dst': dst, 'L0_gnn_W1': _L0_gnn_in['W1'], 'L0_gnn_b1': _L0_gnn_in['b1'], 'L0_gnn_W2': _L0_gnn_in['W2'], 'L0_gnn_b2': _L0_gnn_in['b2'], 'L0_ffn_Wr': _L0_ffn_in['Wr'], 'L0_ffn_br': _L0_ffn_in['br'], 'L0_ffn_ln_g': _L0_ffn_in['ln_g'], 'L0_ffn_ln_b': _L0_ffn_in['ln_b'], 'L0_ffn_W1': _L0_ffn_in['W1'], 'L0_ffn_b1': _L0_ffn_in['b1'], 'L0_ffn_W2': _L0_ffn_in['W2'], 'L0_ffn_b2': _L0_ffn_in['b2'], 'L1_gnn_W': _L1_gnn_in['W'], 'L1_gnn_a': _L1_gnn_in['a'], 'L1_ffn_gate_w': _L1_ffn_in['gate_w'], 'L1_ffn_gate_b': _L1_ffn_in['gate_b'], 'L1_ffn_w1': _L1_ffn_in['w1'], 'L1_ffn_b1': _L1_ffn_in['b1'], 'L1_ffn_w2': _L1_ffn_in['w2'], 'L1_ffn_b2': _L1_ffn_in['b2'], 'L1_ffn_gamma': _L1_ffn_in['gamma'], 'L1_ffn_beta': _L1_ffn_in['beta']}

def reference(x, src, dst, L0_gnn_W1, L0_gnn_b1, L0_gnn_W2, L0_gnn_b2, L0_ffn_Wr, L0_ffn_br, L0_ffn_ln_g, L0_ffn_ln_b, L0_ffn_W1, L0_ffn_b1, L0_ffn_W2, L0_ffn_b2, L1_gnn_W, L1_gnn_a, L1_ffn_gate_w, L1_ffn_gate_b, L1_ffn_w1, L1_ffn_b1, L1_ffn_w2, L1_ffn_b2, L1_ffn_gamma, L1_ffn_beta):
    import jax
    import jax.numpy as jnp

    def _L0_gnn_ref(x, W1, b1, W2, b2, edge_index):
        import jax, jax.numpy as jnp
        import numpy as np
        N, E, D_IN, D_OUT = (3125, 100000, 256, 256)
        dst = edge_index[0]
        nbr = edge_index[1]
        n = x.shape[0]
        agg = jax.ops.segment_sum(x[nbr], dst, num_segments=n)
        cnt = jax.ops.segment_sum(jnp.ones((nbr.shape[0],), x.dtype), dst, num_segments=n)
        mean = agg / jnp.maximum(cnt, 1.0)[:, None]
        return x @ W1.T + b1 + mean @ W2.T + b2

    def _L0_ffn_ref(x, Wr, br, ln_g, ln_b, W1, b1, W2, b2):
        import jax, jax.numpy as jnp
        import numpy as np
        TOP_K = 2
        LN_EPS = 1e-05
        B, S, D = x.shape
        N = B * S
        xt = x.reshape(N, D)
        logits = xt @ Wr + br
        probs = jax.nn.softmax(logits, axis=-1)
        top_p, top_idx = jax.lax.top_k(probs, TOP_K)
        weights = top_p / top_p.sum(axis=-1, keepdims=True)
        mu = xt.mean(axis=-1, keepdims=True)
        var = ((xt - mu) ** 2).mean(axis=-1, keepdims=True)
        xn = (xt - mu) * jax.lax.rsqrt(var + LN_EPS)
        xe = xn[None, :, :] * ln_g[:, None, :] + ln_b[:, None, :]
        h = jax.nn.gelu(jnp.einsum('end,edh->enh', xe, W1) + b1[:, None, :], approximate=False)
        y = jnp.einsum('enh,ehd->end', h, W2) + b2[:, None, :]
        y_tok = jnp.transpose(y, (1, 0, 2))
        sel = jnp.take_along_axis(y_tok, top_idx[:, :, None], axis=1)
        out = (weights[:, :, None] * sel).sum(axis=1)
        return out.reshape(B, S, D)

    def _L1_gnn_ref(x, W, a, src, dst):
        import jax, jax.numpy as jnp
        import numpy as np
        N_NODES = 3125
        N_EDGES = 50000
        IN_F = 256
        HEADS = 8
        D = 32
        ALPHA_SLOPE = 0.2
        EPS = 1e-16
        n = x.shape[0]
        h = jnp.einsum('ni,hio->nho', x, W)
        hs = h[src]
        hd = h[dst]
        diff = hd - hs
        a1, a2, a3, a4, a5 = jnp.split(a, 5, axis=1)
        lin = jnp.einsum('ehd,hd->eh', hs, a1) + jnp.einsum('ehd,hd->eh', hd, a2) + jnp.einsum('ehd,hd->eh', diff, a3) + jnp.einsum('ehd,hd->eh', jnp.abs(diff), a4) + jnp.einsum('ehd,hd->eh', hs * hd, a5)
        alpha = jnp.where(lin > 0, lin, ALPHA_SLOPE * lin)
        mx = jax.ops.segment_max(alpha, src, num_segments=n)
        e = jnp.exp(alpha - mx[src])
        s = jax.ops.segment_sum(e, src, num_segments=n)
        att = e / (s[src] + EPS)
        out = jax.ops.segment_sum(att[..., None] * hd, src, num_segments=n)
        return out.reshape(n, HEADS * D)

    def _L1_ffn_ref(x, gate_w, gate_b, w1, b1, w2, b2, gamma, beta):
        import jax, jax.numpy as jnp
        import numpy as np
        B, S, H, F, E, K = (8, 256, 256, 512, 16, 2)
        EPS = 1e-05
        gate_logits = x @ gate_w + gate_b
        topk_vals, topk_idx = jax.lax.top_k(gate_logits, K)
        topk_w = jax.nn.softmax(topk_vals, axis=-1)
        h = jax.nn.relu(jnp.einsum('bsh,ehf->bsef', x, w1) + b1)
        expert_out = jnp.einsum('bsef,efh->bseh', h, w2) + b2
        sel = jnp.take_along_axis(expert_out, topk_idx[:, :, :, None], axis=2)
        moe = jnp.sum(topk_w[..., None] * sel, axis=2)
        y = x + moe
        mu = jnp.mean(y, axis=-1, keepdims=True)
        var = jnp.var(y, axis=-1, keepdims=True)
        return (y - mu) / jnp.sqrt(var + EPS) * gamma + beta
    edge_index = jnp.stack([src, dst])
    x = x + _L0_gnn_ref(_layernorm(x, axis=-1), L0_gnn_W1, L0_gnn_b1, L0_gnn_W2, L0_gnn_b2, edge_index)
    x = x + _L0_ffn_ref(_layernorm(x, axis=-1)[None], L0_ffn_Wr, L0_ffn_br, L0_ffn_ln_g, L0_ffn_ln_b, L0_ffn_W1, L0_ffn_b1, L0_ffn_W2, L0_ffn_b2)[0]
    x = x + _L1_gnn_ref(_layernorm(x, axis=-1), L1_gnn_W, L1_gnn_a, src, dst)
    x = x + _L1_ffn_ref(_layernorm(x, axis=-1)[None], L1_ffn_gate_w, L1_ffn_gate_b, L1_ffn_w1, L1_ffn_b1, L1_ffn_w2, L1_ffn_b2, L1_ffn_gamma, L1_ffn_beta)[0]
    return x

_drawn_inputs = setup_inputs


def setup_inputs(seed=0):
    import zlib

    import numpy as np

    out = dict(_drawn_inputs(seed))
    spreads = {'L0_ffn_br': (0.0, 0.1),
     'L0_ffn_ln_g': (1.0, 0.2),
     'L0_ffn_ln_b': (0.0, 0.1),
     'L0_ffn_b1': (0.0, 0.1),
     'L0_ffn_b2': (0.0, 0.1),
     'L1_ffn_gate_b': (0.0, 0.296),
     'L1_ffn_b1': (0.0, 0.8),
     'L1_ffn_b2': (0.0, 0.1),
     'L1_ffn_gamma': (1.0, 0.2),
     'L1_ffn_beta': (0.0, 0.1)}
    factors = {}
    for name, (base, spread) in spreads.items():
        noise = np.random.default_rng([zlib.crc32(name.encode()), seed]).standard_normal(out[name].shape)
        drawn = base * np.exp(spread * noise) if base else spread * noise
        out[name] = jnp.asarray(drawn.astype(out[name].dtype))
    for name, factor in factors.items():
        out[name] = (out[name] * factor).astype(out[name].dtype)
    return out
```

```python
import concourse.bass as bass
from concourse import mybir
from contextlib import ExitStack

F32 = mybir.dt.float32
BF16 = mybir.dt.bfloat16
FP16 = mybir.dt.float16
I32 = mybir.dt.int32
ALU = mybir.AluOpType
ACT = mybir.ActivationFunctionType
AX = mybir.AxisListType.X

P = 128
N, D, E = 3125, 256, 53125
KD = D // P
NT = -(-N // P)
TAIL = N - (NT - 1) * P
NR = NT * P
BINS = NT + 1
EC = -(-E // P)
Q = (E + NT * (P - 1)) // P
SLOTS = 8
Q = -(-Q // SLOTS) * SLOTS
QP = -(-Q // 16) * 16
NOWHERE = QP * P
MID = N // 2
HEADS, HD = 8, 32
HROW = D + HEADS
PIECE = 13
NP = EC // PIECE
NEG = -1.0e38
SLOPE = 0.2
ROWG = EC // 4
TOP = 2
LAYERS = (dict(name="L0", experts=8, hidden=1024), dict(name="L1", experts=16, hidden=512))
for layer in LAYERS:
    layer["blocks"] = (TOP * N + layer["experts"] * (P - 1)) // P


class Names:

    whole = ExitStack()

    def __init__(self, nc, stage):
        self.nc, self.stage, self.ctx, self.sems = nc, stage, ExitStack(), []

    def __enter__(self):
        return self

    def __exit__(self, *error):
        if self.sems and error[0] is None:
            with self.nc.Block() as block:
                @block.gpsimd
                def _(pool):
                    for one in self.sems:
                        pool.sem_clear(one)
        return self.ctx.__exit__(*error)

    def sb(self, name, shape, dt=F32):
        return self.ctx.enter_context(self.nc.sbuf_tensor(f"{self.stage}_{name}", shape, dt))

    def ps(self, name, dt=F32):
        return self.ctx.enter_context(self.nc.psum_tensor(f"{self.stage}_{name}", [P, 512], dt))

    def gather_sem(self, name):
        return Names.whole.enter_context(self.nc.semaphore(f"{self.stage}_{name}"))

    def sem(self, name):
        self.sems.append(self.ctx.enter_context(self.nc.semaphore(f"{self.stage}_{name}")))
        return self.sems[-1]


def rows(dram, t0, t1):
    return dram[t0 * P:t1 * P, :].rearrange("(t p) d -> p t d", p=P)


def load_nodes(eng, tiles, dram, sem):
    eng.dma_start(tiles[:, 0:NT - 1, :], rows(dram, 0, NT - 1)).then_inc(sem, 16)
    eng.dma_start(tiles[0:TAIL, NT - 1, :], dram[(NT - 1) * P:N, :]).then_inc(sem, 16)


def per_tile(ap, inner):
    return ap.unsqueeze(2).to_broadcast([P, NT, inner])


class Norm:

    def __init__(self, m, tag, squares):
        self.stat = m.sb(f"{tag}_stat", [P, NT])
        self.var = m.sb(f"{tag}_var", [P, NT])
        self.root = m.sb(f"{tag}_root", [P, NT])
        self.squares = squares
        self.centered = m.sem(f"{tag}_centered")
        self.squared = m.sem(f"{tag}_squared")
        self.var_ready = m.sem(f"{tag}_var_ready")
        self.rooted = m.sem(f"{tag}_rooted")

    def vector(self, nc, ve, x, z, done):
        nc.vector.tensor_reduce(self.stat[:, :], x[:, :, :], AX, ALU.add)
        ve.drain()
        nc.vector.tensor_scalar(self.stat[:, :], self.stat[:, :], 1.0 / D, None, ALU.mult)
        ve.drain()
        nc.vector.tensor_tensor(z[:, :, :], x[:, :, :], per_tile(self.stat[:, :], D), ALU.subtract).then_inc(self.centered, 1)
        ve.wait_ge(self.squared, 1)
        nc.vector.tensor_reduce(self.var[:, :], self.squares[:, :, :], AX, ALU.add)
        ve.drain()
        nc.vector.tensor_scalar(self.var[:, :], self.var[:, :], 1.0 / D, 1e-5, ALU.mult, ALU.add).then_inc(self.var_ready, 1)
        ve.wait_ge(self.rooted, 1)
        nc.vector.reciprocal(self.stat[:, :], self.root[:, :])
        ve.drain()
        nc.vector.tensor_tensor(z[:, :, :], z[:, :, :], per_tile(self.stat[:, :], D), ALU.mult).then_inc(done, 1)

    def scalar(self, nc, act, z):
        act.wait_ge(self.centered, 1)
        nc.scalar.activation(self.squares[:, :, :], z[:, :, :], ACT.Square).then_inc(self.squared, 1)
        act.wait_ge(self.var_ready, 1)
        nc.scalar.activation(self.root[:, :], self.var[:, :], ACT.Sqrt).then_inc(self.rooted, 1)


def constants(nc, c):
    with Names(nc, "const") as m:
        count = m.sb("count", [P, QP], I32)
        lane = m.sb("lane", [P, 1], I32)
        made = m.sem("made")
        copied = m.sem("copied")
        with nc.Block() as block:
            @block.gpsimd
            def _(pool):
                nc.gpsimd.iota(count[:, :], pattern=[[1, QP]], base=0, channel_multiplier=0).then_inc(made, 1)
                nc.gpsimd.iota(lane[:, :], pattern=[[0, 1]], base=0, channel_multiplier=1).then_inc(made, 1)
                nc.gpsimd.memset(c["ident"][:, :], 0.0).then_inc(made, 1)
                nc.gpsimd.memset(c["before"][:, :], 1.0).then_inc(made, 1)
                nc.gpsimd.memset(c["upto"][:, :], 1.0).then_inc(made, 1)
                nc.gpsimd.memset(c["ones"][:, :], 1.0).then_inc(made, 1)
                pool.wait_ge(made, 6)
                nc.gpsimd.affine_select(out=c["ident"][:, :], in_=c["ident"][:, :], compare_op=ALU.not_equal, fill=1.0,
                                        base=0, pattern=[[-1, P]], channel_multiplier=1).then_inc(made, 1)
                nc.gpsimd.affine_select(out=c["before"][:, :], in_=c["before"][:, :], compare_op=ALU.is_gt, fill=0.0,
                                        base=0, pattern=[[1, P]], channel_multiplier=-1).then_inc(made, 1)
                nc.gpsimd.affine_select(out=c["upto"][:, :], in_=c["upto"][:, :], compare_op=ALU.is_ge, fill=0.0,
                                        base=0, pattern=[[1, P]], channel_multiplier=-1).then_inc(made, 1)
                pool.wait_ge(made, 9)

            @block.vector
            def _(ve):
                ve.wait_ge(made, 2)
                nc.vector.tensor_copy(c["count_f"][:, :], count[:, :])
                nc.vector.tensor_copy(c["count_h"][:, :], count[:, :])
                nc.vector.tensor_copy(c["count_b"][:, :], count[:, 0:P])
                nc.vector.tensor_copy(c["lane_f"][:, :], lane[:, :]).then_inc(copied, 1)
                ve.wait_ge(copied, 1)


def sort_edges(nc, c, e, src, dst, low_d):
    with Names(nc, "sort") as m:
        src_rows = m.sb("src_rows", [ROWG, 4, P], I32)
        dst_rows = m.sb("dst_rows", [ROWG, 4, P], I32)
        rows_f = m.sb("rows_f", [ROWG, 2, 4, P])
        low_i = m.sb("low_i", [ROWG, 4, P], I32)
        low_rows = m.sb("low_rows", [ROWG, 4, P], BF16)
        col_i = m.sb("col_i", [P, EC], I32)
        part_i = m.sb("part_i", [P, 2, EC], I32)
        low1_f = m.sb("low1_f", [P, EC])
        dst_f = m.sb("dst_f", [P, EC])
        low_col = m.sb("low_col", [P, EC], BF16)
        tile_col = m.sb("tile_col", [P, EC], BF16)
        in_tile = m.sb("in_tile", [P, EC, BINS], BF16)
        prior = m.sb("prior", [P, (EC + 1) * BINS])
        pos = m.sb("pos", [P, EC])
        pos_i = m.sb("pos_i", [P, EC], I32)
        pos_q = m.sb("pos_q", [P, EC])
        pos_r = m.sb("pos_r", [P, EC])
        low_b = m.sb("low_b", [P, 2, PIECE * P], BF16)
        lane_hot = m.sb("lane_hot", [P, 2, PIECE * P])
        same = m.sb("same", [P, 2, PIECE * P], BF16)
        earlier = m.sb("earlier", [P, 2, PIECE * P], BF16)
        chosen = m.sb("chosen", [P, 2, PIECE, BINS])
        start = m.sb("start", [P, BINS])
        counts_i = m.sb("counts_i", [P, BINS], I32)
        chunks_f = m.sb("chunks_f", [P, BINS])
        upto_f = m.sb("upto_f", [P, BINS])
        zeros = m.sb("zeros", [P, EC])
        tcol_i = m.sb("tcol_i", [BINS, 1], I32)
        tcol_f = m.sb("tcol_f", [BINS, 1])
        tcum_f = m.sb("tcum_f", [BINS, 1])
        past = m.sb("past", [BINS, QP])
        chunk_hot = m.sb("chunk_hot", [P, 4, QP], FP16)
        dst_hot = m.sb("dst_hot", [P, 4, P], FP16)
        src_hot = m.sb("src_hot", [P, 4, P], FP16)
        nothing = m.sb("nothing", [P, QP], FP16)
        ps = [m.ps(f"ps{i}") for i in range(4)]
        ps_dst, ps_src, ps_x = m.ps("ps_dst"), m.ps("ps_src"), m.ps("ps_x")

        filled, loaded, low_ready, low_out = m.sem("filled"), m.sem("loaded"), m.sem("low_ready"), m.sem("low_out")
        rows_ready, turned, cols_ready = m.sem("rows_ready"), m.sem("turned"), m.sem("cols_ready")
        hot_ready, counted, kept = m.sem("hot_ready"), m.sem("counted"), m.sem("kept")
        sums_ready, sums_done, tcol_ready, tcum_done = m.sem("sums_ready"), m.sem("sums_done"), m.sem("tcol_ready"), m.sem("tcum_done")
        tcum_ready, tile_done = m.sem("tcum_ready"), m.sem("tile_done")
        past_ready, start_ready = m.sem("past_ready"), m.sem("start_ready")
        low_in = [m.sem(f"low_in{s}") for s in range(2)]
        lane_ready, same_ready, earlier_ready = m.sem("lane_ready"), m.sem("same_ready"), m.sem("earlier_ready")
        looked, picked = m.sem("looked"), m.sem("picked")
        place_ready, placed, all_placed, end = m.sem("place_ready"), m.sem("placed"), m.sem("all_placed"), m.sem("end")
        tick = m.sem("tick")
        prior_v = prior[:, :].rearrange("p (c t) -> p c t", t=BINS)
        full = E - 3 * ROWG * P

        with nc.Block() as block:
            @block.sync
            def _(sp):
                sp.wait_ge(filled, 1)
                for rows_i, edges in ((src_rows, src), (dst_rows, dst)):
                    for g in range(3):
                        sp.dma_start(rows_i[:, g, :], edges[g * ROWG * P:(g + 1) * ROWG * P].rearrange("(c e) -> c e", e=P)).then_inc(loaded, 16)
                    sp.dma_start(rows_i[0:full // P, 3, :], edges[3 * ROWG * P:3 * ROWG * P + full // P * P].rearrange("(c e) -> c e", e=P)).then_inc(loaded, 16)
                    sp.dma_start(rows_i[full // P:full // P + 1, 3, 0:full % P], edges[E - full % P:E].rearrange("(c e) -> c e", c=1)).then_inc(loaded, 16)
                sp.wait_ge(low_ready, 1)
                for g in range(4):
                    sp.dma_start(low_d[g * ROWG:(g + 1) * ROWG, :], low_rows[:, g, :]).then_inc(low_out, 16)
                sp.wait_ge(low_out, 64)
                with sp.Fori(0, NP // 2) as i:
                    for s in range(2):
                        sp.wait_ge(same_ready, 2 * i + s + 1)
                        sp.dma_start(low_b[:, s, :], low_d[bass.ds((2 * i + s) * PIECE, PIECE), :].rearrange("c e -> (c e)").partition_broadcast(P)).then_inc(low_in[s], 16)

            @block.gpsimd
            def _(pool):
                with pool.Fori(0, NP // 2) as i:
                    for s in range(2):
                        pool.wait_ge(same_ready, 2 + 2 * i + s + 1)
                        pool.wait_ge(looked, 2 * i + s + 1)
                        pool.sem_inc(tick, 1)
                        nc.gpsimd.affine_select(out=earlier[:, s, :].rearrange("p (c e) -> p c e", e=P),
                                                in_=same[:, s, :].rearrange("p (c e) -> p c e", e=P),
                                                compare_op=ALU.is_gt, fill=0.0, base=0, pattern=[[0, PIECE], [1, P]],
                                                channel_multiplier=-1).then_inc(earlier_ready, 1)

            @block.scalar
            def _(act):
                act.sem_inc(kept, 2)
                with act.Fori(0, NP // 2) as i:
                    for s in range(2):
                        act.wait_ge(counted, 2 + 2 * i + s + 1)
                        act.sem_inc(tick, 1)
                        nc.scalar.activation(prior[:, bass.ds(((2 * i + s) * PIECE + 1) * BINS, PIECE * BINS)],
                                             ps[s][:, 0:PIECE * BINS], ACT.Copy).then_inc(kept, 1)

            @block.tensor
            def _(pe):
                pe.wait_ge(rows_ready, 1)
                for k in range(2):
                    for g in range(4):
                        last = nc.tensor.transpose(ps[2 + k][:, g * ROWG:(g + 1) * ROWG], rows_f[:, k, g, :], c["ident"][0:ROWG, 0:ROWG])
                last.then_inc(turned, 1)
                pe.sem_inc(counted, 2)
                with pe.Fori(0, NP // 2) as i:
                    for s in range(2):
                        pe.wait_ge(hot_ready, 2 * i + s + 1)
                        pe.wait_ge(kept, 2 * i + s + 1)
                        pe.sem_inc(tick, 1)
                        for j in range(PIECE):
                            last = nc.tensor.matmul(ps[s][:, j * BINS:(j + 1) * BINS], same[:, s, j * P:(j + 1) * P],
                                                    in_tile[:, bass.ds((2 * i + s) * PIECE + j, 1), :].rearrange("p c t -> p (c t)"),
                                                    start=True, stop=True)
                        last.then_inc(counted, 1)
                pe.wait_ge(sums_ready, 1)
                total = prior_v[:, EC, :]
                nc.tensor.matmul(ps_x[:, 0:BINS], c["ones"][:, :], total, start=True, stop=True)
                nc.tensor.matmul(ps_x[:, BINS:2 * BINS], c["before"][:, :], total, start=True, stop=True)
                nc.tensor.matmul(ps_x[0:BINS, 2 * BINS:2 * BINS + 1], total, c["ones"][:, 0:1], start=True, stop=True).then_inc(sums_done, 1)
                pe.wait_ge(tcol_ready, 1)
                nc.tensor.matmul(ps[3][0:BINS, 0:1], c["upto"][0:BINS, 0:BINS], tcol_f[:, :], start=True, stop=True).then_inc(tcum_done, 1)
                pe.wait_ge(past_ready, 1)
                nc.tensor.matmul(ps[2][:, 0:QP], c["ones"][0:NT, :], past[0:NT, :], start=True, stop=True).then_inc(tile_done, 1)
                pe.wait_ge(start_ready, 1)
                pe.sem_inc(looked, 2)
                with pe.Fori(0, NP // 2) as i:
                    for s in range(2):
                        pe.wait_ge(lane_ready, 2 * i + s + 1)
                        pe.wait_ge(earlier_ready, 2 * i + s + 1)
                        pe.wait_ge(picked, 2 * i + s + 1)
                        pe.sem_inc(tick, 1)
                        for j in range(PIECE):
                            out = ps[s][:, j * BINS:(j + 1) * BINS]
                            hot = lane_hot[:, s, j * P:(j + 1) * P]
                            nc.tensor.matmul(out, hot, prior[:, bass.ds(((2 * i + s) * PIECE + j) * BINS, BINS)], start=True, stop=False)
                            nc.tensor.matmul(out, hot, start[:, :], start=False, stop=False)
                            last = nc.tensor.matmul(out, earlier[:, s, j * P:(j + 1) * P],
                                                    in_tile[:, bass.ds((2 * i + s) * PIECE + j, 1), :].rearrange("p c t -> p (c t)"),
                                                    start=False, stop=True)
                        last.then_inc(looked, 1)
                pe.wait_ge(place_ready, 1)
                nc.tensor.matmul(ps_dst[:, 0:QP], nothing[:, 0:P], nothing[:, :], start=True, stop=False)
                nc.tensor.matmul(ps_src[:, 0:QP], nothing[:, 0:P], nothing[:, :], start=True, stop=False)
                pe.sem_inc(placed, 4)
                with pe.Fori(0, EC // 4) as i:
                    for s in range(4):
                        pe.wait_ge(place_ready, 1 + 4 * i + s + 1)
                        pe.sem_inc(tick, 1)
                        nc.tensor.matmul(ps_dst[:, 0:QP], dst_hot[:, s, :], chunk_hot[:, s, :], start=False, stop=False)
                        nc.tensor.matmul(ps_src[:, 0:QP], src_hot[:, s, :], chunk_hot[:, s, :], start=False, stop=False).then_inc(placed, 1)
                nc.tensor.matmul(ps_dst[:, 0:QP], nothing[:, 0:P], nothing[:, :], start=False, stop=True)
                nc.tensor.matmul(ps_src[:, 0:QP], nothing[:, 0:P], nothing[:, :], start=False, stop=True).then_inc(all_placed, 1)

            @block.vector
            def _(ve):
                nc.vector.memset(src_rows[:, :, :], NT * P)
                nc.vector.memset(dst_rows[:, :, :], 0).then_inc(filled, 1)
                nc.vector.memset(zeros[:, :], 0.0)
                nc.vector.memset(nothing[:, :], 0.0).then_inc(place_ready, 1)
                nc.vector.memset(prior[:, 0:BINS], 0.0)
                ve.wait_ge(loaded, 160)
                nc.vector.tensor_copy(rows_f[:, 0, :, :], src_rows[:, :, :])
                nc.vector.tensor_copy(rows_f[:, 1, :, :], dst_rows[:, :, :]).then_inc(rows_ready, 1)
                nc.vector.tensor_scalar(low_i[:, :, :], src_rows[:, :, :], P - 1, None, ALU.bitwise_and)
                ve.drain()
                nc.vector.tensor_copy(low_rows[:, :, :], low_i[:, :, :]).then_inc(low_ready, 1)
                ve.wait_ge(turned, 1)
                nc.vector.tensor_copy(col_i[:, :], ps[2][:, 0:EC])
                nc.vector.tensor_scalar(dst_f[:, :], ps[3][:, 0:EC], -float(MID), None, ALU.add)
                ve.drain()
                nc.vector.tensor_scalar(part_i[:, 0, :], col_i[:, :], P - 1, None, ALU.bitwise_and)
                nc.vector.tensor_scalar(part_i[:, 1, :], col_i[:, :], 7, None, ALU.arith_shift_right)
                ve.drain()
                nc.vector.tensor_copy(low_col[:, :], part_i[:, 0, :])
                nc.vector.tensor_scalar(low1_f[:, :], part_i[:, 0, :], 1.0, None, ALU.add)
                nc.vector.tensor_copy(tile_col[:, :], part_i[:, 1, :])
                ve.drain()
                nc.vector.tensor_tensor(in_tile[:, :, :], tile_col[:, :].unsqueeze(2).to_broadcast([P, EC, BINS]),
                                        c["count_b"][:, 0:BINS].unsqueeze(1).to_broadcast([P, EC, BINS]), ALU.is_equal)
                ve.drain()
                with ve.Fori(0, NP // 2) as i:
                    for s in range(2):
                        ve.wait_ge(counted, 2 * i + s + 1)
                        nc.vector.tensor_tensor(same[:, s, :].rearrange("p (c e) -> p c e", e=P),
                                                low_col[:, bass.ds((2 * i + s) * PIECE, PIECE)].unsqueeze(2).to_broadcast([P, PIECE, P]),
                                                c["count_b"][:, :].unsqueeze(1).to_broadcast([P, PIECE, P]), ALU.is_equal).then_inc(hot_ready, 1)
                ve.wait_ge(kept, 2 + NP)
                with ve.Fori(0, BINS) as t:
                    sl = prior_v[:, 1:EC + 1, bass.ds(t, 1)].rearrange("p c t -> p (c t)")
                    nc.vector.tensor_tensor_scan(sl, zeros[:, :], sl, 0.0, ALU.add, ALU.add)
                ve.drain()
                nc.vector.tensor_copy(e["degree"][:, :], prior_v[:, EC, 0:NT]).then_inc(sums_ready, 1)
                ve.wait_ge(sums_done, 1)
                nc.vector.tensor_scalar(counts_i[:, :], ps_x[:, 0:BINS], float(P - 1), None, ALU.add)
                nc.vector.tensor_scalar(tcol_i[:, :], ps_x[0:BINS, 2 * BINS:2 * BINS + 1], float(P - 1), None, ALU.add)
                ve.drain()
                nc.vector.tensor_scalar(counts_i[:, :], counts_i[:, :], 7, None, ALU.arith_shift_right)
                nc.vector.tensor_scalar(tcol_i[:, :], tcol_i[:, :], 7, None, ALU.arith_shift_right)
                ve.drain()
                nc.vector.tensor_copy(tcol_f[:, :], tcol_i[:, :]).then_inc(tcol_ready, 1)
                nc.vector.tensor_copy(chunks_f[:, :], counts_i[:, :])
                ve.drain()
                nc.vector.tensor_tensor_scan(upto_f[:, :], zeros[:, 0:BINS], chunks_f[:, :], 0.0, ALU.add, ALU.add)
                ve.drain()
                nc.vector.tensor_tensor(start[:, :], upto_f[:, :], chunks_f[:, :], ALU.subtract)
                ve.drain()
                nc.vector.scalar_tensor_tensor(start[:, :], start[:, :], float(P), ps_x[:, BINS:2 * BINS], ALU.mult, ALU.add)
                ve.drain()
                nc.vector.memset(start[:, NT:BINS], float(NOWHERE)).then_inc(start_ready, 1)
                ve.wait_ge(tcum_done, 1)
                nc.vector.tensor_copy(tcum_f[:, :], ps[3][0:BINS, 0:1])
                ve.drain()
                nc.vector.tensor_scalar(past[:, :], c["count_f"][0:BINS, :], tcum_f[:, 0:1], None, ALU.is_ge).then_inc(past_ready, 1)
                ve.wait_ge(tile_done, 1)
                nc.vector.tensor_scalar(e["tile_f"][:, :], ps[2][:, 0:QP], 1.0, None, ALU.mult)
                nc.vector.tensor_scalar(e["tile_i"][:, :], ps[2][0:1, 0:QP], float(NT - 1), None, ALU.min)
                def compare(piece, s):
                    nc.vector.tensor_scalar(lane_hot[:, s, :], low_b[:, s, :], c["lane_f"][:, 0:1], None, ALU.is_equal).then_inc(lane_ready, 1)
                    nc.vector.tensor_tensor(same[:, s, :].rearrange("p (c e) -> p c e", e=P),
                                            low_b[:, s, :].rearrange("p (c e) -> p c e", e=P),
                                            low_col[:, bass.ds(piece * PIECE, PIECE)].unsqueeze(2).to_broadcast([P, PIECE, P]),
                                            ALU.is_equal).then_inc(same_ready, 1)

                def pick(piece, s):
                    nc.vector.tensor_tensor(chosen[:, s, :, :], ps[s][:, 0:PIECE * BINS].rearrange("p (c t) -> p c t", t=BINS),
                                            in_tile[:, bass.ds(piece * PIECE, PIECE), :], ALU.mult)
                    ve.drain()
                    nc.vector.tensor_reduce(pos[:, bass.ds(piece * PIECE, PIECE)], chosen[:, s, :, :], AX, ALU.add).then_inc(picked, 1)

                ve.sem_inc(same_ready, 2)
                ve.sem_inc(picked, 2)
                for s in range(2):
                    ve.wait_ge(low_in[s], 16)
                    compare(s, s)
                with ve.Fori(1, NP // 2) as i:
                    for s in range(2):
                        ve.wait_ge(looked, 2 * i + s + 1)
                        ve.sem_inc(tick, 1)
                        pick(2 * i + s - 2, s)
                        ve.wait_ge(low_in[s], 16 * i + 16)
                        ve.sem_inc(tick, 1)
                        compare(2 * i + s, s)
                for s in range(2):
                    ve.wait_ge(looked, NP + s + 1)
                    pick(NP - 2 + s, s)
                ve.drain()
                nc.vector.tensor_copy(pos_i[:, :], pos[:, :])
                ve.drain()
                nc.vector.tensor_scalar(part_i[:, 0, :], pos_i[:, :], P - 1, None, ALU.bitwise_and)
                nc.vector.tensor_scalar(part_i[:, 1, :], pos_i[:, :], 7, None, ALU.arith_shift_right)
                ve.drain()
                nc.vector.tensor_copy(pos_r[:, :], part_i[:, 0, :])
                nc.vector.tensor_copy(pos_q[:, :], part_i[:, 1, :])
                ve.drain()
                with ve.Fori(0, EC // 4) as i:
                    for s in range(4):
                        k = 4 * i + s
                        ve.wait_ge(placed, 4 * i + s + 1)
                        nc.vector.tensor_scalar(chunk_hot[:, s, :], c["count_h"][:, :], pos_q[:, bass.ds(k, 1)], None, ALU.is_equal)
                        nc.vector.tensor_scalar(dst_hot[:, s, :], c["count_h"][:, 0:P], pos_r[:, bass.ds(k, 1)], dst_f[:, bass.ds(k, 1)], ALU.is_equal, ALU.mult)
                        nc.vector.tensor_scalar(src_hot[:, s, :], c["count_h"][:, 0:P], pos_r[:, bass.ds(k, 1)], low1_f[:, bass.ds(k, 1)], ALU.is_equal, ALU.mult).then_inc(place_ready, 1)
                ve.wait_ge(all_placed, 1)
                nc.vector.tensor_scalar(e["slot_dst"][:, :], ps_dst[:, 0:QP], float(MID), None, ALU.add)
                nc.vector.tensor_scalar(e["slot_src"][:, :], ps_src[:, 0:QP], -1.0, None, ALU.add)
                ve.drain()
                nc.vector.scalar_tensor_tensor(e["slot_node"][:, :], e["tile_f"][:, :], float(P), e["slot_src"][:, :], ALU.mult, ALU.add).then_inc(end, 1)
                ve.wait_ge(end, 1)


def tile_of(x, t):
    return x[:, bass.ds(t, 1), :].rearrange("p t d -> p (t d)")


class Project:

    def __init__(self, m, chunks, width):
        self.chunks, self.width = chunks, width
        self.turned_ps = [m.ps(f"turned_ps{s}") for s in range(2)]
        self.out_ps = [m.ps(f"out_ps{s}") for s in range(2)]
        self.turned = m.sb("turned", [P, 2, chunks * P])
        self.staged = m.sb("staged", [P, 2, chunks * P])
        self.brought = m.sem("brought")
        self.turn_done, self.copied = m.sem("turn_done"), m.sem("copied")
        self.product, self.used = m.sem("product"), m.sem("used")
        self.tick = m.sem("project_tick")

    def over_tiles(self, eng, step):
        with eng.Fori(0, NT // 2) as i:
            for s in range(2):
                step(2 * i + s, s)
        for t in range(NT // 2 * 2, NT):
            step(t, t % 2)

    def pool(self, nc, pool, parts):
        def step(t, s):
            pool.wait_ge(self.turn_done, t + 1)
            pool.sem_inc(self.tick, 1)
            for j, part in enumerate(parts(t)):
                last = nc.gpsimd.tensor_copy(self.staged[:, s, j * D:(j + 1) * D], part)
            last.then_inc(self.brought, 1)
        self.over_tiles(pool, step)

    def tensor(self, nc, pe, ident, weight):
        pe.sem_inc(self.product, 2)
        pe.sem_inc(self.turn_done, 2)

        def step(t, s):
            pe.wait_ge(self.brought, t + 1)
            pe.wait_ge(self.copied, t + 1)
            pe.sem_inc(self.tick, 1)
            for j in range(self.chunks):
                last = nc.tensor.transpose(self.turned_ps[s][:, j * P:(j + 1) * P], self.staged[:, s, j * P:(j + 1) * P], ident)
            last.then_inc(self.turn_done, 1)
            pe.wait_ge(self.copied, 2 + t + 1)
            pe.wait_ge(self.used, t + 1)
            pe.sem_inc(self.tick, 1)
            for j in range(self.chunks):
                last = nc.tensor.matmul(self.out_ps[s][:, 0:self.width], self.turned[:, s, j * P:(j + 1) * P], weight(j),
                                        start=(j == 0), stop=(j == self.chunks - 1))
            last.then_inc(self.product, 1)
        self.over_tiles(pe, step)

    def scalar(self, nc, act):
        act.sem_inc(self.copied, 2)

        def step(t, s):
            act.wait_ge(self.turn_done, 2 + t + 1)
            act.wait_ge(self.product, t + 1)
            act.sem_inc(self.tick, 1)
            nc.scalar.activation(self.turned[:, s, :], self.turned_ps[s][:, 0:self.chunks * P], ACT.Copy).then_inc(self.copied, 1)
        self.over_tiles(act, step)

    def vector(self, ve, use):
        ve.sem_inc(self.used, 2)

        def step(t, s, earlier):
            ve.wait_ge(self.product, 2 + t + 1)
            ve.sem_inc(self.tick, 1)
            use(t, s, self.out_ps[s][:, 0:self.width], earlier).then_inc(self.used, 1)
        for s in range(2):
            step(s, s, 0)
        with ve.Fori(1, NT // 2) as i:
            for s in range(2):
                step(2 * i + s, s, i)
        step(NT - 1, 0, NT // 2)


def first_norm(nc, x_in, x, z, z_d):
    with Names(nc, "norm0") as m:
        norm = Norm(m, "ln", m.sb("squares", [P, NT, D]))
        cleared, loaded, normed, stored = m.sem("cleared"), m.sem("loaded"), m.sem("normed"), m.sem("stored")
        with nc.Block() as block:
            @block.sync
            def _(sp):
                sp.wait_ge(cleared, 1)
                load_nodes(sp, x, x_in, loaded)
                sp.wait_ge(normed, 1)
                sp.dma_start(rows(z_d, 0, NT), z[:, :, :]).then_inc(stored, 16)
                sp.wait_ge(stored, 16)

            @block.vector
            def _(ve):
                nc.vector.memset(x[:, NT - 1, :], 0.0).then_inc(cleared, 1)
                ve.wait_ge(loaded, 32)
                norm.vector(nc, ve, x, z, normed)
                ve.wait_ge(stored, 16)

            @block.scalar
            def _(act):
                norm.scalar(nc, act, z)


class Gather:

    def __init__(self, m, width):
        self.rows = m.sb("rows", [P, SLOTS, width])
        self.index = m.sb("index", [P, SLOTS], I32)
        self.index_ready = m.sem("index_ready")
        self.landed = [m.gather_sem(f"landed{s}") for s in range(SLOTS)]
        self.freed = m.sem("freed")
        self.tick = m.sem("gather_tick")

    def pool(self, nc, pool, e, table):
        half = SLOTS // 2
        with pool.Fori(0, Q // SLOTS) as i:
            for h in range(2):
                pool.wait_ge(self.freed, SLOTS * i + half * (h + 1))
                pool.sem_inc(self.tick, 1)
                nc.gpsimd.tensor_copy(self.index[:, h * half:(h + 1) * half],
                                      e["slot_dst"][:, bass.ds(SLOTS * i + h * half, half)]).then_inc(self.index_ready, 1)
                pool.wait_ge(self.index_ready, 2 * i + h + 1)
                pool.sem_inc(self.tick, 1)
                for s in range(h * half, (h + 1) * half):
                    pool.indirect_dma_start(out=self.rows[:, s, :], out_offset=None, in_=table[:, :],
                                            in_offset=bass.IndirectOffsetOnAxis(ap=self.index[:, s:s + 1], axis=0)).then_inc(self.landed[s], 16)


def aggregate(nc, stage, c, e, table, width, acc, weight=None):
    out_width = HROW if weight is not None else D
    banks = 4
    with Names(nc, stage) as m:
        g = Gather(m, width)
        pick = m.sb("pick", [P, SLOTS, P])
        scaled = m.sb("scaled", [P, SLOTS, HROW]) if weight is not None else None
        ps = [m.ps(f"ps{i}") for i in range(banks)]
        pick_ready, added, weighed, tick = m.sem("pick_ready"), m.sem("added"), m.sem("weighed"), m.sem("tick")
        with nc.Block() as block:
            @block.gpsimd
            def _(pool):
                g.pool(nc, pool, e, table)

            @block.scalar
            def _(act):
                if weight is None:
                    return
                with act.Fori(0, Q // SLOTS) as i:
                    for s in range(SLOTS):
                        act.wait_ge(g.freed, SLOTS * i + s + 1)
                        act.sem_inc(tick, 1)
                        nc.scalar.activation(scaled[:, s, D:HROW], weight[:, bass.ds((SLOTS * i + s) * HEADS, HEADS)], ACT.Copy).then_inc(weighed, 1)

            @block.tensor
            def _(pe):
                pe.sem_inc(g.freed, SLOTS)
                with pe.Fori(0, Q // SLOTS) as i:
                    for s in range(SLOTS):
                        k = SLOTS * i + s
                        pe.wait_ge(g.landed[s], 16 * i + 16)
                        pe.wait_ge(pick_ready, k + 1)
                        if weight is not None:
                            pe.wait_ge(weighed, k + 1)
                        pe.wait_ge(added, k + 1)
                        pe.sem_inc(tick, 1)
                        rhs = g.rows[:, s, 0:D] if weight is None else scaled[:, s, :]
                        nc.tensor.matmul(ps[s % banks][:, 0:out_width], pick[:, s, :], rhs, start=True, stop=True).then_inc(g.freed, 1)

            @block.vector
            def _(ve):
                def prepare(k, s, turn):
                    if weight is None:
                        nc.vector.tensor_scalar(pick[:, s, :], c["count_f"][:, 0:P], e["slot_src"][:, bass.ds(k, 1)], None, ALU.is_equal).then_inc(pick_ready, 1)
                    else:
                        nc.vector.tensor_scalar(pick[:, s, :], c["count_f"][:, 0:P], e["slot_src"][:, bass.ds(k, 1)], None, ALU.is_equal)
                        ve.wait_ge(g.landed[s], turn)
                        ve.sem_inc(tick, 1)
                        nc.vector.tensor_tensor(scaled[:, s, 0:D].rearrange("p (h d) -> p h d", d=HD),
                                                g.rows[:, s, 0:D].rearrange("p (h d) -> p h d", d=HD),
                                                weight[:, bass.ds(k * HEADS, HEADS)].unsqueeze(2).to_broadcast([P, HEADS, HD]),
                                                ALU.mult).then_inc(pick_ready, 1)

                def add(k, s):
                    tile = ve.value_load(e["tile_i"][0:1, bass.ds(k, 1)], min_val=0, max_val=NT - 1)
                    mine = acc[:, bass.ds(tile * HROW, out_width)]
                    ve.wait_ge(g.freed, SLOTS + k + 1)
                    ve.sem_inc(tick, 1)
                    nc.vector.tensor_tensor(mine, mine, ps[s % banks][:, 0:out_width], ALU.add).then_inc(added, 1)
                    ve.drain()

                nc.vector.memset(acc[:, :], 0.0)
                ve.drain()
                ve.sem_inc(added, banks)
                for s in range(banks):
                    prepare(s, s, 16)
                with ve.Fori(0, Q // SLOTS - 1) as i:
                    for s in range(SLOTS):
                        k = SLOTS * i + s
                        add(k, s)
                        prepare(k + banks, (s + banks) % SLOTS, 16 * i + (16 if s < banks else 32))
                for s in range(SLOTS):
                    k = Q - SLOTS + s
                    add(k, s)
                    if s < SLOTS - banks:
                        prepare(k + banks, s + banks, 16 * (Q // SLOTS))


def mean_layer(nc, c, e, a, x, z, acc):
    with Names(nc, "mean") as m:
        w = m.sb("w", [P, 2 * KD, D])
        bias = m.sb("bias", [P, 2, D])
        per = m.sb("per", [P, NT])
        project = Project(m, 2 * KD, D)
        loaded, ready, end = m.sem("loaded"), m.sem("ready"), m.sem("end")
        acc_v = acc[:, :].rearrange("p (t d) -> p t d", d=HROW)
        with nc.Block() as block:
            @block.sync
            def _(sp):
                for j, name in enumerate(("L0_gnn_W1", "L0_gnn_W2")):
                    sp.dma_start(w[:, j * KD:(j + 1) * KD, :], a[name].rearrange("(k p) o -> p k o", p=P)).then_inc(loaded, 16)
                for j, name in enumerate(("L0_gnn_b1", "L0_gnn_b2")):
                    sp.dma_start(bias[:, j, :], a[name].partition_broadcast(P)).then_inc(loaded, 16)

            @block.vector
            def _(ve):
                nc.vector.tensor_scalar(per[:, :], e["degree"][:, :], 1.0, None, ALU.max)
                ve.drain()
                nc.vector.reciprocal(per[:, :], per[:, :])
                ve.drain()
                nc.vector.tensor_tensor(acc_v[:, :, 0:D], acc_v[:, :, 0:D], per_tile(per[:, :], D), ALU.mult).then_inc(ready, 1)
                ve.wait_ge(loaded, 64)
                nc.vector.tensor_tensor(bias[:, 0, :], bias[:, 0, :], bias[:, 1, :], ALU.add)
                ve.drain()
                nc.vector.tensor_tensor(x[:, :, :], x[:, :, :], bias[:, 0, :].unsqueeze(1).to_broadcast([P, NT, D]), ALU.add)
                ve.drain()

                def use(t, s, out, earlier):
                    mine = x[:, bass.ds(t, 1), :].rearrange("p t d -> p (t d)")
                    return nc.vector.tensor_tensor(mine, mine, out, ALU.add)
                project.vector(ve, use)
                ve.drain().then_inc(end, 1)

            @block.scalar
            def _(act):
                project.scalar(nc, act)

            @block.tensor
            def _(pe):
                pe.wait_ge(loaded, 64)
                project.tensor(nc, pe, c["ident"][:, :], lambda j: w[:, j, :])

            @block.gpsimd
            def _(pool):
                pool.wait_ge(ready, 1)
                pool.sem_inc(end, 1)
                project.pool(nc, pool, lambda t: (tile_of(z, t), acc[:, bass.ds(t * HROW, D)]))


def route(nc, layer, c, a, x, r, gate, gate_bias, z_d, xs_d, again):
    EX, NB, tag = layer["experts"], layer["blocks"], layer["name"]
    with Names(nc, f"route{tag}") as m:
        z = m.sb("z", [P, NT, D])
        z2 = m.sb("z2", [P, NT, D]) if again else z
        squares = m.sb("squares", [P, NT, D])
        norm = Norm(m, "ln", squares)
        norm2 = Norm(m, "ln2", squares) if again else None
        gate_w = m.sb("gate_w", [P, KD, EX])
        gate_b = m.sb("gate_b", [P, EX])
        logits = m.sb("logits", [P, NT, EX])
        rank = m.sb("rank", [P, EX])
        valid = m.sb("valid", [P, NT])
        best = m.sb("best", [P, TOP, NT])
        first = m.sb("first", [P, NT])
        taken = m.sb("taken", [P, NT, EX])
        hot = m.sb("hot", [P, TOP, NT, EX])
        before = m.sb("before", [P, TOP, NT, EX])
        column = m.sb("column", [P, TOP * NT, EX])
        prior = m.sb("prior", [P, TOP * NT, EX])
        size_i = m.sb("size_i", [P, EX], I32)
        size_f = m.sb("size_f", [P, EX])
        ends = m.sb("ends", [P, EX])
        base = m.sb("base", [P, EX])
        zeros = m.sb("zeros", [P, TOP * NT])
        owner = m.sb("owner", [1, NB, EX])
        owner_f = m.sb("owner_f", [1, NB])
        pos_f = m.sb("pos_f", [P, TOP, NT])
        blank = m.sb("blank", [P, D])
        index = m.sb("index", [P, 2, TOP], I32)
        project = Project(m, KD, EX)
        before_ps = [m.ps(f"before_ps{k}") for k in range(2)]
        total_ps = [m.ps(f"total_ps{k}") for k in range(2)]
        loaded, normed, normed2, cleared, zeroed = m.sem("loaded"), m.sem("normed"), m.sem("normed2"), m.sem("cleared"), m.sem("zeroed")
        tables, hot_ready, summed, spread, away, pos_ready = m.sem("tables"), m.sem("hot_ready"), m.sem("summed"), m.sem("spread"), m.sem("away"), m.sem("pos_ready")
        index_ready, sent = m.sem("index_ready"), [m.gather_sem(f"sent{s}") for s in range(2)]
        kept, tick = m.sem("kept"), m.sem("tick")
        z_done = 1 if z_d is not None else 0
        with nc.Block() as block:
            @block.sync
            def _(sp):
                sp.dma_start(gate_w[:, :, :], gate.rearrange("(k p) e -> p k e", p=P)).then_inc(loaded, 16)
                sp.dma_start(gate_b[:, :], gate_bias.partition_broadcast(P)).then_inc(loaded, 16)
                sp.wait_ge(cleared, 1)
                with sp.Fori(0, NB) as b:
                    sp.dma_start(xs_d[bass.ds(b * P, P), :], blank[:, :]).then_inc(zeroed, 16)
                if z_d is not None:
                    sp.wait_ge(normed, 1)
                    sp.dma_start(rows(z_d, 0, NT), z[:, :, :]).then_inc(kept, 16)
                    sp.wait_ge(kept, 16)

            @block.scalar
            def _(act):
                norm.scalar(nc, act, z)
                if again:
                    norm2.scalar(nc, act, z2)
                project.scalar(nc, act)
                act.wait_ge(spread, 1)
                nc.scalar.activation(r["weight"][:, 1, :], first[:, :], ACT.Exp).then_inc(away, 1)

            @block.tensor
            def _(pe):
                pe.wait_ge(loaded, 32)
                project.tensor(nc, pe, c["ident"][:, :], lambda j: gate_w[:, j, :])
                pe.wait_ge(hot_ready, 1)
                for k in range(TOP):
                    chosen = hot[:, k, :, :].rearrange("p t e -> p (t e)")
                    nc.tensor.matmul(before_ps[k][:, 0:NT * EX], c["before"][:, :], chosen, start=True, stop=True)
                    last = nc.tensor.matmul(total_ps[k][:, 0:NT * EX], c["ones"][:, :], chosen, start=True, stop=True)
                last.then_inc(summed, 1)

            @block.vector
            def _(ve):
                nc.vector.memset(blank[:, :], 0.0).then_inc(cleared, 1)
                nc.vector.memset(zeros[:, :], 0.0)
                norm.vector(nc, ve, x, z, normed)
                if again:
                    ve.drain()
                    norm2.vector(nc, ve, z, z2, normed2)

                def use(t, s, out, earlier):
                    return nc.vector.tensor_tensor(logits[:, bass.ds(t, 1), :].rearrange("p t e -> p (t e)"), out, gate_b[:, :], ALU.add)
                project.vector(ve, use)
                ve.wait_ge(tables, 2)
                nc.vector.tensor_scalar(rank[:, :], c["count_f"][:, 0:EX], -1.0, float(EX), ALU.mult, ALU.add)
                ve.drain()
                for k in range(TOP):
                    shape = [P, NT, EX]
                    mine = hot[:, k, :, :]
                    nc.vector.tensor_reduce(best[:, k, :], logits[:, :, :], AX, ALU.max)
                    ve.drain()
                    nc.vector.tensor_tensor(taken[:, :, :], logits[:, :, :], best[:, k, :].unsqueeze(2).to_broadcast(shape), ALU.is_equal)
                    ve.drain()
                    nc.vector.tensor_tensor(taken[:, :, :], taken[:, :, :], rank[:, :].unsqueeze(1).to_broadcast(shape), ALU.mult)
                    ve.drain()
                    nc.vector.tensor_reduce(first[:, :], taken[:, :, :], AX, ALU.max)
                    ve.drain()
                    nc.vector.tensor_tensor(mine, rank[:, :].unsqueeze(1).to_broadcast(shape), first[:, :].unsqueeze(2).to_broadcast(shape), ALU.is_equal)
                    ve.drain()
                    nc.vector.scalar_tensor_tensor(logits[:, :, :], mine, NEG, logits[:, :, :], ALU.mult, ALU.add)
                    ve.drain()
                    nc.vector.tensor_tensor(mine, mine, valid[:, :].unsqueeze(2).to_broadcast(shape), ALU.mult)
                    ve.drain()
                nc.vector.tensor_tensor(first[:, :], best[:, 1, :], best[:, 0, :], ALU.subtract).then_inc(spread, 1)
                nc.vector.memset(prior[:, 0, :], 0.0).then_inc(hot_ready, 1)
                ve.wait_ge(away, 1)
                nc.vector.tensor_scalar(first[:, :], r["weight"][:, 1, :], 1.0, None, ALU.add)
                ve.drain()
                nc.vector.reciprocal(r["weight"][:, 0, :], first[:, :])
                ve.drain()
                nc.vector.tensor_tensor(r["weight"][:, 1, :], r["weight"][:, 1, :], r["weight"][:, 0, :], ALU.mult)
                ve.wait_ge(summed, 1)
                for k in range(TOP):
                    nc.vector.tensor_copy(before[:, k, :, :].rearrange("p t e -> p (t e)"), before_ps[k][:, 0:NT * EX])
                    nc.vector.tensor_copy(column[:, k * NT:(k + 1) * NT, :].rearrange("p t e -> p (t e)"), total_ps[k][:, 0:NT * EX])
                ve.drain()
                with ve.Fori(0, EX) as ex:
                    sl = column[:, :, bass.ds(ex, 1)].rearrange("p t e -> p (t e)")
                    nc.vector.tensor_tensor_scan(sl, zeros[:, :], sl, 0.0, ALU.add, ALU.add)
                ve.drain()
                nc.vector.tensor_copy(prior[:, 1:, :], column[:, 0:TOP * NT - 1, :])
                nc.vector.tensor_scalar(size_i[:, :], column[:, TOP * NT - 1, :], float(P - 1), None, ALU.add)
                ve.drain()
                nc.vector.tensor_scalar(size_i[:, :], size_i[:, :], 7, None, ALU.arith_shift_right)
                ve.drain()
                nc.vector.tensor_copy(size_f[:, :], size_i[:, :])
                ve.drain()
                nc.vector.tensor_tensor_scan(ends[:, :], zeros[:, 0:EX], size_f[:, :], 0.0, ALU.add, ALU.add)
                ve.drain()
                nc.vector.tensor_tensor(base[:, :], ends[:, :], size_f[:, :], ALU.subtract)
                nc.vector.tensor_tensor(owner[:, :, :], c["count_f"][0:1, 0:NB].unsqueeze(2).to_broadcast([1, NB, EX]),
                                        ends[0:1, :].unsqueeze(1).to_broadcast([1, NB, EX]), ALU.is_ge)
                ve.drain()
                nc.vector.tensor_reduce(owner_f[:, :], owner[:, :, :], AX, ALU.add)
                nc.vector.tensor_scalar(base[:, :], base[:, :], float(P), None, ALU.mult)
                ve.drain()
                nc.vector.tensor_scalar(r["owner"][:, 0:NB], owner_f[:, :], float(EX - 1), None, ALU.min)
                flat = [P, TOP * NT, EX]
                before_v = before[:, :, :, :].rearrange("p k t e -> p (k t) e")
                nc.vector.tensor_tensor(prior[:, :, :], prior[:, :, :], before_v, ALU.add)
                ve.drain()
                nc.vector.tensor_tensor(prior[:, :, :], prior[:, :, :], base[:, :].unsqueeze(1).to_broadcast(flat), ALU.add)
                ve.drain()
                nc.vector.tensor_tensor(prior[:, :, :], prior[:, :, :], hot[:, :, :, :].rearrange("p k t e -> p (k t) e"), ALU.mult)
                ve.drain()
                nc.vector.tensor_reduce(pos_f[:, :, :].rearrange("p k t -> p (k t)"), prior[:, :, :], AX, ALU.add)
                ve.drain()
                nc.vector.tensor_copy(r["pos"][:, :, :], pos_f[:, :, :].rearrange("p k t -> p t k")).then_inc(pos_ready, 1)
                ve.wait_ge(pos_ready, 1)

            @block.gpsimd
            def _(pool):
                nc.gpsimd.memset(valid[:, :], 1.0).then_inc(tables, 1)
                pool.wait_ge(tables, 1)
                nc.gpsimd.affine_select(out=valid[:, :], in_=valid[:, :], compare_op=ALU.is_gt, fill=0.0, base=N,
                                        pattern=[[-P, NT]], channel_multiplier=-1).then_inc(tables, 1)
                pool.wait_ge(normed, 1)
                pool.sem_inc(tick, 1)
                project.pool(nc, pool, lambda t: (tile_of(z, t),))
                pool.wait_ge(zeroed, 16 * NB)
                pool.wait_ge(pos_ready, 1)
                if again:
                    pool.wait_ge(normed2, 1)
                pool.sem_inc(tick, 1)
                with pool.Fori(0, NT // 2) as i:
                    for s in range(2):
                        nc.gpsimd.tensor_copy(index[:, s, :], r["pos"][:, bass.ds(2 * i + s, 1), :].rearrange("p t k -> p (t k)")).then_inc(index_ready, 1)
                        nc.gpsimd.tensor_copy(squares[:, s, :], z2[:, bass.ds(2 * i + s, 1), :].rearrange("p t d -> p (t d)")).then_inc(index_ready, 1)
                        pool.wait_ge(index_ready, 4 * i + 2 * s + 2)
                        pool.sem_inc(tick, 1)
                        for k in range(TOP):
                            pool.indirect_dma_start(out=xs_d[:, :], out_offset=bass.IndirectOffsetOnAxis(ap=index[:, s, k:k + 1], axis=0),
                                                    in_=squares[:, s, :], in_offset=None).then_inc(sent[s], 16)
                    for s in range(2):
                        pool.wait_ge(sent[s], 32 * i + 32)
                        pool.sem_inc(tick, 1)
                for k in range(TOP):
                    pool.indirect_dma_start(out=xs_d[:, :], out_offset=bass.IndirectOffsetOnAxis(ap=r["pos"][0:TAIL, NT - 1, k:k + 1], axis=0),
                                            in_=z2[0:TAIL, NT - 1, :], in_offset=None).then_inc(sent[0], 16)
                pool.wait_ge(sent[0], 32 * (NT // 2) + 32)


def experts(nc, layer, c, a, r, xs_d, ys_d):
    EX, NB, H, tag = layer["experts"], layer["blocks"], layer["hidden"], layer["name"]
    HC = H // P
    scaled = tag == "L0"
    func = ACT.Gelu if scaled else ACT.Relu
    low = "L0_ffn_W" if scaled else "L1_ffn_w"
    w1, w2, b1, b2 = a[low + "1"], a[low + "2"], a[f"{tag}_ffn_b1"], a[f"{tag}_ffn_b2"]
    with Names(nc, f"experts{tag}") as m:
        w1_sb = m.sb("w1", [P, 2, KD * H])
        w2_sb = m.sb("w2", [P, EX * HC * D])
        b1_sb = m.sb("b1", [P, EX * HC])
        b2_sb = m.sb("b2", [P, EX * D])
        ln = m.sb("ln", [P, 2, EX * KD]) if scaled else None
        xb = m.sb("xb", [P, 2, D])
        xT = m.sb("xT", [P, 2, KD, P])
        hT = m.sb("hT", [P, 2, HC, P])
        yb = m.sb("yb", [P, 2, D])
        banks = HC // 4
        turn_ps = [m.ps(f"turn_ps{s}") for s in range(2)]
        hid_ps = [[m.ps(f"hid_ps{s}{q}") for q in range(banks)] for s in range(2)]
        out_ps = [m.ps(f"out_ps{s}") for s in range(2)]
        w_in = m.sem("w_in")
        w1_in = [m.sem(f"w1_in{s}") for s in range(2)]
        x_in = [m.sem(f"x_in{s}") for s in range(2)]
        y_out = [m.gather_sem(f"y_out{s}") for s in range(2)]
        turned, ready, hidden, acted, product, done = (m.sem(n) for n in ("turned", "ready", "hidden", "acted", "product", "done"))
        tick = m.sem("tick")
        loads = 16 * (EX + 2 + (2 if scaled else 0))
        with nc.Block() as block:
            @block.sync
            def _(sp):
                sp.dma_start(b1_sb[:, :], b1.rearrange("p e c -> p (e c)")).then_inc(w_in, 16)
                sp.dma_start(b2_sb[:, :], b2.rearrange("e d -> (e d)").partition_broadcast(P)).then_inc(w_in, 16)
                if scaled:
                    for j, name in enumerate(("L0_ffn_ln_g", "L0_ffn_ln_b")):
                        sp.dma_start(ln[:, j, :], a[name].rearrange("p e k -> p (e k)")).then_inc(w_in, 16)
                for ex in range(EX):
                    sp.dma_start(w2_sb[:, ex * HC * D:(ex + 1) * HC * D].rearrange("p (k d) -> p k d", d=D),
                                 w2[ex].rearrange("(k p) d -> p k d", p=P)).then_inc(w_in, 16)
                sp.sem_inc(turned, 2)

                def load(b, s, lagging):
                    ex = sp.value_load(r["owner"][0:1, bass.ds(b, 1)], min_val=0, max_val=EX - 1)
                    sp.wait_ge(turned, b + 1)
                    sp.dma_start(xb[:, s, :], xs_d[bass.ds(b * P, P), :]).then_inc(x_in[s], 16)
                    if lagging:
                        sp.wait_ge(hidden, (b - 1) * banks)
                    sp.dma_start(w1_sb[:, s, :].rearrange("p (k h) -> p k h", h=H),
                                 w1[bass.ds(ex, 1)].rearrange("o (k p) h -> p (o k) h", p=P)).then_inc(w1_in[s], 16)
                for s in range(2):
                    load(s, s, False)
                with sp.Fori(1, NB // 2) as i:
                    for s in range(2):
                        load(2 * i + s, s, True)

            @block.gpsimd
            def _(pool):
                with pool.Fori(0, NB // 2) as i:
                    for s in range(2):
                        pool.wait_ge(done, 2 + 2 * i + s + 1)
                        pool.sem_inc(tick, 1)
                        pool.dma_start(ys_d[bass.ds((2 * i + s) * P, P), :], yb[:, s, :]).then_inc(y_out[s], 16)
                for s in range(2):
                    pool.wait_ge(y_out[s], 16 * (NB // 2))

            @block.tensor
            def _(pe):
                def turn(b, s, count):
                    pe.wait_ge(x_in[s], 16 * count)
                    pe.wait_ge(ready, b + 1)
                    pe.sem_inc(tick, 1)
                    for k in range(KD):
                        last = nc.tensor.transpose(turn_ps[s][:, k * P:(k + 1) * P], xb[:, s, k * P:(k + 1) * P], c["ident"][:, :])
                    last.then_inc(turned, 1)

                def hide(b, s, count):
                    pe.wait_ge(w1_in[s], 16 * count)
                    pe.wait_ge(ready, 2 + b + 1)
                    pe.wait_ge(acted, (b + 1) * banks)
                    pe.sem_inc(tick, 1)
                    for hc in range(HC):
                        for k in range(KD):
                            last = nc.tensor.matmul(hid_ps[s][hc // 4][:, hc % 4 * P:(hc % 4 + 1) * P],
                                                    w1_sb[:, s, k * H + hc * P:k * H + (hc + 1) * P],
                                                    xT[:, s, k, :], start=(k == 0), stop=(k == KD - 1))
                        if hc % 4 == 3:
                            last.then_inc(hidden, 1)

                def finish(b, s):
                    ex = pe.value_load(r["owner"][0:1, bass.ds(b, 1)], min_val=0, max_val=EX - 1)
                    pe.wait_ge(acted, (2 + b + 1) * banks)
                    pe.wait_ge(done, b + 1)
                    pe.sem_inc(tick, 1)
                    for hc in range(HC):
                        last = nc.tensor.matmul(out_ps[s][:, 0:D], hT[:, s, hc, :], w2_sb[:, bass.ds(ex * (HC * D) + hc * D, D)],
                                                start=(hc == 0), stop=(hc == HC - 1))
                    last.then_inc(product, 1)

                pe.sem_inc(product, 2)
                pe.wait_ge(w_in, loads)
                turn(0, 0, 1)
                turn(1, 1, 1)
                hide(0, 0, 1)
                with pe.Fori(0, (NB - 2) // 2) as i:
                    for s in range(2):
                        b = 2 * i + s + 1
                        turn(b + 1, s, i + 2)
                        hide(b, 1 - s, i + 1 + s)
                        finish(b - 1, s)
                hide(NB - 1, 1, NB // 2)
                finish(NB - 2, 0)
                finish(NB - 1, 1)

            @block.scalar
            def _(act):
                act.sem_inc(acted, 2 * banks)
                act.wait_ge(w_in, loads)
                with act.Fori(0, NB // 2) as i:
                    for s in range(2):
                        b = 2 * i + s
                        ex = act.value_load(r["owner"][0:1, bass.ds(b, 1)], min_val=0, max_val=EX - 1)
                        act.wait_ge(product, b + 1)
                        act.sem_inc(tick, 1)
                        for q in range(banks):
                            act.wait_ge(hidden, b * banks + q + 1)
                            act.sem_inc(tick, 1)
                            for j in range(4):
                                hc = 4 * q + j
                                last = nc.scalar.activation(hT[:, s, hc, :], hid_ps[s][q][:, j * P:(j + 1) * P], func,
                                                            bias=b1_sb[:, bass.ds(ex * HC + hc, 1)])
                            last.then_inc(acted, 1)

            @block.vector
            def _(ve):
                def scale(b, s, lagging):
                    ve.wait_ge(turned, 2 + b + 1)
                    if lagging:
                        ve.wait_ge(hidden, (b - 1) * banks)
                    ve.sem_inc(tick, 1)
                    if not scaled:
                        nc.vector.tensor_copy(xT[:, s, :, :].rearrange("p k t -> p (k t)"), turn_ps[s][:, 0:D]).then_inc(ready, 1)
                        return
                    ex = ve.value_load(r["owner"][0:1, bass.ds(b, 1)], min_val=0, max_val=EX - 1)
                    for k in range(KD):
                        last = nc.vector.tensor_scalar(xT[:, s, k, :], turn_ps[s][:, k * P:(k + 1) * P], ln[:, 0, bass.ds(ex * KD + k, 1)],
                                                       ln[:, 1, bass.ds(ex * KD + k, 1)], ALU.mult, ALU.add)
                    last.then_inc(ready, 1)

                def shift(b, s, count):
                    ex = ve.value_load(r["owner"][0:1, bass.ds(b, 1)], min_val=0, max_val=EX - 1)
                    ve.wait_ge(product, 2 + b + 1)
                    if count is not None:
                        ve.wait_ge(y_out[s], 16 * count)
                    ve.sem_inc(tick, 1)
                    nc.vector.tensor_tensor(yb[:, s, :], out_ps[s][:, 0:D], b2_sb[:, bass.ds(ex * D, D)], ALU.add).then_inc(done, 1)

                ve.sem_inc(ready, 2)
                ve.sem_inc(done, 2)
                ve.wait_ge(w_in, loads)
                scale(0, 0, False)
                scale(1, 1, False)
                scale(2, 0, True)
                shift(0, 0, None)
                scale(3, 1, True)
                shift(1, 1, None)
                with ve.Fori(1, NB // 2 - 1) as i:
                    for s in range(2):
                        scale(2 * i + s + 2, s, True)
                        shift(2 * i + s, s, i)
                for s in range(2):
                    shift(NB - 2 + s, s, NB // 2 - 1)


def combine(nc, layer, r, ys_d, target, after):
    tag = layer["name"]
    with Names(nc, f"combine{tag}") as m:
        ys = m.sb("ys", [P, 2, TOP, D])
        index = m.sb("index", [P, 2, TOP], I32)
        index_ready, used, end, tick = m.sem("index_ready"), m.sem("used"), m.sem("end"), m.sem("tick")
        landed = [m.gather_sem(f"landed{s}") for s in range(2)]
        extra = after(m) if after else None
        with nc.Block() as block:
            @block.gpsimd
            def _(pool):
                with pool.Fori(0, NT // 2) as i:
                    for s in range(2):
                        pool.wait_ge(used, 2 * i + s + 1)
                        pool.sem_inc(tick, 1)
                        nc.gpsimd.tensor_copy(index[:, s, :], r["pos"][:, bass.ds(2 * i + s, 1), :].rearrange("p t k -> p (t k)")).then_inc(index_ready, 1)
                        pool.wait_ge(index_ready, 2 * i + s + 1)
                        pool.sem_inc(tick, 1)
                        for k in range(TOP):
                            pool.indirect_dma_start(out=ys[:, s, k, :], out_offset=None, in_=ys_d[:, :],
                                                    in_offset=bass.IndirectOffsetOnAxis(ap=index[:, s, k:k + 1], axis=0)).then_inc(landed[s], 16)
                pool.wait_ge(used, NT)
                for k in range(TOP):
                    pool.indirect_dma_start(out=ys[0:TAIL, 0, k, :], out_offset=None, in_=ys_d[:, :],
                                            in_offset=bass.IndirectOffsetOnAxis(ap=r["pos"][0:TAIL, NT - 1, k:k + 1], axis=0)).then_inc(landed[0], 16)

            @block.vector
            def _(ve):
                if extra:
                    extra.before(ve)
                def add(t, s, n, turn):
                    ve.wait_ge(landed[s], turn)
                    ve.sem_inc(tick, 1)
                    mine = target[0:n, bass.ds(t, 1), :].rearrange("p t d -> p (t d)")
                    for k in range(TOP):
                        last = nc.vector.scalar_tensor_tensor(mine, ys[0:n, s, k, :], r["weight"][0:n, k, bass.ds(t, 1)], mine, ALU.mult, ALU.add)
                        if k < TOP - 1:
                            ve.drain()
                    last.then_inc(used, 1)
                ve.sem_inc(used, 2)
                with ve.Fori(0, NT // 2) as i:
                    for s in range(2):
                        add(2 * i + s, s, P, 32 * i + 32)
                add(NT - 1, 0, TAIL, 32 * (NT // 2) + 32)
                ve.drain()
                if extra:
                    extra.vector(ve)
                ve.drain().then_inc(end, 1)

            if extra:
                extra.rest(block)


class Finish:

    def __init__(self, nc, m, a, x, z, z_d, out):
        self.nc, self.a, self.x, self.z, self.z_d, self.out = nc, a, x, z, z_d, out
        self.affine = m.sb("affine", [P, 2, D])
        self.norm = Norm(m, "ln", m.sb("squares", [P, NT, D]))
        self.loaded, self.normed, self.total, self.stored = m.sem("loaded"), m.sem("normed"), m.sem("total"), m.sem("stored")

    def before(self, ve):
        ve.wait_ge(self.loaded, 48)

    def vector(self, ve):
        nc, x, z = self.nc, self.x, self.z
        self.norm.vector(nc, ve, z, z, self.normed)
        ve.drain()
        shape = [P, NT, D]
        nc.vector.tensor_tensor(z[:, :, :], z[:, :, :], self.affine[:, 0, :].unsqueeze(1).to_broadcast(shape), ALU.mult)
        nc.vector.tensor_tensor(x[:, :, :], x[:, :, :], self.affine[:, 1, :].unsqueeze(1).to_broadcast(shape), ALU.add)
        ve.drain()
        nc.vector.tensor_tensor(x[:, :, :], x[:, :, :], z[:, :, :], ALU.add).then_inc(self.total, 1)

    def rest(self, block):
        nc, a, x, z = self.nc, self.a, self.x, self.z

        @block.scalar
        def _(act):
            self.norm.scalar(nc, act, z)

        @block.sync
        def _(sp):
            sp.dma_start(z[:, :, :], rows(self.z_d, 0, NT)).then_inc(self.loaded, 16)
            for j, name in enumerate(("L1_ffn_gamma", "L1_ffn_beta")):
                sp.dma_start(self.affine[:, j, :], a[name].partition_broadcast(P)).then_inc(self.loaded, 16)
            sp.wait_ge(self.total, 1)
            sp.dma_start(rows(self.out, 0, NT - 1), x[:, 0:NT - 1, :]).then_inc(self.stored, 16)
            sp.dma_start(self.out[(NT - 1) * P:N, :], x[0:TAIL, NT - 1, :]).then_inc(self.stored, 16)
            sp.wait_ge(self.stored, 32)


def heads(nc, c, a, x, h, h_d, coef):
    with Names(nc, "heads") as m:
        z = m.sb("z", [P, NT, D])
        norm = Norm(m, "ln", m.sb("squares", [P, NT, D]))
        w = m.sb("w", [P, KD, D])
        att = m.sb("att", [P, HEADS, 5, HD])
        ends = m.sb("ends", [P, 3, D])
        row = m.sb("row", [P, 2, HROW])
        work = m.sb("work", [P, 3, D])
        term = m.sb("term", [P, 2, HEADS])
        project = Project(m, KD, D)
        loaded, normed, row_ready, end = m.sem("loaded"), m.sem("normed"), m.sem("row_ready"), m.sem("end")
        stored = [m.sem(f"stored{s}") for s in range(2)]

        def by_head(ap):
            return ap.rearrange("p (h d) -> p h d", d=HD)

        with nc.Block() as block:
            @block.sync
            def _(sp):
                sp.dma_start(w[:, :, :], a["L1_gnn_W"].rearrange("(k p) o -> p k o", p=P)).then_inc(loaded, 16)
                sp.dma_start(att[:, :, :, :].rearrange("p h f d -> p (h f d)"), a["L1_gnn_a"].rearrange("h f -> (h f)").partition_broadcast(P)).then_inc(loaded, 16)

                def store(t, s):
                    sp.wait_ge(row_ready, t + 1)
                    sp.dma_start(h_d[bass.ds(t * P, P), :], row[:, s, :]).then_inc(stored[s], 16)
                with sp.Fori(0, NT // 2) as i:
                    for s in range(2):
                        store(2 * i + s, s)
                store(NT - 1, 0)
                sp.wait_ge(stored[0], 16 * (NT // 2 + 1))
                sp.wait_ge(stored[1], 16 * (NT // 2))

            @block.scalar
            def _(act):
                norm.scalar(nc, act, z)
                project.scalar(nc, act)

            @block.tensor
            def _(pe):
                pe.wait_ge(loaded, 32)
                project.tensor(nc, pe, c["ident"][:, :], lambda j: w[:, j, :])

            @block.gpsimd
            def _(pool):
                pool.wait_ge(normed, 1)
                pool.sem_inc(end, 1)
                project.pool(nc, pool, lambda t: (tile_of(z, t),))

            @block.vector
            def _(ve):
                norm.vector(nc, ve, x, z, normed)
                ve.wait_ge(loaded, 32)
                nc.vector.tensor_tensor(by_head(ends[:, 0, :]), att[:, :, 0, :], att[:, :, 2, :], ALU.subtract)
                nc.vector.tensor_tensor(by_head(ends[:, 1, :]), att[:, :, 1, :], att[:, :, 2, :], ALU.add)
                nc.vector.tensor_scalar(by_head(ends[:, 2, :]), att[:, :, 4, :], 0.5, None, ALU.mult)
                nc.vector.tensor_copy(by_head(coef[:, 0:D]), att[:, :, 3, :])
                nc.vector.tensor_scalar(by_head(coef[:, D:2 * D]), att[:, :, 4, :], -0.5, None, ALU.mult)
                ve.drain()
                def use(t, s, out, earlier):
                    nc.vector.tensor_tensor(work[:, 0, :], out, ends[:, 2, :], ALU.mult)
                    ve.drain()
                    for j in range(2):
                        nc.vector.tensor_tensor(work[:, 1 + j, :], work[:, 0, :], ends[:, j, :], ALU.add)
                    ve.drain()
                    for j in range(2):
                        nc.vector.tensor_tensor(work[:, 1 + j, :], work[:, 1 + j, :], out, ALU.mult)
                    ve.drain()
                    for j in range(2):
                        nc.vector.tensor_reduce(term[:, j, :], by_head(work[:, 1 + j, :]), AX, ALU.add)
                    ve.drain()
                    nc.vector.tensor_scalar(h[:, bass.ds(t * HROW + D, HEADS)], term[:, 0, :], -1.0, None, ALU.mult)
                    nc.vector.tensor_scalar(h[:, bass.ds(t * HROW, D)], out, 1.0, None, ALU.mult)
                    if not (isinstance(earlier, int) and earlier == 0):
                        ve.wait_ge(stored[s], 16 * earlier)
                        ve.sem_inc(project.tick, 1)
                    nc.vector.tensor_copy(row[:, s, D:HROW], term[:, 1, :])
                    last = nc.vector.tensor_copy(row[:, s, 0:D], out)
                    last.then_inc(row_ready, 1)
                    return ve.drain()

                project.vector(ve, use)
                ve.drain().then_inc(end, 1)


def scores(nc, c, e, h, h_d, coef, score):
    banks = 4
    with Names(nc, "scores") as m:
        g = Gather(m, HROW)
        pick = m.sb("pick", [P, 4, P])
        minus = m.sb("minus", [P, 2, P])
        both = m.sb("both", [P, 2, 2 * D])
        part = m.sb("part", [P, 2, HEADS])
        turn_ps = [m.ps(f"turn_ps{s}") for s in range(2)]
        diff_ps = [m.ps(f"diff_ps{s}") for s in range(banks)]
        pick_ready, turned, copied, absed, scored, tick = (m.sem(n) for n in ("pick_ready", "turned", "copied", "absed", "scored", "tick"))
        diffed = g.freed
        with nc.Block() as block:
            @block.gpsimd
            def _(pool):
                g.pool(nc, pool, e, h_d)

            @block.tensor
            def _(pe):
                def turn(k, s):
                    pe.wait_ge(pick_ready, k + 1)
                    pe.wait_ge(copied, k + 1)
                    pe.sem_inc(tick, 1)
                    nc.tensor.transpose(turn_ps[s % 2][:, 0:P], pick[:, s % 4, :], c["ident"][:, :]).then_inc(turned, 1)

                pe.sem_inc(diffed, SLOTS)
                pe.sem_inc(turned, 4)
                turn(0, 0)
                with pe.Fori(0, Q // SLOTS) as i:
                    for s in range(SLOTS):
                        k = SLOTS * i + s
                        turn(k + 1, s + 1)
                        tile = pe.value_load(e["tile_i"][0:1, bass.ds(k, 1)], min_val=0, max_val=NT - 1)
                        pe.wait_ge(g.landed[s], 16 * i + 16)
                        pe.wait_ge(copied, 2 + k + 1)
                        pe.wait_ge(scored, k + 1)
                        pe.sem_inc(tick, 1)
                        nc.tensor.matmul(diff_ps[s % banks][:, 0:HROW], c["ident"][:, :], g.rows[:, s, :], start=True, stop=False)
                        nc.tensor.matmul(diff_ps[s % banks][:, 0:HROW], minus[:, s % 2, :], h[:, bass.ds(tile * HROW, HROW)],
                                         start=False, stop=True).then_inc(diffed, 1)

            @block.scalar
            def _(act):
                def copy(k, s):
                    act.wait_ge(turned, 4 + k + 1)
                    act.sem_inc(tick, 1)
                    nc.scalar.activation(minus[:, s % 2, :], turn_ps[s % 2][:, 0:P], ACT.Copy, scale=-1.0).then_inc(copied, 1)

                act.sem_inc(copied, 2)
                copy(0, 0)
                with act.Fori(0, Q // SLOTS) as i:
                    for s in range(SLOTS):
                        k = SLOTS * i + s
                        act.wait_ge(diffed, SLOTS + k)
                        copy(k + 1, s + 1)
                        act.wait_ge(diffed, SLOTS + k + 1)
                        act.wait_ge(scored, 2 + k + 1)
                        act.sem_inc(tick, 1)
                        nc.scalar.activation(both[:, s % 2, 0:D], diff_ps[s % banks][:, 0:D], ACT.Abs)
                        nc.scalar.activation(both[:, s % 2, D:2 * D], diff_ps[s % banks][:, 0:D], ACT.Square).then_inc(absed, 1)

            @block.vector
            def _(ve):
                def prepare(k, s):
                    ve.wait_ge(turned, k + 1)
                    ve.sem_inc(tick, 1)
                    nc.vector.tensor_scalar(pick[:, s % 4, :], c["count_f"][:, 0:P], e["slot_src"][:, bass.ds(k, 1)], None, ALU.is_equal).then_inc(pick_ready, 1)

                nc.vector.memset(score[:, :], 0.0)
                ve.drain()
                ve.sem_inc(scored, banks)
                prepare(0, 0)
                prepare(1, 1)
                with ve.Fori(0, Q // SLOTS) as i:
                    for s in range(SLOTS):
                        k = SLOTS * i + s
                        prepare(k + 2, s + 2)
                        ve.wait_ge(absed, k + 1)
                        ve.sem_inc(tick, 1)
                        nc.vector.tensor_tensor(both[:, s % 2, :], both[:, s % 2, :], coef[:, :], ALU.mult)
                        ve.drain()
                        nc.vector.tensor_reduce(part[:, s % 2, :], both[:, s % 2, :].rearrange("p (f h d) -> p h f d", f=2, d=HD),
                                                mybir.AxisListType.XY, ALU.add)
                        ve.drain()
                        nc.vector.tensor_tensor(score[:, bass.ds(k * HEADS, HEADS)], part[:, s % 2, :], diff_ps[s % banks][:, D:HROW], ALU.add).then_inc(scored, 1)


def edge_softmax(nc, c, e, score):
    W = QP * HEADS
    BLK = W // P
    with Names(nc, "softmax") as m:
        slope = m.sb("slope", [P, W])
        node_h = m.sb("node_h", [P, W])
        turned = m.sb("turned", [P, W])
        change = m.sb("change", [P, W + 1])
        forth = m.sb("forth", [P, W])
        back = m.sb("back", [P, W])
        picks = m.sb("picks", [P, 2, P])
        ends = m.sb("ends", [P, 2, QP])
        joins = m.sb("joins", [P, QP + 1])
        whole = m.sb("whole", [P, QP])
        step = m.sb("step", [P, 2, QP])
        apart = m.sb("apart", [P, 2, QP])
        ps = [m.ps(f"ps{s}") for s in range(2)]
        lin, named, moved, emptied, scanned, topped, bounded, exped, end = (
            m.sem(n) for n in ("lin", "named", "moved", "emptied", "scanned", "topped", "bounded", "exped", "end"))
        back1, seen = m.sem("back1"), m.sem("seen")
        G = BLK // 4
        with nc.Block() as block:
            @block.tensor
            def _(pe):
                n = 0

                def four(source, g):
                    nonlocal n
                    pe.wait_ge(emptied, n + 1)
                    for j in range(4):
                        b = 4 * g + j
                        last = nc.tensor.transpose(ps[n % 2][:, j * P:(j + 1) * P], source[:, b * P:(b + 1) * P], c["ident"][:, :])
                    last.then_inc(moved, 1)
                    n += 1
                pe.wait_ge(lin, 1)
                for g in range(G):
                    four(score, g)
                pe.wait_ge(named, 1)
                for g in range(G):
                    four(node_h, g)
                pe.wait_ge(scanned, 1)
                for g in range(G):
                    four(forth, g)
                pe.wait_ge(topped, 1)
                for j in range(2):
                    for g in range(G):
                        pe.wait_ge(emptied, n + 1)
                        nc.tensor.matmul(ps[n % 2][:, :], picks[:, j, :], back[:, g * 512:(g + 1) * 512], start=True, stop=True).then_inc(moved, 1)
                        n += 1
                for j in range(2):
                    pe.wait_ge(emptied, n + 1)
                    nc.tensor.matmul(ps[n % 2][:, 0:QP], picks[:, j, :], e["slot_node"][:, :], start=True, stop=True).then_inc(moved, 1)
                    n += 1

            @block.scalar
            def _(act):
                act.wait_ge(bounded, 1)
                nc.scalar.activation(score[:, :], score[:, :], ACT.Exp).then_inc(exped, 1)

            @block.vector
            def _(ve):
                n = 0

                def empty(out):
                    nonlocal n
                    ve.wait_ge(moved, n + 1)
                    nc.vector.tensor_copy(out, ps[n % 2][:, 0:out.shape[1]]).then_inc(emptied, 1)
                    n += 1
                ve.sem_inc(emptied, 2)
                nc.vector.tensor_scalar(slope[:, :], score[:, :], SLOPE, None, ALU.mult)
                ve.drain()
                nc.vector.tensor_tensor(score[:, :], score[:, :], slope[:, :], ALU.max).then_inc(lin, 1)
                nc.vector.tensor_copy(node_h[:, :].rearrange("p (q h) -> p q h", h=HEADS), e["slot_node"][:, :].unsqueeze(2).to_broadcast([P, QP, HEADS])).then_inc(named, 1)
                for j, lane in enumerate((0, P - 1)):
                    nc.vector.tensor_copy(picks[:, j, :], c["ident"][:, lane:lane + 1].to_broadcast([P, P]))
                for g in range(G):
                    empty(turned[:, g * 512:(g + 1) * 512])
                for g in range(G):
                    empty(forth[:, g * 512:(g + 1) * 512])
                ve.drain()
                nc.vector.tensor_tensor(change[:, 1:W], forth[:, 1:W], forth[:, 0:W - 1], ALU.not_equal)
                ve.drain()
                nc.vector.tensor_scalar(change[:, 1:W], change[:, 1:W], NEG, None, ALU.mult)
                ve.drain()
                nc.vector.memset(change[:, 0:W + 1:P], NEG)
                ve.drain()
                nc.vector.tensor_tensor_scan(forth[:, :], change[:, 0:W], turned[:, :], NEG, ALU.add, ALU.max)
                nc.vector.tensor_tensor_scan(back[:, ::-1], change[:, W:0:-1], turned[:, ::-1], NEG, ALU.add, ALU.max)
                ve.drain()
                nc.vector.tensor_tensor(forth[:, :], forth[:, :], back[:, :], ALU.max).then_inc(scanned, 1)
                for g in range(G):
                    empty(back[:, g * 512:(g + 1) * 512])
                ve.drain().then_inc(topped, 1)
                top = back
                for g in range(G):
                    empty(turned[:, g * 512:(g + 1) * 512])
                for g in range(G):
                    empty(slope[:, g * 512:(g + 1) * 512])
                for j in range(2):
                    empty(ends[:, j, :])
                ve.drain()
                nc.vector.memset(joins[:, :], NEG)
                ve.drain()
                nc.vector.tensor_tensor(joins[:, 1:QP], ends[:, 0, 1:QP], ends[:, 1, 0:QP - 1], ALU.not_equal)
                nc.vector.tensor_tensor(whole[:, :], ends[:, 0, :], ends[:, 1, :], ALU.not_equal)
                for j in range(2):
                    nc.vector.tensor_tensor(apart[:, j, :], e["slot_node"][:, :], ends[:, j, :], ALU.not_equal)
                ve.drain()
                nc.vector.tensor_scalar(joins[:, 1:QP], joins[:, 1:QP], NEG, None, ALU.mult)
                nc.vector.tensor_scalar(whole[:, :], whole[:, :], NEG, None, ALU.mult)
                nc.vector.tensor_scalar(apart[:, :, :], apart[:, :, :], NEG, None, ALU.mult)
                ve.drain()
                nc.vector.tensor_tensor(step[:, 0, :], joins[:, 0:QP], whole[:, :], ALU.min)
                nc.vector.tensor_tensor(step[:, 1, :], joins[:, 1:QP + 1], whole[:, :], ALU.min)
                ve.drain()
                first_v = turned[:, :].rearrange("p (q h) -> p q h", h=HEADS)
                last_v = slope[:, :].rearrange("p (q h) -> p q h", h=HEADS)
                for hd in range(HEADS):
                    nc.vector.tensor_tensor_scan(last_v[:, :, hd], step[:, 0, :], last_v[:, :, hd], NEG, ALU.add, ALU.max)
                    nc.vector.tensor_tensor_scan(first_v[:, ::-1, hd], step[:, 1, ::-1], first_v[:, ::-1, hd], NEG, ALU.add, ALU.max)
                ve.drain()
                wide = [P, QP, HEADS]
                carry = node_h[:, :].rearrange("p (q h) -> p q h", h=HEADS)
                top_v = top[:, :].rearrange("p (q h) -> p q h", h=HEADS)
                nc.vector.memset(carry[:, 0, :], NEG)
                nc.vector.tensor_tensor(carry[:, 1:QP, :], last_v[:, 0:QP - 1, :], joins[:, 1:QP].unsqueeze(2).to_broadcast([P, QP - 1, HEADS]), ALU.add)
                ve.drain()
                nc.vector.tensor_tensor(carry, carry, apart[:, 0, :].unsqueeze(2).to_broadcast(wide), ALU.add)
                ve.drain()
                nc.vector.tensor_tensor(top_v, top_v, carry, ALU.max)
                ve.drain()
                nc.vector.memset(carry[:, QP - 1, :], NEG)
                nc.vector.tensor_tensor(carry[:, 0:QP - 1, :], first_v[:, 1:QP, :], joins[:, 1:QP].unsqueeze(2).to_broadcast([P, QP - 1, HEADS]), ALU.add)
                ve.drain()
                nc.vector.tensor_tensor(carry, carry, apart[:, 1, :].unsqueeze(2).to_broadcast(wide), ALU.add)
                ve.drain()
                nc.vector.tensor_tensor(top_v, top_v, carry, ALU.max)
                ve.drain()
                nc.vector.tensor_tensor(score[:, :], score[:, :], top[:, :], ALU.subtract).then_inc(bounded, 1)
                ve.wait_ge(exped, 1)


def attend(nc, x, acc):
    with Names(nc, "attend") as m:
        per = m.sb("per", [P, NT, HEADS])
        end = m.sem("end")
        acc_v = acc[:, :].rearrange("p (t d) -> p t d", d=HROW)
        with nc.Block() as block:
            @block.vector
            def _(ve):
                nc.vector.tensor_scalar(per[:, :, :], acc_v[:, :, D:HROW], 1e-16, None, ALU.add)
                ve.drain()
                nc.vector.reciprocal(per[:, :, :], per[:, :, :])
                ve.drain()
                for hd in range(HEADS):
                    mine = acc_v[:, :, hd * HD:(hd + 1) * HD]
                    nc.vector.tensor_tensor(mine, mine, per[:, :, hd].unsqueeze(2).to_broadcast([P, NT, HD]), ALU.mult)
                ve.drain()
                nc.vector.tensor_tensor(x[:, :, :], x[:, :, :], acc_v[:, :, 0:D], ALU.add).then_inc(end, 1)
                ve.wait_ge(end, 1)


def feed_forward(nc, layer, c, a, x, dram, out):
    tag = layer["name"]
    with Names(nc, f"ffn{tag}") as m:
        r = dict(weight=m.sb("weight", [P, TOP, NT]), pos=m.sb("pos", [P, NT, TOP], I32), owner=m.sb("owner", [1, layer["blocks"]], I32))
        xs_d, ys_d = dram(f"xs_{tag}", [layer["blocks"] * P, D]), dram(f"ys_{tag}", [layer["blocks"] * P, D])
        first = tag == "L0"
        z_d = None if first else dram(f"z_{tag}", [NR, D])
        gate, bias = (a["L0_ffn_Wr"], a["L0_ffn_br"]) if first else (a["L1_ffn_gate_w"], a["L1_ffn_gate_b"])
        route(nc, layer, c, a, x, r, gate, bias, z_d, xs_d, first)
        experts(nc, layer, c, a, r, xs_d, ys_d)
        if first:
            combine(nc, layer, r, ys_d, x, None)
        else:
            with Names(nc, "last") as k:
                z = k.sb("z", [P, NT, D])
                combine(nc, layer, r, ys_d, z, lambda mm: Finish(nc, mm, a, x, z, z_d, out))


def build(nc, a, out):
    with Names.whole, Names(nc, "all") as keep:
        def dram(name, shape, dt=F32):
            return nc.dram_tensor(name, shape, dt, kind="Internal").ap()

        sb = keep.sb
        c = dict(ident=sb("ident", [P, P]), before=sb("before", [P, P]), upto=sb("upto", [P, P]), ones=sb("ones", [P, P]),
                 count_f=sb("count_f", [P, QP]), count_h=sb("count_h", [P, QP], FP16), count_b=sb("count_b", [P, P], BF16),
                 lane_f=sb("lane_f", [P, 1]))
        e = dict(degree=sb("degree", [P, NT]), tile_f=sb("tile_f", [P, QP]), tile_i=sb("tile_i", [1, QP], I32),
                 slot_dst=sb("slot_dst", [P, QP], I32), slot_src=sb("slot_src", [P, QP]), slot_node=sb("slot_node", [P, QP]))
        x = sb("x", [P, NT, D])
        constants(nc, c)
        with Names(nc, "gnn0") as m:
            z = m.sb("z", [P, NT, D])
            z_d = dram("z_gnn0", [NR, D])
            first_norm(nc, a["x"], x, z, z_d)
            sort_edges(nc, c, e, a["src"], a["dst"], dram("low_lanes", [EC, P], BF16))
            acc = m.sb("acc", [P, NT * HROW])
            aggregate(nc, "sum0", c, e, z_d, D, acc)
            mean_layer(nc, c, e, a, x, z, acc)
        feed_forward(nc, LAYERS[0], c, a, x, dram, out)
        with Names(nc, "gnn1") as m:
            score = m.sb("score", [P, QP * HEADS])
            h_d = dram("h_gnn1", [NR, HROW])
            with Names(nc, "gnn1a") as k:
                h = k.sb("h", [P, NT * HROW])
                coef = k.sb("coef", [P, 2 * D])
                heads(nc, c, a, x, h, h_d, coef)
                scores(nc, c, e, h, h_d, coef, score)
            edge_softmax(nc, c, e, score)
            acc = m.sb("acc1", [P, NT * HROW])
            aggregate(nc, "sum1", c, e, h_d, HROW, acc, score)
            attend(nc, x, acc)
        feed_forward(nc, LAYERS[1], c, a, x, dram, out)


def kernel(**inputs):
    import numpy as np
    import concourse.bacc as bacc
    from concourse.bass_utils import run_bass_kernel_spmd

    laid = dict(inputs)
    for name in ("L0_gnn_W1", "L0_gnn_W2"):
        laid[name] = np.transpose(laid[name])
    laid["L1_gnn_W"] = np.transpose(laid["L1_gnn_W"], (1, 0, 2)).reshape(D, HEADS * HD)

    def on_partitions(v):
        return np.transpose(np.reshape(v, (v.shape[0], -1, P)), (2, 0, 1))
    for name in ("L0_ffn_b1", "L1_ffn_b1", "L0_ffn_ln_g", "L0_ffn_ln_b"):
        laid[name] = on_partitions(np.asarray(laid[name]))
    nc = bacc.Bacc("TRN2", target_bir_lowering=False, num_devices=1)
    arrays, args = {}, {}
    for name, v in laid.items():
        v = np.ascontiguousarray(v)
        arrays[f"in_{name}"] = v
        args[name] = nc.dram_tensor(f"in_{name}", v.shape, mybir.dt.from_np(v.dtype), kind="ExternalInput").ap()
    out = nc.dram_tensor("out_x", (N, D), F32, kind="ExternalOutput").ap()
    build(nc, args, out)
    return run_bass_kernel_spmd(nc, [arrays], core_ids=[0]).results[0]["out_x"]
```

```python
import concourse.bass as bass
from concourse import mybir
from contextlib import ExitStack

F32 = mybir.dt.float32
BF16 = mybir.dt.bfloat16
FP16 = mybir.dt.float16
I32 = mybir.dt.int32
ALU = mybir.AluOpType
ACT = mybir.ActivationFunctionType
AX = mybir.AxisListType.X

P = 128
N, D, E = 3125, 256, 53125
KD = D // P
NT = -(-N // P)
TAIL = N - (NT - 1) * P
NR = NT * P
BINS = NT + 1
EC = -(-E // P)
Q = (E + NT * (P - 1)) // P
HALF = 10
SLOTS = 2 * HALF
PAIRS = SLOTS // 2
Q = -(-Q // SLOTS) * SLOTS
QP = -(-Q // 16) * 16
NOWHERE = QP * P
MID = N // 2
HEADS, HD = 8, 32
HPART = HD // KD
HROW = D + HEADS
DEPTH = 4
PIECE = 13
NP = EC // PIECE
NEG = -1.0e38
SLOPE = 0.2
ROWG = EC // 4
TOP = 2
LAYERS = (dict(name="L0", experts=8, hidden=1024), dict(name="L1", experts=16, hidden=512))
for layer in LAYERS:
    layer["blocks"] = (TOP * N + layer["experts"] * (P - 1)) // P


class Names:

    whole = ExitStack()

    def __init__(self, nc, stage):
        self.nc, self.stage, self.ctx, self.sems = nc, stage, ExitStack(), []

    def __enter__(self):
        return self

    def __exit__(self, *error):
        if self.sems and error[0] is None:
            with self.nc.Block() as block:
                @block.gpsimd
                def _(pool):
                    for one in self.sems:
                        pool.sem_clear(one)
        return self.ctx.__exit__(*error)

    def sb(self, name, shape, dt=F32):
        return self.ctx.enter_context(self.nc.sbuf_tensor(f"{self.stage}_{name}", shape, dt))

    def ps(self, name, dt=F32):
        return self.ctx.enter_context(self.nc.psum_tensor(f"{self.stage}_{name}", [P, 512], dt))

    def gather_sem(self, name):
        return Names.whole.enter_context(self.nc.semaphore(f"{self.stage}_{name}"))

    def sem(self, name):
        self.sems.append(self.ctx.enter_context(self.nc.semaphore(f"{self.stage}_{name}")))
        return self.sems[-1]


def rows(dram, t0, t1):
    return dram[t0 * P:t1 * P, :].rearrange("(t p) d -> p t d", p=P)


def load_nodes(eng, tiles, dram, sem):
    eng.dma_start(tiles[:, 0:NT - 1, :], rows(dram, 0, NT - 1)).then_inc(sem, 16)
    eng.dma_start(tiles[0:TAIL, NT - 1, :], dram[(NT - 1) * P:N, :]).then_inc(sem, 16)


def per_tile(ap, inner):
    return ap.unsqueeze(2).to_broadcast([P, NT, inner])


def tile_of(x, t):
    return x[:, bass.ds(t, 1), :].rearrange("p t d -> p (t d)")


class Norm:
    GROUP = 5
    MINE = 3

    def __init__(self, m, tag):
        self.stats = m.sb(f"{tag}_stats", [P, NT, 6])
        self.mean = m.sb(f"{tag}_mean", [P, NT])
        self.var = m.sb(f"{tag}_var", [P, NT])
        self.gap = m.sb(f"{tag}_gap", [P, NT])
        self.root = m.sb(f"{tag}_root", [P, NT])
        self.scale = m.sb(f"{tag}_scale", [P, NT])
        self.shift = m.sb(f"{tag}_shift", [P, NT])
        self.var_ready = m.sem(f"{tag}_var_ready")
        self.rooted = m.sem(f"{tag}_rooted")
        self.scaled = m.sem(f"{tag}_scaled")

    def over_tiles(self, eng, first, last, step):
        with eng.Fori(0, NT // self.GROUP) as i:
            for j in range(first, last):
                op = step(self.GROUP * i + j)
        return op

    def vector(self, nc, ve, x, z, done):
        self.over_tiles(ve, 0, self.GROUP, lambda t: nc.vector.bn_stats(self.stats[:, bass.ds(t, 1), :].rearrange("p t s -> p (t s)"), tile_of(x, t)))
        ve.drain()
        nc.vector.tensor_tensor(self.mean[:, :], self.stats[:, :, 1], self.stats[:, :, 4], ALU.add)
        nc.vector.tensor_tensor(self.gap[:, :], self.stats[:, :, 1], self.stats[:, :, 4], ALU.subtract)
        nc.vector.tensor_tensor(self.var[:, :], self.stats[:, :, 2], self.stats[:, :, 5], ALU.add)
        ve.drain()
        nc.vector.scalar_tensor_tensor(self.gap[:, :], self.gap[:, :], 0.25, self.gap[:, :], ALU.mult, ALU.mult)
        nc.vector.tensor_scalar(self.var[:, :], self.var[:, :], 1.0 / D, 1e-5, ALU.mult, ALU.add)
        nc.vector.tensor_scalar(self.mean[:, :], self.mean[:, :], 0.5, None, ALU.mult)
        ve.drain()
        nc.vector.tensor_tensor(self.var[:, :], self.var[:, :], self.gap[:, :], ALU.add).then_inc(self.var_ready, 1)
        ve.wait_ge(self.rooted, 1)
        nc.vector.reciprocal(self.scale[:, :], self.root[:, :])
        ve.drain()
        nc.vector.scalar_tensor_tensor(self.shift[:, :], self.mean[:, :], -1.0, self.scale[:, :], ALU.mult, ALU.mult).then_inc(self.scaled, 1)
        self.over_tiles(ve, 0, self.MINE, lambda t: nc.vector.tensor_scalar(
            tile_of(z, t), tile_of(x, t), self.mean[:, bass.ds(t, 1)], self.scale[:, bass.ds(t, 1)], ALU.subtract, ALU.mult))
        ve.drain().then_inc(done, 1)

    def scalar(self, nc, act, x, z, done):
        act.wait_ge(self.var_ready, 1)
        nc.scalar.activation(self.root[:, :], self.var[:, :], ACT.Sqrt).then_inc(self.rooted, 1)
        act.wait_ge(self.scaled, 1)
        act.sem_inc(self.scaled, 1)
        self.over_tiles(act, self.MINE, self.GROUP, lambda t: nc.scalar.activation(
            tile_of(z, t), tile_of(x, t), ACT.Identity, bias=self.shift[:, bass.ds(t, 1)], scale=self.scale[:, bass.ds(t, 1)]))
        act.drain().then_inc(done, 1)


def constants(nc, c):
    with Names(nc, "const") as m:
        count = m.sb("count", [P, QP], I32)
        lane = m.sb("lane", [P, 1], I32)
        made = m.sem("made")
        copied = m.sem("copied")
        with nc.Block() as block:
            @block.gpsimd
            def _(pool):
                nc.gpsimd.iota(count[:, :], pattern=[[1, QP]], base=0, channel_multiplier=0).then_inc(made, 1)
                nc.gpsimd.iota(lane[:, :], pattern=[[0, 1]], base=0, channel_multiplier=1).then_inc(made, 1)
                nc.gpsimd.memset(c["ident"][:, :], 0.0).then_inc(made, 1)
                nc.gpsimd.memset(c["before"][:, :], 1.0).then_inc(made, 1)
                nc.gpsimd.memset(c["upto"][:, :], 1.0).then_inc(made, 1)
                nc.gpsimd.memset(c["ones"][:, :], 1.0).then_inc(made, 1)
                pool.wait_ge(made, 6)
                nc.gpsimd.affine_select(out=c["ident"][:, :], in_=c["ident"][:, :], compare_op=ALU.not_equal, fill=1.0,
                                        base=0, pattern=[[-1, P]], channel_multiplier=1).then_inc(made, 1)
                nc.gpsimd.affine_select(out=c["before"][:, :], in_=c["before"][:, :], compare_op=ALU.is_gt, fill=0.0,
                                        base=0, pattern=[[1, P]], channel_multiplier=-1).then_inc(made, 1)
                nc.gpsimd.affine_select(out=c["upto"][:, :], in_=c["upto"][:, :], compare_op=ALU.is_ge, fill=0.0,
                                        base=0, pattern=[[1, P]], channel_multiplier=-1).then_inc(made, 1)
                nc.gpsimd.memset(c["by_head"][:, HEADS:], 0.0)
                nc.gpsimd.memset(c["by_head"][:, 0:HEADS], 1.0).then_inc(made, 1)
                pool.wait_ge(made, 10)
                nc.gpsimd.affine_select(out=c["by_head"][:, 0:HEADS], in_=c["by_head"][:, 0:HEADS], compare_op=ALU.is_ge, fill=0.0,
                                        base=0, pattern=[[-HPART, HEADS]], channel_multiplier=1).then_inc(made, 1)
                pool.wait_ge(made, 11)
                nc.gpsimd.affine_select(out=c["by_head"][:, 0:HEADS], in_=c["by_head"][:, 0:HEADS], compare_op=ALU.is_gt, fill=0.0,
                                        base=HPART, pattern=[[HPART, HEADS]], channel_multiplier=-1).then_inc(made, 1)
                pool.wait_ge(made, 12)

            @block.vector
            def _(ve):
                ve.wait_ge(made, 2)
                nc.vector.tensor_copy(c["count_f"][:, :], count[:, 0:P])
                nc.vector.tensor_copy(c["count_h"][:, :], count[:, :])
                nc.vector.tensor_copy(c["count_b"][:, :], count[:, 0:P])
                nc.vector.tensor_copy(c["lane_f"][:, :], lane[:, :])
                ve.wait_ge(made, 9)
                nc.vector.tensor_copy(c["before_b"][:, :], c["before"][:, :])
                nc.vector.tensor_copy(c["ones_b"][:, :], c["ones"][:, :]).then_inc(copied, 1)
                ve.wait_ge(copied, 1)


def sort_edges(nc, c, e, src, dst, low_d, slot_d):
    with Names(nc, "sort") as m:
        src_rows = m.sb("src_rows", [ROWG, 4, P], I32)
        dst_rows = m.sb("dst_rows", [ROWG, 4, P], I32)
        rows_f = m.sb("rows_f", [ROWG, 2, 4, P])
        low_i = m.sb("low_i", [ROWG, 4, P], I32)
        low_rows = m.sb("low_rows", [ROWG, 4, P], BF16)
        col_i = m.sb("col_i", [P, EC], I32)
        part_i = m.sb("part_i", [P, 2, EC], I32)
        low1_f = m.sb("low1_f", [P, EC])
        dst_f = m.sb("dst_f", [P, EC])
        low_col = m.sb("low_col", [P, EC], BF16)
        tile_col = m.sb("tile_col", [P, EC], BF16)
        in_tile = m.sb("in_tile", [P, EC, BINS], BF16)
        prior = m.sb("prior", [P, (EC + 1) * BINS])
        pos = m.sb("pos", [P, EC])
        pos_i = m.sb("pos_i", [P, EC], I32)
        pos_q = m.sb("pos_q", [P, EC])
        pos_r = m.sb("pos_r", [P, EC])
        low_b = m.sb("low_b", [P, DEPTH, PIECE * P], BF16)
        lane_hot = m.sb("lane_hot", [P, DEPTH, PIECE * P], BF16)
        same = m.sb("same", [P, DEPTH, PIECE * P], BF16)
        earlier = m.sb("earlier", [P, DEPTH, PIECE * P], BF16)
        high = m.sb("high", [P, DEPTH, PIECE * BINS], BF16)
        rest = m.sb("rest", [P, DEPTH, PIECE * BINS], BF16)
        tiles = m.sb("tiles", [P, DEPTH, PIECE * BINS], BF16)
        chosen = m.sb("chosen", [P, PIECE, BINS])
        start = m.sb("start", [P, BINS])
        counts_i = m.sb("counts_i", [P, BINS], I32)
        chunks_f = m.sb("chunks_f", [P, BINS])
        upto_f = m.sb("upto_f", [P, BINS])
        zeros = m.sb("zeros", [P, EC])
        tcol_i = m.sb("tcol_i", [BINS, 1], I32)
        tcol_f = m.sb("tcol_f", [BINS, 1])
        tcum_f = m.sb("tcum_f", [BINS, 1])
        tile_f = m.sb("tile_f", [P, QP])
        past = m.sb("past", [BINS, QP])
        chunk_hot = m.sb("chunk_hot", [P, 4, QP], FP16)
        lane_of = m.sb("lane_of", [P, 4, P], FP16)
        dst_hot = m.sb("dst_hot", [P, 4, P], FP16)
        src_hot = m.sb("src_hot", [P, 4, P], FP16)
        nothing = m.sb("nothing", [P, QP], FP16)
        slot_rows = m.sb("slot_rows", [P, -(-QP // P), P], FP16)
        ps = [m.ps(f"ps{i}") for i in range(4)]
        ps_dst, ps_src, ps_x = m.ps("ps_dst"), m.ps("ps_src"), m.ps("ps_x")

        filled, loaded, low_ready, low_out = m.sem("filled"), m.sem("loaded"), m.sem("low_ready"), m.sem("low_out")
        rows_ready, turned, cols_ready = m.sem("rows_ready"), m.sem("turned"), m.sem("cols_ready")
        hot_ready, counted, kept = m.sem("hot_ready"), m.sem("counted"), m.sem("kept")
        sums_ready, sums_done, tcol_ready, tcum_done = m.sem("sums_ready"), m.sem("sums_done"), m.sem("tcol_ready"), m.sem("tcum_done")
        tcum_ready, tile_done = m.sem("tcum_ready"), m.sem("tile_done")
        past_ready = m.sem("past_ready")
        low_in = [m.sem(f"low_in{s}") for s in range(DEPTH)]
        first_ready, high_ready, rest_ready, tiles_ready = m.sem("first_ready"), m.sem("high_ready"), m.sem("rest_ready"), m.sem("tiles_ready")
        scaled = m.sem("scaled")
        lane_ready, same_ready, earlier_ready = m.sem("lane_ready"), m.sem("same_ready"), m.sem("earlier_ready")
        looked, picked = m.sem("looked"), m.sem("picked")
        place_ready, placed, all_placed, end = m.sem("place_ready"), m.sem("placed"), m.sem("all_placed"), m.sem("end")
        slots_ready, slots_turned, rows_kept, rows_out = m.sem("slots_ready"), m.sem("slots_turned"), m.sem("rows_kept"), m.sem("rows_out")
        tick = m.sem("tick")
        prior_v = prior[:, :].rearrange("p (c t) -> p c t", t=BINS)
        full = E - 3 * ROWG * P

        with nc.Block() as block:
            @block.sync
            def _(sp):
                sp.wait_ge(filled, 1)
                for rows_i, edges in ((src_rows, src), (dst_rows, dst)):
                    for g in range(3):
                        sp.dma_start(rows_i[:, g, :], edges[g * ROWG * P:(g + 1) * ROWG * P].rearrange("(c e) -> c e", e=P)).then_inc(loaded, 16)
                    sp.dma_start(rows_i[0:full // P, 3, :], edges[3 * ROWG * P:3 * ROWG * P + full // P * P].rearrange("(c e) -> c e", e=P)).then_inc(loaded, 16)
                    sp.dma_start(rows_i[full // P:full // P + 1, 3, 0:full % P], edges[E - full % P:E].rearrange("(c e) -> c e", c=1)).then_inc(loaded, 16)
                sp.wait_ge(low_ready, 1)
                for g in range(4):
                    sp.dma_start(low_d[g * ROWG:(g + 1) * ROWG, :], low_rows[:, g, :]).then_inc(low_out, 16)
                sp.wait_ge(low_out, 64)

                def spread(piece, s):
                    sp.dma_start(low_b[:, s, :], low_d[bass.ds(piece * PIECE, PIECE), :].rearrange("c e -> (c e)").partition_broadcast(P)).then_inc(low_in[s], 16)
                for s in range(DEPTH):
                    spread(s, s)
                with sp.Fori(1, NP // DEPTH) as i:
                    for s in range(DEPTH):
                        sp.wait_ge(same_ready, DEPTH * (i - 1) + s + 1)
                        spread(DEPTH * i + s, s)
                sp.wait_ge(rows_kept, 1)
                for g in range(-(-QP // P)):
                    n = min(P, QP - g * P)
                    sp.dma_start(slot_d[g * P:g * P + n, :], slot_rows[0:n, g, :]).then_inc(rows_out, 16)
                sp.wait_ge(rows_out, 16 * -(-QP // P))

            @block.gpsimd
            def _(pool):
                with pool.Fori(0, NP // DEPTH) as i:
                    for s in range(DEPTH):
                        pool.wait_ge(same_ready, DEPTH * i + s + 1)
                        pool.wait_ge(looked, DEPTH * i + s + 1)
                        pool.sem_inc(tick, 1)
                        nc.gpsimd.affine_select(out=earlier[:, s, :].rearrange("p (c e) -> p c e", e=P),
                                                in_=same[:, s, :].rearrange("p (c e) -> p c e", e=P),
                                                compare_op=ALU.is_gt, fill=0.0, base=0, pattern=[[0, PIECE], [1, P]],
                                                channel_multiplier=-1).then_inc(earlier_ready, 1)

            @block.scalar
            def _(act):
                act.sem_inc(kept, 2)
                with act.Fori(0, NP // 2) as i:
                    for s in range(2):
                        act.wait_ge(counted, 2 + 2 * i + s + 1)
                        act.sem_inc(tick, 1)
                        nc.scalar.activation(prior[:, bass.ds(((2 * i + s) * PIECE + 1) * BINS, PIECE * BINS)],
                                             ps[s][:, 0:PIECE * BINS], ACT.Copy).then_inc(kept, 1)
                act.wait_ge(first_ready, 1)
                act.sem_inc(tick, 1)
                with act.Fori(0, NP // DEPTH) as i:
                    for s in range(DEPTH):
                        piece = bass.ds((DEPTH * i + s) * PIECE, PIECE)
                        act.wait_ge(looked, DEPTH * i + s + 1)
                        act.sem_inc(tick, 1)
                        nc.scalar.activation(high[:, s, :], prior_v[:, piece, :].rearrange("p c t -> p (c t)"), ACT.Copy).then_inc(high_ready, 1)
                        nc.scalar.activation(tiles[:, s, :], in_tile[:, piece, :].rearrange("p c t -> p (c t)"), ACT.Copy).then_inc(tiles_ready, 1)
                with act.Fori(0, EC // 4) as i:
                    for s in range(4):
                        k = 4 * i + s
                        act.wait_ge(place_ready, 1 + k + 1)
                        act.wait_ge(placed, k + 1)
                        act.sem_inc(tick, 1)
                        if s % 2 == 0:
                            nc.scalar.activation(src_hot[:, s, :], lane_of[:, s, :], ACT.Copy, scale=low1_f[:, bass.ds(k, 1)])
                        nc.scalar.activation(dst_hot[:, s, :], lane_of[:, s, :], ACT.Copy, scale=dst_f[:, bass.ds(k, 1)]).then_inc(scaled, 1)

            @block.tensor
            def _(pe):
                pe.wait_ge(rows_ready, 1)
                for k in range(2):
                    for g in range(4):
                        last = nc.tensor.transpose(ps[2 + k][:, g * ROWG:(g + 1) * ROWG], rows_f[:, k, g, :], c["ident"][0:ROWG, 0:ROWG])
                last.then_inc(turned, 1)
                pe.sem_inc(counted, 2)
                with pe.Fori(0, NP // 2) as i:
                    for s in range(2):
                        pe.wait_ge(hot_ready, 2 * i + s + 1)
                        pe.wait_ge(kept, 2 * i + s + 1)
                        pe.sem_inc(tick, 1)
                        for j in range(PIECE):
                            last = nc.tensor.matmul(ps[s][:, j * BINS:(j + 1) * BINS], same[:, s, j * P:(j + 1) * P],
                                                    in_tile[:, bass.ds((2 * i + s) * PIECE + j, 1), :].rearrange("p c t -> p (c t)"),
                                                    start=True, stop=True)
                        last.then_inc(counted, 1)
                pe.wait_ge(sums_ready, 1)
                total = prior_v[:, EC, :]
                nc.tensor.matmul(ps_x[:, 0:BINS], c["ones"][:, :], total, start=True, stop=True)
                nc.tensor.matmul(ps_x[:, BINS:2 * BINS], c["before"][:, :], total, start=True, stop=True)
                nc.tensor.matmul(ps_x[0:BINS, 2 * BINS:2 * BINS + 1], total, c["ones"][:, 0:1], start=True, stop=True).then_inc(sums_done, 1)
                pe.wait_ge(tcol_ready, 1)
                nc.tensor.matmul(ps[3][0:BINS, 0:1], c["upto"][0:BINS, 0:BINS], tcol_f[:, :], start=True, stop=True).then_inc(tcum_done, 1)
                pe.wait_ge(past_ready, 1)
                nc.tensor.matmul(ps[2][:, 0:QP], c["ones"][0:NT, :], past[0:NT, :], start=True, stop=True).then_inc(tile_done, 1)
                pe.sem_inc(looked, DEPTH)
                with pe.Fori(0, NP // DEPTH) as i:
                    for s in range(DEPTH):
                        n = DEPTH * i + s
                        pe.wait_ge(lane_ready, n + 1)
                        pe.wait_ge(rest_ready, n + 1)
                        pe.wait_ge(earlier_ready, n + 1)
                        pe.wait_ge(tiles_ready, n + 1)
                        pe.wait_ge(picked, n + 1)
                        pe.sem_inc(tick, 1)
                        for j in range(PIECE):
                            bins = slice(j * BINS, (j + 1) * BINS)
                            hot = lane_hot[:, s, j * P:(j + 1) * P]
                            nc.tensor.matmul(ps[s][:, bins], hot, high[:, s, bins], start=True, stop=False)
                            nc.tensor.matmul(ps[s][:, bins], hot, rest[:, s, bins], start=False, stop=False)
                            last = nc.tensor.matmul(ps[s][:, bins], earlier[:, s, j * P:(j + 1) * P], tiles[:, s, bins], start=False, stop=True)
                        last.then_inc(looked, 1)
                pe.wait_ge(place_ready, 1)
                nc.tensor.matmul(ps_dst[:, 0:QP], nothing[:, 0:P], nothing[:, :], start=True, stop=False)
                nc.tensor.matmul(ps_src[:, 0:QP], nothing[:, 0:P], nothing[:, :], start=True, stop=False)
                pe.sem_inc(placed, 4)
                with pe.Fori(0, EC // 4) as i:
                    for s in range(4):
                        pe.wait_ge(scaled, 4 * i + s + 1)
                        pe.sem_inc(tick, 1)
                        nc.tensor.matmul(ps_dst[:, 0:QP], dst_hot[:, s, :], chunk_hot[:, s, :], start=False, stop=False)
                        nc.tensor.matmul(ps_src[:, 0:QP], src_hot[:, s, :], chunk_hot[:, s, :], start=False, stop=False).then_inc(placed, 1)
                nc.tensor.matmul(ps_dst[:, 0:QP], nothing[:, 0:P], nothing[:, :], start=False, stop=True)
                nc.tensor.matmul(ps_src[:, 0:QP], nothing[:, 0:P], nothing[:, :], start=False, stop=True).then_inc(all_placed, 1)
                pe.wait_ge(slots_ready, 1)
                for g in range(-(-QP // P)):
                    n = min(P, QP - g * P)
                    last = nc.tensor.transpose(ps_x[0:n, g * P:(g + 1) * P], e["slot_src"][:, g * P:g * P + n], c["ident"][:, :])
                last.then_inc(slots_turned, 1)

            @block.vector
            def _(ve):
                nc.vector.memset(src_rows[:, :, :], NT * P)
                nc.vector.memset(dst_rows[:, :, :], 0).then_inc(filled, 1)
                nc.vector.memset(zeros[:, :], 0.0)
                nc.vector.memset(nothing[:, :], 0.0).then_inc(place_ready, 1)
                nc.vector.memset(prior[:, 0:BINS], 0.0)
                ve.wait_ge(loaded, 160)
                nc.vector.tensor_copy(rows_f[:, 0, :, :], src_rows[:, :, :])
                nc.vector.tensor_copy(rows_f[:, 1, :, :], dst_rows[:, :, :]).then_inc(rows_ready, 1)
                nc.vector.tensor_scalar(low_i[:, :, :], src_rows[:, :, :], P - 1, None, ALU.bitwise_and)
                ve.drain()
                nc.vector.tensor_copy(low_rows[:, :, :], low_i[:, :, :]).then_inc(low_ready, 1)
                ve.wait_ge(turned, 1)
                nc.vector.tensor_copy(col_i[:, :], ps[2][:, 0:EC])
                nc.vector.tensor_scalar(dst_f[:, :], ps[3][:, 0:EC], -float(MID), None, ALU.add)
                ve.drain()
                nc.vector.tensor_scalar(part_i[:, 0, :], col_i[:, :], P - 1, None, ALU.bitwise_and)
                nc.vector.tensor_scalar(part_i[:, 1, :], col_i[:, :], 7, None, ALU.arith_shift_right)
                ve.drain()
                nc.vector.tensor_copy(low_col[:, :], part_i[:, 0, :])
                nc.vector.tensor_scalar(low1_f[:, :], part_i[:, 0, :], 1.0, None, ALU.add)
                nc.vector.tensor_copy(tile_col[:, :], part_i[:, 1, :])
                ve.drain()
                nc.vector.tensor_tensor(in_tile[:, :, :], tile_col[:, :].unsqueeze(2).to_broadcast([P, EC, BINS]),
                                        c["count_b"][:, 0:BINS].unsqueeze(1).to_broadcast([P, EC, BINS]), ALU.is_equal)
                ve.drain()
                with ve.Fori(0, NP // 2) as i:
                    for s in range(2):
                        ve.wait_ge(counted, 2 * i + s + 1)
                        nc.vector.tensor_tensor(same[:, s, :].rearrange("p (c e) -> p c e", e=P),
                                                low_col[:, bass.ds((2 * i + s) * PIECE, PIECE)].unsqueeze(2).to_broadcast([P, PIECE, P]),
                                                c["count_b"][:, :].unsqueeze(1).to_broadcast([P, PIECE, P]), ALU.is_equal).then_inc(hot_ready, 1)
                ve.wait_ge(kept, 2 + NP)
                with ve.Fori(0, BINS) as t:
                    sl = prior_v[:, 1:EC + 1, bass.ds(t, 1)].rearrange("p c t -> p (c t)")
                    nc.vector.tensor_tensor_scan(sl, zeros[:, :], sl, 0.0, ALU.add, ALU.add)
                ve.drain()
                nc.vector.tensor_copy(e["degree"][:, :], prior_v[:, EC, 0:NT]).then_inc(sums_ready, 1)
                ve.wait_ge(sums_done, 1)
                nc.vector.tensor_scalar(counts_i[:, :], ps_x[:, 0:BINS], float(P - 1), None, ALU.add)
                nc.vector.tensor_scalar(tcol_i[:, :], ps_x[0:BINS, 2 * BINS:2 * BINS + 1], float(P - 1), None, ALU.add)
                ve.drain()
                nc.vector.tensor_scalar(counts_i[:, :], counts_i[:, :], 7, None, ALU.arith_shift_right)
                nc.vector.tensor_scalar(tcol_i[:, :], tcol_i[:, :], 7, None, ALU.arith_shift_right)
                ve.drain()
                nc.vector.tensor_copy(tcol_f[:, :], tcol_i[:, :]).then_inc(tcol_ready, 1)
                nc.vector.tensor_copy(chunks_f[:, :], counts_i[:, :])
                ve.drain()
                nc.vector.tensor_tensor_scan(upto_f[:, :], zeros[:, 0:BINS], chunks_f[:, :], 0.0, ALU.add, ALU.add)
                ve.drain()
                nc.vector.tensor_tensor(start[:, :], upto_f[:, :], chunks_f[:, :], ALU.subtract)
                ve.drain()
                nc.vector.scalar_tensor_tensor(start[:, :], start[:, :], float(P), ps_x[:, BINS:2 * BINS], ALU.mult, ALU.add)
                ve.drain()
                nc.vector.memset(start[:, NT:BINS], float(NOWHERE))
                ve.drain()
                nc.vector.tensor_tensor(prior_v[:, 0:EC, :], prior_v[:, 0:EC, :], start[:, :].unsqueeze(1).to_broadcast([P, EC, BINS]),
                                        ALU.add).then_inc(first_ready, 1)
                ve.wait_ge(tcum_done, 1)
                nc.vector.tensor_copy(tcum_f[:, :], ps[3][0:BINS, 0:1])
                ve.drain()
                nc.vector.tensor_scalar(past[:, :], c["count_h"][0:BINS, :], tcum_f[:, 0:1], None, ALU.is_ge).then_inc(past_ready, 1)
                ve.wait_ge(tile_done, 1)
                nc.vector.tensor_scalar(tile_f[:, :], ps[2][:, 0:QP], 1.0, None, ALU.mult)
                nc.vector.tensor_scalar(e["tile_i"][:, :], ps[2][0:1, 0:QP], float(NT - 1), None, ALU.min)
                def compare(piece, s):
                    nc.vector.tensor_scalar(lane_hot[:, s, :], low_b[:, s, :], c["lane_f"][:, 0:1], None, ALU.is_equal).then_inc(lane_ready, 1)
                    nc.vector.tensor_tensor(same[:, s, :].rearrange("p (c e) -> p c e", e=P),
                                            low_b[:, s, :].rearrange("p (c e) -> p c e", e=P),
                                            low_col[:, bass.ds(piece * PIECE, PIECE)].unsqueeze(2).to_broadcast([P, PIECE, P]),
                                            ALU.is_equal).then_inc(same_ready, 1)

                def split(piece, s):
                    ve.wait_ge(high_ready, piece + 1)
                    ve.sem_inc(tick, 1)
                    nc.vector.tensor_tensor(rest[:, s, :], prior_v[:, bass.ds(piece * PIECE, PIECE), :].rearrange("p c t -> p (c t)"),
                                            high[:, s, :], ALU.subtract).then_inc(rest_ready, 1)

                def pick(piece, s):
                    ve.wait_ge(looked, DEPTH + piece + 1)
                    ve.sem_inc(tick, 1)
                    nc.vector.tensor_tensor(chosen[:, :, :], ps[s][:, 0:PIECE * BINS].rearrange("p (c t) -> p c t", t=BINS),
                                            in_tile[:, bass.ds(piece * PIECE, PIECE), :], ALU.mult).then_inc(picked, 1)
                    ve.drain()
                    nc.vector.tensor_reduce(pos[:, bass.ds(piece * PIECE, PIECE)], chosen[:, :, :], AX, ALU.add)
                    ve.drain()

                def look(piece, s, turn):
                    ve.wait_ge(low_in[s], turn)
                    ve.sem_inc(tick, 1)
                    compare(piece, s)
                    split(piece, s)

                lag = DEPTH - 1
                ve.sem_inc(picked, DEPTH)
                for s in range(DEPTH):
                    if s >= lag:
                        pick(s - lag, s - lag)
                    look(s, s, 16)
                with ve.Fori(1, NP // DEPTH) as i:
                    for s in range(DEPTH):
                        pick(DEPTH * i + s - lag, (s - lag) % DEPTH)
                        look(DEPTH * i + s, s, 16 * i + 16)
                for n in range(NP - lag, NP):
                    pick(n, n % DEPTH)
                ve.drain()
                nc.vector.tensor_copy(pos_i[:, :], pos[:, :])
                ve.drain()
                nc.vector.tensor_scalar(part_i[:, 0, :], pos_i[:, :], P - 1, None, ALU.bitwise_and)
                nc.vector.tensor_scalar(part_i[:, 1, :], pos_i[:, :], 7, None, ALU.arith_shift_right)
                ve.drain()
                nc.vector.tensor_copy(pos_r[:, :], part_i[:, 0, :])
                nc.vector.tensor_copy(pos_q[:, :], part_i[:, 1, :])
                ve.drain()
                with ve.Fori(0, EC // 4) as i:
                    for s in range(4):
                        k = 4 * i + s
                        ve.wait_ge(placed, 4 * i + s + 1)
                        nc.vector.tensor_scalar(chunk_hot[:, s, :], c["count_h"][:, :], pos_q[:, bass.ds(k, 1)], None, ALU.is_equal)
                        if s % 2:
                            nc.vector.tensor_scalar(src_hot[:, s, :], c["count_h"][:, 0:P], pos_r[:, bass.ds(k, 1)], low1_f[:, bass.ds(k, 1)], ALU.is_equal, ALU.mult)
                        nc.vector.tensor_scalar(lane_of[:, s, :], c["count_h"][:, 0:P], pos_r[:, bass.ds(k, 1)], None, ALU.is_equal).then_inc(place_ready, 1)
                ve.wait_ge(all_placed, 1)
                nc.vector.tensor_scalar(e["slot_src"][:, :], ps_src[:, 0:QP], -1.0, None, ALU.add).then_inc(slots_ready, 1)
                nc.vector.tensor_scalar(e["slot_dst"][:, :], ps_dst[:, 0:QP], float(MID), None, ALU.add)
                ve.wait_ge(slots_turned, 1)
                for g in range(-(-QP // P)):
                    n = min(P, QP - g * P)
                    last = nc.vector.tensor_copy(slot_rows[0:n, g, :], ps_x[0:n, g * P:(g + 1) * P])
                last.then_inc(rows_kept, 1)
                nc.vector.scalar_tensor_tensor(e["slot_node"][:, :], tile_f[:, :], float(P), e["slot_src"][:, :], ALU.mult, ALU.add).then_inc(end, 1)
                ve.wait_ge(end, 1)


class Project:

    def __init__(self, m, chunks, width):
        self.chunks, self.width = chunks, width
        self.turned_ps = [m.ps(f"turned_ps{s}") for s in range(2)]
        self.out_ps = [m.ps(f"out_ps{s}") for s in range(2)]
        self.turned = m.sb("turned", [P, 2, chunks * P])
        self.staged = m.sb("staged", [P, 2, chunks * P])
        self.brought = m.sem("brought")
        self.turn_done, self.copied = m.sem("turn_done"), m.sem("copied")
        self.product, self.used = m.sem("product"), m.sem("used")
        self.tick = m.sem("project_tick")

    def over_tiles(self, eng, step, tiles=NT):
        with eng.Fori(0, tiles // 2) as i:
            for s in range(2):
                step(2 * i + s, s)
        for t in range(tiles // 2 * 2, tiles):
            step(t, t % 2)

    def pool(self, nc, pool, parts):
        def step(t, s):
            pool.wait_ge(self.turn_done, t + 1)
            pool.sem_inc(self.tick, 1)
            for j, part in enumerate(parts(t)):
                last = nc.gpsimd.tensor_copy(self.staged[:, s, j * D:(j + 1) * D], part)
            last.then_inc(self.brought, 1)
        self.over_tiles(pool, step)

    def tensor(self, nc, pe, ident, weight):
        pe.sem_inc(self.product, 2)
        pe.sem_inc(self.turn_done, 2)

        def turn(t, s):
            pe.wait_ge(self.brought, t + 1)
            pe.wait_ge(self.copied, t + 1)
            pe.sem_inc(self.tick, 1)
            for j in range(self.chunks):
                last = nc.tensor.transpose(self.turned_ps[s][:, j * P:(j + 1) * P], self.staged[:, s, j * P:(j + 1) * P], ident)
            last.then_inc(self.turn_done, 1)

        def multiply(t, s):
            pe.wait_ge(self.copied, 2 + t + 1)
            pe.wait_ge(self.used, t + 1)
            pe.sem_inc(self.tick, 1)
            for j in range(self.chunks):
                last = nc.tensor.matmul(self.out_ps[s][:, 0:self.width], self.turned[:, s, j * P:(j + 1) * P], weight(j),
                                        start=(j == 0), stop=(j == self.chunks - 1))
            last.then_inc(self.product, 1)

        def step(t, s):
            turn(t + 1, 1 - s)
            multiply(t, s)
        turn(0, 0)
        self.over_tiles(pe, step, NT - 1)
        multiply(NT - 1, (NT - 1) % 2)

    def scalar(self, nc, act, keep=None):
        act.sem_inc(self.copied, 2)

        def copy(t, s):
            act.wait_ge(self.turn_done, 2 + t + 1)
            act.wait_ge(self.product, t + 1)
            act.sem_inc(self.tick, 1)
            nc.scalar.activation(self.turned[:, s, :], self.turned_ps[s][:, 0:self.chunks * P], ACT.Copy).then_inc(self.copied, 1)

        def store(t, s):
            act.wait_ge(self.product, 2 + t + 1)
            act.sem_inc(self.tick, 1)
            nc.scalar.activation(keep(t), self.out_ps[s][:, 0:self.width], ACT.Copy).then_inc(self.used, 1)

        if keep is None:
            self.over_tiles(act, copy)
            return
        act.sem_inc(self.used, 2)

        def step(t, s):
            copy(t + 1, 1 - s)
            store(t, s)
        copy(0, 0)
        self.over_tiles(act, step, NT - 1)
        store(NT - 1, (NT - 1) % 2)

    def vector(self, ve, use):
        ve.sem_inc(self.used, 2)

        def step(t, s):
            ve.wait_ge(self.product, 2 + t + 1)
            ve.sem_inc(self.tick, 1)
            use(t, self.out_ps[s][:, 0:self.width]).then_inc(self.used, 1)
        self.over_tiles(ve, step)


def first_norm(nc, x_in, x, z_d):
    with Names(nc, "norm0") as m:
        z = m.sb("z", [P, NT, D])
        norm = Norm(m, "ln")
        cleared, loaded, normed, stored = m.sem("cleared"), m.sem("loaded"), m.sem("normed"), m.sem("stored")
        with nc.Block() as block:
            @block.sync
            def _(sp):
                sp.wait_ge(cleared, 1)
                load_nodes(sp, x, x_in, loaded)
                sp.wait_ge(normed, 2)
                sp.dma_start(rows(z_d, 0, NT), z[:, :, :]).then_inc(stored, 16)
                sp.wait_ge(stored, 16)

            @block.vector
            def _(ve):
                nc.vector.memset(x[:, NT - 1, :], 0.0).then_inc(cleared, 1)
                ve.wait_ge(loaded, 32)
                norm.vector(nc, ve, x, z, normed)
                ve.wait_ge(stored, 16)

            @block.scalar
            def _(act):
                norm.scalar(nc, act, x, z, normed)


class Gather:

    def __init__(self, m, width):
        self.rows = m.sb("rows", [P, SLOTS, width])
        self.index = m.sb("index", [P, SLOTS], I32)
        self.index_ready = m.sem("index_ready")
        self.landed = [m.gather_sem(f"landed{p}") for p in range(PAIRS)]
        self.freed = m.sem("freed")
        self.tick = m.sem("gather_tick")

    def pool(self, nc, pool, e, table):
        with pool.Fori(0, Q // SLOTS) as i:
            for h in range(2):
                pool.wait_ge(self.freed, 2 * i + h + 1)
                pool.sem_inc(self.tick, 1)
                nc.gpsimd.tensor_copy(self.index[:, h * HALF:(h + 1) * HALF],
                                      e["slot_dst"][:, bass.ds(SLOTS * i + h * HALF, HALF)]).then_inc(self.index_ready, 1)
                pool.wait_ge(self.index_ready, 2 * i + h + 1)
                pool.sem_inc(self.tick, 1)
                for s in range(h * HALF, (h + 1) * HALF):
                    pool.indirect_dma_start(out=self.rows[:, s, :], out_offset=None, in_=table[:, :],
                                            in_offset=bass.IndirectOffsetOnAxis(ap=self.index[:, s:s + 1], axis=0)).then_inc(self.landed[s // 2], 16)


def tiles_of(nc, engine, e, first):
    return nc.values_load_multi_w_load_instructions(e["tile_i"][0:1, bass.ds(first, HALF)], engines=[engine], min_val=0, max_val=NT - 1)[1]


def aggregate(nc, stage, c, e, table, width, acc, weight=None):
    out_width = HROW if weight is not None else D
    banks = HALF // 2
    turns = Q // SLOTS
    lead = 2
    with Names(nc, stage) as m:
        g = Gather(m, width)
        pick = m.sb("pick", [P, 2, HALF, P])
        scaled = m.sb("scaled", [P, SLOTS, HROW]) if weight is not None else None
        ps = [m.ps(f"ps{i}") for i in range(banks)]
        pick_ready, scaled_ready, summed, added, weighed, tick = (
            m.sem(n) for n in ("pick_ready", "scaled_ready", "summed", "added", "weighed", "tick"))
        with nc.Block() as block:
            @block.gpsimd
            def _(pool):
                g.pool(nc, pool, e, table)

            @block.scalar
            def _(act):
                if weight is None:
                    return
                with act.Fori(0, turns) as i:
                    for h in range(2):
                        act.wait_ge(g.freed, 2 * i + h + 1)
                        act.sem_inc(tick, 1)
                        nc.scalar.activation(scaled[:, h * HALF:(h + 1) * HALF, D:HROW],
                                             weight[:, bass.ds((2 * i + h) * HALF * HEADS, HALF * HEADS)].rearrange("p (s h) -> p s h", h=HEADS),
                                             ACT.Copy).then_inc(weighed, 1)

            @block.tensor
            def _(pe):
                pe.sem_inc(g.freed, 2)
                with pe.Fori(0, turns) as i:
                    for s in range(SLOTS):
                        k, h = SLOTS * i + s, s // HALF
                        if s % HALF == 0:
                            pe.wait_ge(pick_ready, 2 * i + h + 1)
                            if weight is not None:
                                pe.wait_ge(weighed, 2 * i + h + 1)
                        if s % 2 == 0 and weight is None:
                            pe.wait_ge(g.landed[s // 2], 32 * i + 32)
                        elif s % 2 == 0:
                            pe.wait_ge(scaled_ready, PAIRS * i + s // 2 + 1)
                        pe.wait_ge(added, k + 1)
                        pe.sem_inc(tick, 1)
                        rhs = g.rows[:, s, 0:D] if weight is None else scaled[:, s, :]
                        last = nc.tensor.matmul(ps[s % banks][:, 0:out_width], pick[:, h, s % HALF, :], rhs, start=True, stop=True)
                        last.then_inc(summed, 1)
                        if s % HALF == HALF - 1:
                            pe.wait_ge(summed, k + 1)
                            pe.sem_inc(g.freed, 1)

            @block.vector
            def _(ve):
                def choose(half, h):
                    nc.vector.tensor_tensor(pick[:, h, :, :], c["count_f"][:, 0:P].unsqueeze(1).to_broadcast([P, HALF, P]),
                                            e["slot_src"][:, bass.ds(half * HALF, HALF)].unsqueeze(2).to_broadcast([P, HALF, P]),
                                            ALU.is_equal).then_inc(pick_ready, 1)

                def scale(pair, p, turn):
                    if weight is None:
                        return
                    ve.wait_ge(g.landed[p], turn)
                    ve.sem_inc(tick, 1)
                    nc.vector.tensor_tensor(scaled[:, 2 * p:2 * p + 2, 0:D].rearrange("p s (h d) -> p s h d", d=HD),
                                            g.rows[:, 2 * p:2 * p + 2, 0:D].rearrange("p s (h d) -> p s h d", d=HD),
                                            weight[:, bass.ds(pair * 2 * HEADS, 2 * HEADS)].rearrange("p (s h) -> p s h", h=HEADS).unsqueeze(3).to_broadcast([P, 2, HEADS, HD]),
                                            ALU.mult).then_inc(scaled_ready, 1)

                def add(k, s, tile):
                    mine = acc[:, bass.ds(tile * HROW, out_width)]
                    ve.wait_ge(summed, k + 1)
                    ve.wait_ge(added, banks + k)
                    ve.sem_inc(tick, 1)
                    nc.vector.tensor_tensor(mine, mine, ps[s % banks][:, 0:out_width], ALU.add).then_inc(added, 1)

                def half(i, h, last):
                    tiles = tiles_of(nc, nc.vector.engine, e, SLOTS * i + h * HALF)
                    if not (last and h):
                        ve.wait_ge(g.freed, 2 * i + h + 1)
                        ve.sem_inc(tick, 1)
                        choose(2 * i + h + 1, 1 - h)
                    for p in range(h * HALF // 2, (h + 1) * HALF // 2):
                        ahead = p + lead
                        if not (last and ahead >= PAIRS):
                            scale(PAIRS * i + ahead, ahead % PAIRS, 32 * i + 32 * (1 + ahead // PAIRS))
                        for s in (2 * p, 2 * p + 1):
                            add(SLOTS * i + s, s, tiles[s % HALF])

                nc.vector.memset(acc[:, :], 0.0).then_inc(added, 1)
                choose(0, 0)
                for p in range(lead):
                    scale(p, p, 32)
                ve.sem_inc(added, banks - 1)
                with ve.Fori(0, turns - 1) as i:
                    for h in range(2):
                        half(i, h, False)
                for h in range(2):
                    half(turns - 1, h, True)


def mean_layer(nc, c, e, a, x, z_d, acc):
    with Names(nc, "mean") as m:
        z = m.sb("z", [P, NT, D])
        w = m.sb("w", [P, 2 * KD, D])
        bias = m.sb("bias", [P, 2, D])
        per = m.sb("per", [P, NT])
        project = Project(m, 2 * KD, D)
        loaded, z_in, ready, end = m.sem("loaded"), m.sem("z_in"), m.sem("ready"), m.sem("end")
        acc_v = acc[:, :].rearrange("p (t d) -> p t d", d=HROW)
        with nc.Block() as block:
            @block.sync
            def _(sp):
                sp.dma_start(z[:, :, :], rows(z_d, 0, NT)).then_inc(z_in, 16)
                for j, name in enumerate(("L0_gnn_W1", "L0_gnn_W2")):
                    sp.dma_start(w[:, j * KD:(j + 1) * KD, :], a[name].rearrange("(k p) o -> p k o", p=P)).then_inc(loaded, 16)
                for j, name in enumerate(("L0_gnn_b1", "L0_gnn_b2")):
                    sp.dma_start(bias[:, j, :], a[name].partition_broadcast(P)).then_inc(loaded, 16)

            @block.vector
            def _(ve):
                nc.vector.tensor_scalar(per[:, :], e["degree"][:, :], 1.0, None, ALU.max)
                ve.drain()
                nc.vector.reciprocal(per[:, :], per[:, :])
                ve.drain()
                nc.vector.tensor_tensor(acc_v[:, :, 0:D], acc_v[:, :, 0:D], per_tile(per[:, :], D), ALU.mult).then_inc(ready, 1)
                ve.wait_ge(loaded, 64)
                nc.vector.tensor_tensor(bias[:, 0, :], bias[:, 0, :], bias[:, 1, :], ALU.add)
                ve.drain()
                nc.vector.tensor_tensor(x[:, :, :], x[:, :, :], bias[:, 0, :].unsqueeze(1).to_broadcast([P, NT, D]), ALU.add)
                ve.drain()

                def use(t, out):
                    mine = x[:, bass.ds(t, 1), :].rearrange("p t d -> p (t d)")
                    return nc.vector.tensor_tensor(mine, mine, out, ALU.add)
                project.vector(ve, use)
                ve.drain().then_inc(end, 1)

            @block.scalar
            def _(act):
                project.scalar(nc, act)

            @block.tensor
            def _(pe):
                pe.wait_ge(loaded, 64)
                project.tensor(nc, pe, c["ident"][:, :], lambda j: w[:, j, :])

            @block.gpsimd
            def _(pool):
                pool.wait_ge(z_in, 16)
                pool.wait_ge(ready, 1)
                pool.sem_inc(end, 1)
                project.pool(nc, pool, lambda t: (tile_of(z, t), acc[:, bass.ds(t * HROW, D)]))


def route(nc, layer, c, a, x, r, w, gate, gate_bias, z_d, xs_d, again):
    EX, NB, H, tag = layer["experts"], layer["blocks"], layer["hidden"], layer["name"]
    low = f"{tag}_ffn_W" if tag == "L0" else f"{tag}_ffn_w"
    with Names(nc, f"route{tag}") as m:
        z = m.sb("z", [P, NT, D])
        z2 = z
        norm = Norm(m, "ln")
        norm2 = Norm(m, "ln2") if again else None
        leaving = m.sb("leaving", [P, 2, D])
        gate_w = m.sb("gate_w", [P, KD, EX])
        gate_b = m.sb("gate_b", [P, EX])
        logits = m.sb("logits", [P, NT, EX])
        rank = m.sb("rank", [P, EX])
        valid = m.sb("valid", [P, NT])
        best = m.sb("best", [P, TOP, NT])
        first = m.sb("first", [P, NT])
        taken = m.sb("taken", [P, NT, EX])
        hot = m.sb("hot", [P, TOP, NT, EX], BF16)
        before = m.sb("before", [P, TOP, NT, EX], BF16)
        column = m.sb("column", [P, 1 + TOP * NT, EX])
        size_i = m.sb("size_i", [P, EX], I32)
        size_f = m.sb("size_f", [P, EX])
        ends = m.sb("ends", [P, EX])
        base = m.sb("base", [P, EX])
        zeros = m.sb("zeros", [P, TOP * NT])
        owner_f = m.sb("owner_f", [1, NB])
        pos_f = m.sb("pos_f", [P, TOP, NT])
        blank = leaving[:, 0, :]
        index = m.sb("index", [P, 2, TOP], I32)
        project = Project(m, KD, EX)
        before_ps = [m.ps(f"before_ps{k}") for k in range(2)]
        total_ps = [m.ps(f"total_ps{k}") for k in range(2)]
        loaded, normed, normed2, cleared, zeroed = m.sem("loaded"), m.sem("normed"), m.sem("normed2"), m.sem("cleared"), m.sem("zeroed")
        tables, hot_ready, summed, spread, away, pos_ready = m.sem("tables"), m.sem("hot_ready"), m.sem("summed"), m.sem("spread"), m.sem("away"), m.sem("pos_ready")
        index_ready, sent = m.sem("index_ready"), [m.gather_sem(f"sent{s}") for s in range(2)]
        kept, tick = m.sem("kept"), m.sem("tick")
        z_done = 1 if z_d is not None else 0
        with nc.Block() as block:
            @block.sync
            def _(sp):
                sp.dma_start(gate_w[:, :, :], gate.rearrange("(k p) e -> p k e", p=P)).then_inc(loaded, 16)
                sp.dma_start(gate_b[:, :], gate_bias.partition_broadcast(P)).then_inc(loaded, 16)
                sp.wait_ge(cleared, 1)
                with sp.Fori(0, NB) as b:
                    sp.dma_start(xs_d[bass.ds(b * P, P), :], blank).then_inc(zeroed, 16)
                if z_d is not None:
                    sp.wait_ge(normed, 2)
                    sp.dma_start(rows(z_d, 0, NT), z[:, :, :]).then_inc(kept, 16)
                    sp.wait_ge(kept, 16)

            @block.scalar
            def _(act):
                for ex in range(EX):
                    act.dma_start(w["first"][:, ex * KD * H:(ex + 1) * KD * H].rearrange("p (k h) -> p k h", h=H),
                                  a[low + "1"][ex].rearrange("(k p) h -> p k h", p=P)).then_inc(w["landed"], 16)
                    act.dma_start(w["second"][:, ex * H // P * D:(ex + 1) * H // P * D].rearrange("p (k d) -> p k d", d=D),
                                  a[low + "2"][ex].rearrange("(k p) d -> p k d", p=P)).then_inc(w["landed"], 16)
                norm.scalar(nc, act, x, z, normed)
                project.scalar(nc, act)
                if again:
                    norm2.scalar(nc, act, z, z2, normed2)
                act.wait_ge(spread, 1)
                nc.scalar.activation(r["weight"][:, 1, :], first[:, :], ACT.Exp).then_inc(away, 1)

            @block.tensor
            def _(pe):
                pe.wait_ge(loaded, 32)
                project.tensor(nc, pe, c["ident"][:, :], lambda j: gate_w[:, j, :])
                pe.wait_ge(hot_ready, 1)
                for k in range(TOP):
                    chosen = hot[:, k, :, :].rearrange("p t e -> p (t e)")
                    nc.tensor.matmul(before_ps[k][:, 0:NT * EX], c["before_b"][:, :], chosen, start=True, stop=True)
                    last = nc.tensor.matmul(total_ps[k][:, 0:NT * EX], c["ones_b"][:, :], chosen, start=True, stop=True)
                last.then_inc(summed, 1)

            @block.vector
            def _(ve):
                nc.vector.memset(blank, 0.0).then_inc(cleared, 1)
                nc.vector.memset(zeros[:, :], 0.0)
                norm.vector(nc, ve, x, z, normed)
                def use(t, out):
                    return nc.vector.tensor_tensor(logits[:, bass.ds(t, 1), :].rearrange("p t e -> p (t e)"), out, gate_b[:, :], ALU.add)
                project.vector(ve, use)
                if again:
                    norm2.vector(nc, ve, z, z2, normed2)
                ve.wait_ge(tables, 2)
                nc.vector.tensor_scalar(rank[:, :], c["count_f"][:, 0:EX], -1.0, float(EX), ALU.mult, ALU.add)
                ve.drain()
                for k in range(TOP):
                    shape = [P, NT, EX]
                    mine = hot[:, k, :, :]
                    nc.vector.tensor_reduce(best[:, k, :], logits[:, :, :], AX, ALU.max)
                    ve.drain()
                    nc.vector.tensor_tensor(taken[:, :, :], logits[:, :, :], best[:, k, :].unsqueeze(2).to_broadcast(shape), ALU.is_equal)
                    ve.drain()
                    nc.vector.tensor_tensor(taken[:, :, :], taken[:, :, :], rank[:, :].unsqueeze(1).to_broadcast(shape), ALU.mult)
                    ve.drain()
                    nc.vector.tensor_reduce(first[:, :], taken[:, :, :], AX, ALU.max)
                    ve.drain()
                    nc.vector.tensor_tensor(mine, rank[:, :].unsqueeze(1).to_broadcast(shape), first[:, :].unsqueeze(2).to_broadcast(shape), ALU.is_equal)
                    ve.drain()
                    nc.vector.scalar_tensor_tensor(logits[:, :, :], mine, NEG, logits[:, :, :], ALU.mult, ALU.add)
                    ve.drain()
                    nc.vector.tensor_tensor(mine, mine, valid[:, :].unsqueeze(2).to_broadcast(shape), ALU.mult)
                    ve.drain()
                nc.vector.tensor_tensor(first[:, :], best[:, 1, :], best[:, 0, :], ALU.subtract).then_inc(spread, 1)
                nc.vector.memset(column[:, 0, :], 0.0).then_inc(hot_ready, 1)
                ve.wait_ge(away, 1)
                nc.vector.tensor_scalar(first[:, :], r["weight"][:, 1, :], 1.0, None, ALU.add)
                ve.drain()
                nc.vector.reciprocal(r["weight"][:, 0, :], first[:, :])
                ve.drain()
                nc.vector.tensor_tensor(r["weight"][:, 1, :], r["weight"][:, 1, :], r["weight"][:, 0, :], ALU.mult)
                ve.wait_ge(summed, 1)
                for k in range(TOP):
                    nc.vector.tensor_copy(before[:, k, :, :].rearrange("p t e -> p (t e)"), before_ps[k][:, 0:NT * EX])
                    nc.vector.tensor_copy(column[:, 1 + k * NT:1 + (k + 1) * NT, :].rearrange("p t e -> p (t e)"), total_ps[k][:, 0:NT * EX])
                ve.drain()
                with ve.Fori(0, EX) as ex:
                    sl = column[:, 1:, bass.ds(ex, 1)].rearrange("p t e -> p (t e)")
                    nc.vector.tensor_tensor_scan(sl, zeros[:, :], sl, 0.0, ALU.add, ALU.add)
                ve.drain()
                prior = column[:, 0:TOP * NT, :]
                nc.vector.tensor_scalar(size_i[:, :], column[:, TOP * NT, :], float(P - 1), None, ALU.add)
                ve.drain()
                nc.vector.tensor_scalar(size_i[:, :], size_i[:, :], 7, None, ALU.arith_shift_right)
                ve.drain()
                nc.vector.tensor_copy(size_f[:, :], size_i[:, :])
                ve.drain()
                nc.vector.tensor_tensor_scan(ends[:, :], zeros[:, 0:EX], size_f[:, :], 0.0, ALU.add, ALU.add)
                ve.drain()
                nc.vector.tensor_tensor(base[:, :], ends[:, :], size_f[:, :], ALU.subtract)
                nc.vector.memset(owner_f[:, :], 0.0)
                ve.drain()
                for ex in range(EX):
                    nc.vector.scalar_tensor_tensor(owner_f[:, :], c["count_f"][0:1, 0:NB], ends[0:1, ex:ex + 1], owner_f[:, :], ALU.is_ge, ALU.add)
                    ve.drain()
                nc.vector.tensor_scalar(base[:, :], base[:, :], float(P), None, ALU.mult)
                ve.drain()
                nc.vector.tensor_scalar(r["owner"][:, 0:NB], owner_f[:, :], float(EX - 1), None, ALU.min)
                flat = [P, TOP * NT, EX]
                before_v = before[:, :, :, :].rearrange("p k t e -> p (k t) e")
                nc.vector.tensor_tensor(prior, prior, before_v, ALU.add)
                ve.drain()
                nc.vector.tensor_tensor(prior, prior, base[:, :].unsqueeze(1).to_broadcast(flat), ALU.add)
                ve.drain()
                nc.vector.tensor_tensor(prior, prior, hot[:, :, :, :].rearrange("p k t e -> p (k t) e"), ALU.mult)
                ve.drain()
                nc.vector.tensor_reduce(pos_f[:, :, :].rearrange("p k t -> p (k t)"), prior, AX, ALU.add)
                ve.drain()
                nc.vector.tensor_copy(r["pos"][:, :, :], pos_f[:, :, :].rearrange("p k t -> p t k")).then_inc(pos_ready, 1)
                ve.wait_ge(pos_ready, 1)

            @block.gpsimd
            def _(pool):
                nc.gpsimd.memset(valid[:, :], 1.0).then_inc(tables, 1)
                pool.wait_ge(tables, 1)
                nc.gpsimd.affine_select(out=valid[:, :], in_=valid[:, :], compare_op=ALU.is_gt, fill=0.0, base=N,
                                        pattern=[[-P, NT]], channel_multiplier=-1).then_inc(tables, 1)
                pool.wait_ge(normed, 2)
                pool.sem_inc(tick, 1)
                project.pool(nc, pool, lambda t: (tile_of(z, t),))
                pool.wait_ge(zeroed, 16 * NB)
                pool.wait_ge(pos_ready, 1)
                if again:
                    pool.wait_ge(normed2, 2)
                pool.sem_inc(tick, 1)
                with pool.Fori(0, NT // 2) as i:
                    for s in range(2):
                        nc.gpsimd.tensor_copy(index[:, s, :], r["pos"][:, bass.ds(2 * i + s, 1), :].rearrange("p t k -> p (t k)")).then_inc(index_ready, 1)
                        nc.gpsimd.tensor_copy(leaving[:, s, :], z2[:, bass.ds(2 * i + s, 1), :].rearrange("p t d -> p (t d)")).then_inc(index_ready, 1)
                        pool.wait_ge(index_ready, 4 * i + 2 * s + 2)
                        pool.sem_inc(tick, 1)
                        for k in range(TOP):
                            pool.indirect_dma_start(out=xs_d[:, :], out_offset=bass.IndirectOffsetOnAxis(ap=index[:, s, k:k + 1], axis=0),
                                                    in_=leaving[:, s, :], in_offset=None).then_inc(sent[s], 16)
                    for s in range(2):
                        pool.wait_ge(sent[s], 32 * i + 32)
                        pool.sem_inc(tick, 1)
                for k in range(TOP):
                    pool.indirect_dma_start(out=xs_d[:, :], out_offset=bass.IndirectOffsetOnAxis(ap=r["pos"][0:TAIL, NT - 1, k:k + 1], axis=0),
                                            in_=z2[0:TAIL, NT - 1, :], in_offset=None).then_inc(sent[0], 16)
                pool.wait_ge(sent[0], 32 * (NT // 2) + 32)


def experts(nc, layer, c, a, r, w, xs_d, ys_d):
    EX, NB, H, tag = layer["experts"], layer["blocks"], layer["hidden"], layer["name"]
    HC = H // P
    scaled = tag == "L0"
    func = ACT.Gelu if scaled else ACT.Relu
    w1_all, w2_sb, b1, b2 = w["first"], w["second"], a[f"{tag}_ffn_b1"], a[f"{tag}_ffn_b2"]
    with Names(nc, f"experts{tag}") as m:
        w1_sb = m.sb("w1", [P, 2, KD * H])
        b1_sb = m.sb("b1", [P, EX * HC])
        b2_sb = m.sb("b2", [P, EX * D])
        ln = m.sb("ln", [P, 2, EX * KD]) if scaled else None
        xb = m.sb("xb", [P, 2, D])
        xT = m.sb("xT", [P, 2, KD, P])
        hT = m.sb("hT", [P, 2, HC, P])
        yb = m.sb("yb", [P, 2, D])
        banks = HC // 4
        turn_ps = [m.ps(f"turn_ps{s}") for s in range(2)]
        hid_ps = [[m.ps(f"hid_ps{s}{q}") for q in range(banks)] for s in range(2)]
        out_ps = [m.ps(f"out_ps{s}") for s in range(2)]
        w_in = m.sem("w_in")
        w1_ready = m.sem("w1_ready")
        x_in = [m.sem(f"x_in{s}") for s in range(2)]
        y_out = [m.gather_sem(f"y_out{s}") for s in range(2)]
        turned, ready, hidden, acted, product, done = (m.sem(n) for n in ("turned", "ready", "hidden", "acted", "product", "done"))
        tick = m.sem("tick")
        loads = 16 * (2 + (2 if scaled else 0))
        with nc.Block() as block:
            @block.sync
            def _(sp):
                sp.dma_start(b1_sb[:, :], b1.rearrange("p e c -> p (e c)")).then_inc(w_in, 16)
                sp.dma_start(b2_sb[:, :], b2.rearrange("e d -> (e d)").partition_broadcast(P)).then_inc(w_in, 16)
                if scaled:
                    for j, name in enumerate(("L0_ffn_ln_g", "L0_ffn_ln_b")):
                        sp.dma_start(ln[:, j, :], a[name].rearrange("p e k -> p (e k)")).then_inc(w_in, 16)
                sp.sem_inc(turned, 2)

                with sp.Fori(0, NB // 2) as i:
                    for s in range(2):
                        b = 2 * i + s
                        sp.wait_ge(turned, b + 1)
                        sp.dma_start(xb[:, s, :], xs_d[bass.ds(b * P, P), :]).then_inc(x_in[s], 16)

            @block.gpsimd
            def _(pool):
                with pool.Fori(0, NB // 2) as i:
                    for s in range(2):
                        pool.wait_ge(done, 2 + 2 * i + s + 1)
                        pool.sem_inc(tick, 1)
                        pool.dma_start(ys_d[bass.ds((2 * i + s) * P, P), :], yb[:, s, :]).then_inc(y_out[s], 16)
                for s in range(2):
                    pool.wait_ge(y_out[s], 16 * (NB // 2))

            @block.tensor
            def _(pe):
                def turn(b, s, count):
                    pe.wait_ge(x_in[s], 16 * count)
                    pe.wait_ge(ready, b + 1)
                    pe.sem_inc(tick, 1)
                    for k in range(KD):
                        last = nc.tensor.transpose(turn_ps[s][:, k * P:(k + 1) * P], xb[:, s, k * P:(k + 1) * P], c["ident"][:, :])
                    last.then_inc(turned, 1)

                def hide(b, s):
                    pe.wait_ge(w1_ready, b + 1)
                    pe.wait_ge(ready, 2 + b + 1)
                    pe.wait_ge(acted, (b + 1) * banks)
                    pe.sem_inc(tick, 1)
                    for hc in range(HC):
                        for k in range(KD):
                            last = nc.tensor.matmul(hid_ps[s][hc // 4][:, hc % 4 * P:(hc % 4 + 1) * P],
                                                    w1_sb[:, s, k * H + hc * P:k * H + (hc + 1) * P],
                                                    xT[:, s, k, :], start=(k == 0), stop=(k == KD - 1))
                        if hc % 4 == 3:
                            last.then_inc(hidden, 1)

                def finish(b, s):
                    ex = pe.value_load(r["owner"][0:1, bass.ds(b, 1)], min_val=0, max_val=EX - 1)
                    pe.wait_ge(acted, (2 + b + 1) * banks)
                    pe.wait_ge(done, b + 1)
                    pe.sem_inc(tick, 1)
                    for hc in range(HC):
                        last = nc.tensor.matmul(out_ps[s][:, 0:D], hT[:, s, hc, :], w2_sb[:, bass.ds(ex * (HC * D) + hc * D, D)],
                                                start=(hc == 0), stop=(hc == HC - 1))
                    last.then_inc(product, 1)

                pe.sem_inc(product, 2)
                pe.wait_ge(w["landed"], 16 * 2 * EX)
                turn(0, 0, 1)
                turn(1, 1, 1)
                hide(0, 0)
                with pe.Fori(0, (NB - 2) // 2) as i:
                    for s in range(2):
                        b = 2 * i + s + 1
                        turn(b + 1, s, i + 2)
                        hide(b, 1 - s)
                        finish(b - 1, s)
                hide(NB - 1, 1)
                finish(NB - 2, 0)
                finish(NB - 1, 1)

            @block.scalar
            def _(act):
                act.sem_inc(acted, 2 * banks)
                act.wait_ge(w_in, loads)
                with act.Fori(0, NB // 2) as i:
                    for s in range(2):
                        b = 2 * i + s
                        ex = act.value_load(r["owner"][0:1, bass.ds(b, 1)], min_val=0, max_val=EX - 1)
                        act.wait_ge(product, b + 1)
                        act.sem_inc(tick, 1)
                        for q in range(banks):
                            act.wait_ge(hidden, b * banks + q + 1)
                            act.sem_inc(tick, 1)
                            for j in range(4):
                                hc = 4 * q + j
                                last = nc.scalar.activation(hT[:, s, hc, :], hid_ps[s][q][:, j * P:(j + 1) * P], func,
                                                            bias=b1_sb[:, bass.ds(ex * HC + hc, 1)])
                            last.then_inc(acted, 1)

            @block.vector
            def _(ve):
                def scale(b, s, lagging):
                    ve.wait_ge(turned, 2 + b + 1)
                    if lagging:
                        ve.wait_ge(hidden, (b - 1) * banks)
                    ve.sem_inc(tick, 1)
                    ex = ve.value_load(r["owner"][0:1, bass.ds(b, 1)], min_val=0, max_val=EX - 1)
                    nc.vector.tensor_copy(w1_sb[:, s, :], w1_all[:, bass.ds(ex * (KD * H), KD * H)]).then_inc(w1_ready, 1)
                    if not scaled:
                        nc.vector.tensor_copy(xT[:, s, :, :].rearrange("p k t -> p (k t)"), turn_ps[s][:, 0:D]).then_inc(ready, 1)
                        return
                    for k in range(KD):
                        last = nc.vector.tensor_scalar(xT[:, s, k, :], turn_ps[s][:, k * P:(k + 1) * P], ln[:, 0, bass.ds(ex * KD + k, 1)],
                                                       ln[:, 1, bass.ds(ex * KD + k, 1)], ALU.mult, ALU.add)
                    last.then_inc(ready, 1)

                def shift(b, s, count):
                    ex = ve.value_load(r["owner"][0:1, bass.ds(b, 1)], min_val=0, max_val=EX - 1)
                    ve.wait_ge(product, 2 + b + 1)
                    if count is not None:
                        ve.wait_ge(y_out[s], 16 * count)
                    ve.sem_inc(tick, 1)
                    nc.vector.tensor_tensor(yb[:, s, :], out_ps[s][:, 0:D], b2_sb[:, bass.ds(ex * D, D)], ALU.add).then_inc(done, 1)

                ve.sem_inc(ready, 2)
                ve.sem_inc(done, 2)
                ve.wait_ge(w_in, loads)
                ve.wait_ge(w["landed"], 16 * 2 * EX)
                scale(0, 0, False)
                scale(1, 1, False)
                scale(2, 0, True)
                shift(0, 0, None)
                scale(3, 1, True)
                shift(1, 1, None)
                with ve.Fori(1, NB // 2 - 1) as i:
                    for s in range(2):
                        scale(2 * i + s + 2, s, True)
                        shift(2 * i + s, s, i)
                for s in range(2):
                    shift(NB - 2 + s, s, NB // 2 - 1)


def combine(nc, layer, r, ys_d, target, after):
    tag = layer["name"]
    with Names(nc, f"combine{tag}") as m:
        ys = m.sb("ys", [P, 2, TOP, D])
        index = m.sb("index", [P, 2, TOP], I32)
        index_ready, used, end, tick = m.sem("index_ready"), m.sem("used"), m.sem("end"), m.sem("tick")
        landed = [m.gather_sem(f"landed{s}") for s in range(2)]
        extra = after(m) if after else None
        with nc.Block() as block:
            @block.gpsimd
            def _(pool):
                with pool.Fori(0, NT // 2) as i:
                    for s in range(2):
                        pool.wait_ge(used, 2 * i + s + 1)
                        pool.sem_inc(tick, 1)
                        nc.gpsimd.tensor_copy(index[:, s, :], r["pos"][:, bass.ds(2 * i + s, 1), :].rearrange("p t k -> p (t k)")).then_inc(index_ready, 1)
                        pool.wait_ge(index_ready, 2 * i + s + 1)
                        pool.sem_inc(tick, 1)
                        for k in range(TOP):
                            pool.indirect_dma_start(out=ys[:, s, k, :], out_offset=None, in_=ys_d[:, :],
                                                    in_offset=bass.IndirectOffsetOnAxis(ap=index[:, s, k:k + 1], axis=0)).then_inc(landed[s], 16)
                pool.wait_ge(used, NT)
                for k in range(TOP):
                    pool.indirect_dma_start(out=ys[0:TAIL, 0, k, :], out_offset=None, in_=ys_d[:, :],
                                            in_offset=bass.IndirectOffsetOnAxis(ap=r["pos"][0:TAIL, NT - 1, k:k + 1], axis=0)).then_inc(landed[0], 16)

            @block.vector
            def _(ve):
                if extra:
                    extra.before(ve)
                def add(t, s, n, turn):
                    ve.wait_ge(landed[s], turn)
                    ve.sem_inc(tick, 1)
                    mine = target[0:n, bass.ds(t, 1), :].rearrange("p t d -> p (t d)")
                    for k in range(TOP):
                        last = nc.vector.scalar_tensor_tensor(mine, ys[0:n, s, k, :], r["weight"][0:n, k, bass.ds(t, 1)], mine, ALU.mult, ALU.add)
                        if k < TOP - 1:
                            ve.drain()
                    last.then_inc(used, 1)
                ve.sem_inc(used, 2)
                with ve.Fori(0, NT // 2) as i:
                    for s in range(2):
                        add(2 * i + s, s, P, 32 * i + 32)
                add(NT - 1, 0, TAIL, 32 * (NT // 2) + 32)
                ve.drain()
                if extra:
                    extra.vector(ve)
                ve.drain().then_inc(end, 1)

            if extra:
                extra.rest(block)


class Finish:

    def __init__(self, nc, m, a, x, z, z_d, out):
        self.nc, self.a, self.x, self.z, self.z_d, self.out = nc, a, x, z, z_d, out
        self.affine = m.sb("affine", [P, 2, D])
        self.norm = Norm(m, "ln")
        self.loaded, self.normed, self.total, self.stored = m.sem("loaded"), m.sem("normed"), m.sem("total"), m.sem("stored")

    def before(self, ve):
        ve.wait_ge(self.loaded, 48)

    def vector(self, ve):
        nc, x, z = self.nc, self.x, self.z
        self.norm.vector(nc, ve, z, z, self.normed)
        ve.wait_ge(self.normed, 2)
        shape = [P, NT, D]
        nc.vector.tensor_tensor(z[:, :, :], z[:, :, :], self.affine[:, 0, :].unsqueeze(1).to_broadcast(shape), ALU.mult)
        nc.vector.tensor_tensor(x[:, :, :], x[:, :, :], self.affine[:, 1, :].unsqueeze(1).to_broadcast(shape), ALU.add)
        ve.drain()
        nc.vector.tensor_tensor(x[:, :, :], x[:, :, :], z[:, :, :], ALU.add).then_inc(self.total, 1)

    def rest(self, block):
        nc, a, x, z = self.nc, self.a, self.x, self.z

        @block.scalar
        def _(act):
            self.norm.scalar(nc, act, z, z, self.normed)

        @block.sync
        def _(sp):
            sp.dma_start(z[:, :, :], rows(self.z_d, 0, NT)).then_inc(self.loaded, 16)
            for j, name in enumerate(("L1_ffn_gamma", "L1_ffn_beta")):
                sp.dma_start(self.affine[:, j, :], a[name].partition_broadcast(P)).then_inc(self.loaded, 16)
            sp.wait_ge(self.total, 1)
            sp.dma_start(rows(self.out, 0, NT - 1), x[:, 0:NT - 1, :]).then_inc(self.stored, 16)
            sp.dma_start(self.out[(NT - 1) * P:N, :], x[0:TAIL, NT - 1, :]).then_inc(self.stored, 16)
            sp.wait_ge(self.stored, 32)


def heads(nc, c, a, x, split, h_d, coef):
    G = 5
    with Names(nc, "heads") as m:
        z = m.sb("z", [P, NT, D])
        norm = Norm(m, "ln")
        w = m.sb("w", [P, KD, D])
        att = m.sb("att", [P, HEADS, 5, HD])
        ends = m.sb("ends", [P, 3, D])
        line = m.sb("line", [1, 2, KD, HEADS, HPART])
        row = m.sb("row", [P, NT, HROW])
        rest = m.sb("rest", [P, 2, G, D])
        work = m.sb("work", [P, 3, G, D])
        term = m.sb("term", [P, 3, NT, HEADS])
        coef_ps = m.ps("coef_ps")
        project = Project(m, KD, D)
        line_ready, turned = m.sem("line_ready"), m.sem("turned")
        loaded, normed, tick, rounded, left, row_ready, stored = (
            m.sem(n) for n in ("loaded", "normed", "tick", "rounded", "left", "row_ready", "stored"))
        groups = [slice(g, g + G) for g in range(0, NT, G)]

        def by_head(ap):
            return ap.rearrange("p (h d) -> p h d", d=HD)

        with nc.Block() as block:
            @block.sync
            def _(sp):
                sp.dma_start(w[:, :, :], a["L1_gnn_W"].rearrange("(k p) o -> p k o", p=P)).then_inc(loaded, 16)
                sp.dma_start(att[:, :, :, :].rearrange("p h f d -> p (h f d)"), a["L1_gnn_a"].rearrange("h f -> (h f)").partition_broadcast(P)).then_inc(loaded, 16)
                for n, tiles in enumerate(groups):
                    sp.wait_ge(row_ready, n + 1)
                    sp.dma_start(rows(h_d, tiles.start, tiles.stop), row[:, tiles, :]).then_inc(stored, 16)
                sp.wait_ge(stored, 16 * len(groups))

            @block.scalar
            def _(act):
                norm.scalar(nc, act, x, z, normed)
                project.scalar(nc, act, lambda t: row[:, bass.ds(t, 1), 0:D].rearrange("p t d -> p (t d)"))
                for n, tiles in enumerate(groups):
                    act.wait_ge(project.used, 2 + tiles.stop)
                    nc.scalar.activation(split[:, tiles, 0, 0:D], row[:, tiles, 0:D], ACT.Copy).then_inc(rounded, 1)
                    for part in range(2):
                        act.wait_ge(left, 2 * n + part + 1)
                        nc.scalar.activation(split[:, tiles, 1 + part, 0:D], rest[:, part, :, :], ACT.Copy).then_inc(rounded, 1)

            @block.tensor
            def _(pe):
                pe.wait_ge(loaded, 32)
                pe.wait_ge(line_ready, 1)
                flat = line[:, :, :, :, :].rearrange("p j f h d -> p (j f h d)")
                for j in range(2 * KD):
                    last = nc.tensor.transpose(coef_ps[:, j:j + 1], flat[:, j * P:(j + 1) * P], c["ident"][0:1, 0:1])
                last.then_inc(turned, 1)
                project.tensor(nc, pe, c["ident"][:, :], lambda j: w[:, j, :])

            @block.gpsimd
            def _(pool):
                pool.wait_ge(normed, 2)
                pool.sem_inc(tick, 1)
                project.pool(nc, pool, lambda t: (tile_of(z, t),))

            @block.vector
            def _(ve):
                norm.vector(nc, ve, x, z, normed)
                ve.wait_ge(loaded, 32)
                nc.vector.tensor_tensor(by_head(ends[:, 0, :]), att[:, :, 0, :], att[:, :, 2, :], ALU.subtract)
                nc.vector.tensor_tensor(by_head(ends[:, 1, :]), att[:, :, 1, :], att[:, :, 2, :], ALU.add)
                nc.vector.tensor_scalar(by_head(ends[:, 2, :]), att[:, :, 4, :], 0.5, None, ALU.mult)
                for j, scale in enumerate((1.0, -0.5)):
                    for f in range(KD):
                        last = nc.vector.tensor_scalar(line[:, j, f, :, :], att[0:1, :, 3 + j, f:HD:KD], scale, None, ALU.mult)
                last.then_inc(line_ready, 1)
                ve.wait_ge(turned, 1)
                nc.vector.tensor_copy(coef[:, :, :].rearrange("p j f -> p (j f)"), coef_ps[:, 0:2 * KD])
                ve.drain()
                shape = [P, G, D]

                def wide(j):
                    return ends[:, j, :].unsqueeze(1).to_broadcast(shape)

                for n, tiles in enumerate(groups):
                    mine = row[:, tiles, 0:D]
                    ve.wait_ge(project.used, 2 + tiles.stop)
                    nc.vector.tensor_tensor(work[:, 0, :, :], mine, wide(2), ALU.mult)
                    ve.wait_ge(rounded, 3 * n + 1)
                    nc.vector.tensor_tensor(rest[:, 0, :, :], mine, split[:, tiles, 0, 0:D], ALU.subtract).then_inc(left, 1)
                    ve.drain()
                    for j in range(2):
                        nc.vector.tensor_tensor(work[:, 1 + j, :, :], work[:, 0, :, :], wide(j), ALU.add)
                    ve.wait_ge(rounded, 3 * n + 2)
                    nc.vector.tensor_tensor(rest[:, 1, :, :], rest[:, 0, :, :], split[:, tiles, 1, 0:D], ALU.subtract).then_inc(left, 1)
                    ve.drain()
                    for j in range(2):
                        nc.vector.tensor_tensor(work[:, 1 + j, :, :], work[:, 1 + j, :, :], mine, ALU.mult)
                    ve.drain()
                    nc.vector.tensor_reduce(term[:, 0, tiles, :], work[:, 1, :, :].rearrange("p t (h d) -> p t h d", d=HD), AX, ALU.add)
                    nc.vector.tensor_reduce(row[:, tiles, D:HROW], work[:, 2, :, :].rearrange("p t (h d) -> p t h d", d=HD), AX, ALU.add).then_inc(row_ready, 1)
                    ve.wait_ge(rounded, 3 * n + 3)
                ve.drain()
                nc.vector.tensor_scalar(term[:, 0, :, :], term[:, 0, :, :], -1.0, None, ALU.mult)
                ve.drain()
                for part in range(3):
                    nc.vector.tensor_copy(split[:, :, part, D:HROW], term[:, part, :, :])
                    ve.drain()
                    if part < 2:
                        nc.vector.tensor_tensor(term[:, part + 1, :, :], term[:, part, :, :], split[:, :, part, D:HROW], ALU.subtract)
                        ve.drain()


def scores(nc, c, e, split, h_d, slot_d, coef, score):
    turns = Q // SLOTS
    HP = HALF // 2
    PARTS = 3
    W = PARTS * HEADS
    JOINED = (0, 2, 3, 4)
    with Names(nc, "scores") as m:
        g = Gather(m, HROW)
        lanes = m.sb("lanes", [P, 2, HALF * P], FP16)
        minus = m.sb("minus", [P, 2, HALF * P], BF16)
        node = m.sb("node", [P, PAIRS, 2, PARTS, HROW], BF16)
        size = m.sb("size", [P, HP, 2, KD, P])
        slope = m.sb("slope", [P, HP, 2, KD, P])
        joint = m.sb("joint", [P, HP, 2, P])
        total = m.sb("total", [P, HALF, HEADS])
        diff_ps = [m.ps(f"diff_ps{s}") for s in range(HP)]
        sum_ps = [m.ps(f"sum_ps{s}") for s in range(2)]
        lanes_in = [m.sem(f"lanes_in{s}") for s in range(2)]
        minus_ready, staged, diffed, absed, sized, joined, multiplied, reduced, half_done, summed, tick = (
            m.sem(n) for n in ("minus_ready", "staged", "diffed", "absed", "sized", "joined", "multiplied", "reduced", "half_done", "summed", "tick"))

        def chunk(row, f):
            return row[:, f:D:KD]

        with nc.Block() as block:
            @block.sync
            def _(sp):
                with sp.Fori(0, turns) as i:
                    for f in range(2):
                        sp.wait_ge(minus_ready, 2 * i + f + 1)
                        sp.dma_start(lanes[:, f, :], slot_d[bass.ds((2 * i + f) * HALF, HALF), :].rearrange("c e -> (c e)").partition_broadcast(P)).then_inc(lanes_in[f], 16)

            @block.gpsimd
            def _(pool):
                g.pool(nc, pool, e, h_d)

            @block.tensor
            def _(pe):
                def differ(i, p):
                    if p % HP == 0:
                        pe.wait_ge(minus_ready, 2 + 2 * i + p // HP + 1)
                    pe.wait_ge(g.landed[p], 32 * i + 32)
                    pe.wait_ge(staged, PAIRS * i + p + 1)
                    pe.wait_ge(absed, PAIRS * i + p + 1)
                    pe.sem_inc(tick, 1)
                    for j in range(2):
                        s = 2 * p + j
                        for f in range(KD):
                            out = diff_ps[p % HP][:, (KD * j + f) * P:(KD * j + f + 1) * P]
                            nc.tensor.matmul(out, chunk(g.rows[:, s, :], f), c["ident"][:, :], start=True, stop=False)
                            for part in range(PARTS):
                                last = nc.tensor.matmul(out, chunk(node[:, p, j, part, :], f), minus[:, s // HALF, s % HALF * P:(s % HALF + 1) * P],
                                                        start=False, stop=(part == PARTS - 1))
                    last.then_inc(diffed, 1)

                def reduce(i, p):
                    if p % HP == 0:
                        pe.wait_ge(g.freed, 2 * i + p // HP + 1)
                    pe.wait_ge(joined, HP + PAIRS * i + p + 1)
                    pe.sem_inc(tick, 1)
                    for j in range(2):
                        s, half = 2 * p + j, p // HP
                        out = sum_ps[half][:, s % HALF * W:(s % HALF + 1) * W]
                        nc.tensor.matmul(out, minus[:, half, s % HALF * P:(s % HALF + 1) * P], node[:, p, j, :, D:HROW], start=True, stop=False)
                        parts = [joint[:, p % HP, j, :]] if p % HP in JOINED else [size[:, p % HP, j, f, :] for f in range(KD)]
                        for n, part in enumerate(parts):
                            last = nc.tensor.matmul(out, part, c["by_head"][:, :], start=False, stop=(n == len(parts) - 1))
                    last.then_inc(reduced, 1)

                lead = 3
                pe.sem_inc(reduced, PAIRS)
                for p in range(lead):
                    differ(0, p)
                with pe.Fori(0, turns - 1) as i:
                    for p in range(PAIRS):
                        differ(*((i, p + lead) if p + lead < PAIRS else (i + 1, p + lead - PAIRS)))
                        reduce(i, p)
                for p in range(PAIRS):
                    if p + lead < PAIRS:
                        differ(turns - 1, p + lead)
                    reduce(turns - 1, p)

            @block.scalar
            def _(act):
                act.sem_inc(absed, HP)
                with act.Fori(0, turns) as i:
                    for p in range(PAIRS):
                        act.wait_ge(diffed, PAIRS * i + p + 1)
                        act.wait_ge(joined, PAIRS * i + p + 1)
                        if p % HP not in JOINED:
                            act.wait_ge(reduced, PAIRS - HP + PAIRS * i + p + 1)
                        act.sem_inc(tick, 1)
                        nc.scalar.activation(size[:, p % HP, :, :, :].rearrange("p j f e -> p (j f e)"), diff_ps[p % HP][:, :], ACT.Abs).then_inc(absed, 1)
                        act.wait_ge(absed, HP + PAIRS * i + p + 1)
                        act.sem_inc(tick, 1)
                        for f in range(KD):
                            last = nc.scalar.activation(slope[:, p % HP, :, f, :], size[:, p % HP, :, f, :], ACT.Identity,
                                                        bias=coef[:, 0, f:f + 1], scale=coef[:, 1, f:f + 1])
                        last.then_inc(sized, 1)

            @block.vector
            def _(ve):
                def keep(half, f):
                    ve.wait_ge(reduced, PAIRS + half * HP + HP)
                    ve.sem_inc(tick, 1)
                    nc.vector.tensor_reduce(total[:, :, :], sum_ps[f][:, 0:HALF * W].rearrange("p (s k h) -> p s h k", h=HEADS, k=PARTS), AX, ALU.add).then_inc(summed, 1)
                    ve.wait_ge(summed, half + 1)
                    ve.sem_inc(tick, 1)
                    nc.vector.tensor_tensor(score[:, bass.ds(half * (HALF * HEADS), HALF * HEADS)].rearrange("p (s h) -> p s h", h=HEADS),
                                            total[:, :, :], g.rows[:, f * HALF:(f + 1) * HALF, D:HROW], ALU.add).then_inc(g.freed, 1)

                def choose(i, f):
                    ve.wait_ge(lanes_in[f], 16 * i + 16)
                    ve.wait_ge(g.freed, 2 * i + f + 1)
                    ve.sem_inc(tick, 1)
                    nc.vector.tensor_scalar(minus[:, f, :], lanes[:, f, :], c["lane_f"][:, 0:1], -1.0, ALU.is_equal, ALU.mult).then_inc(minus_ready, 1)

                def stage(i, p, tiles):
                    ve.wait_ge(reduced, PAIRS * i + p + 1)
                    ve.sem_inc(tick, 1)
                    for j in range(2):
                        last = nc.vector.tensor_copy(node[:, p, j, :, :].rearrange("p k d -> p (k d)"),
                                                     split[:, bass.ds(tiles[2 * (p % HP) + j], 1), :, :].rearrange("p t k d -> p (t k d)"))
                    last.then_inc(staged, 1)

                def multiply(i, p):
                    ve.wait_ge(sized, PAIRS * i + p + 1)
                    ve.sem_inc(tick, 1)
                    mine = size[:, p % HP, :, :, :]
                    nc.vector.tensor_tensor(mine, mine, slope[:, p % HP, :, :, :], ALU.mult).then_inc(multiplied if p % HP in JOINED else joined, 1)

                def join(i, p):
                    ve.wait_ge(multiplied, len(JOINED) * (2 * i + p // HP) + JOINED.index(p % HP) + 1)
                    ve.wait_ge(reduced, PAIRS - HP + PAIRS * i + p + 1)
                    ve.sem_inc(tick, 1)
                    nc.vector.tensor_tensor(joint[:, p % HP, :, :], size[:, p % HP, :, 0, :], size[:, p % HP, :, 1, :], ALU.add).then_inc(joined, 1)

                def half(i, f, first=False, last=False):
                    more = not (last and f)
                    nxt, other = i + f, 1 - f
                    ahead = {1: (0,), 2: (1, 2), 3: (3,), 4: (4,)}
                    for p in range(HP):
                        multiply(i, f * HP + p)
                        if p == 1:
                            if not (first and f == 0):
                                keep(2 * i + f - 1, other)
                            if more:
                                choose(nxt, other)
                                tiles = tiles_of(nc, nc.vector.engine, e, SLOTS * i + (f + 1) * HALF)
                        if more:
                            for q in ahead.get(p, ()):
                                stage(nxt, other * HP + q, tiles)
                        if p in JOINED:
                            join(i, f * HP + p)

                nc.vector.memset(score[:, Q * HEADS:], 0.0)
                ve.sem_inc(g.freed, 2)
                ve.sem_inc(minus_ready, 2)
                ve.sem_inc(joined, HP)
                tiles = tiles_of(nc, nc.vector.engine, e, 0)
                choose(0, 0)
                for p in range(HP):
                    stage(0, p, tiles)
                for f in range(2):
                    half(0, f, first=True)
                with ve.Fori(1, turns - 1) as i:
                    for f in range(2):
                        half(i, f)
                for f in range(2):
                    half(turns - 1, f, last=True)
                keep(2 * turns - 1, 1)
                ve.drain().then_inc(tick, 1)


def edge_softmax(nc, c, e, score):
    W = QP * HEADS
    BLK = W // P
    with Names(nc, "softmax") as m:
        slope = m.sb("slope", [P, W])
        node_h = m.sb("node_h", [P, W])
        turned = m.sb("turned", [P, W])
        change = m.sb("change", [P, W + 1])
        forth = m.sb("forth", [P, W])
        back = m.sb("back", [P, W])
        picks = m.sb("picks", [P, 2, P])
        ends = m.sb("ends", [P, 2, QP])
        joins = m.sb("joins", [P, QP + 1])
        whole = m.sb("whole", [P, QP])
        step = m.sb("step", [P, 2, QP])
        apart = m.sb("apart", [P, 2, QP])
        ps = [m.ps(f"ps{s}") for s in range(2)]
        lin, named, moved, emptied, scanned, topped, bounded, exped, end = (
            m.sem(n) for n in ("lin", "named", "moved", "emptied", "scanned", "topped", "bounded", "exped", "end"))
        back1, seen = m.sem("back1"), m.sem("seen")
        G = BLK // 4
        with nc.Block() as block:
            @block.tensor
            def _(pe):
                n = 0

                def four(source, g):
                    nonlocal n
                    pe.wait_ge(emptied, n + 1)
                    for j in range(4):
                        b = 4 * g + j
                        last = nc.tensor.transpose(ps[n % 2][:, j * P:(j + 1) * P], source[:, b * P:(b + 1) * P], c["ident"][:, :])
                    last.then_inc(moved, 1)
                    n += 1
                pe.wait_ge(lin, 1)
                for g in range(G):
                    four(score, g)
                pe.wait_ge(named, 1)
                for g in range(G):
                    four(node_h, g)
                pe.wait_ge(scanned, 1)
                for g in range(G):
                    four(forth, g)
                pe.wait_ge(topped, 1)
                for j in range(2):
                    for g in range(G):
                        pe.wait_ge(emptied, n + 1)
                        nc.tensor.matmul(ps[n % 2][:, :], picks[:, j, :], back[:, g * 512:(g + 1) * 512], start=True, stop=True).then_inc(moved, 1)
                        n += 1
                for j in range(2):
                    pe.wait_ge(emptied, n + 1)
                    nc.tensor.matmul(ps[n % 2][:, 0:QP], picks[:, j, :], e["slot_node"][:, :], start=True, stop=True).then_inc(moved, 1)
                    n += 1

            @block.scalar
            def _(act):
                act.wait_ge(bounded, 1)
                nc.scalar.activation(score[:, :], score[:, :], ACT.Exp).then_inc(exped, 1)

            @block.vector
            def _(ve):
                n = 0

                def empty(out):
                    nonlocal n
                    ve.wait_ge(moved, n + 1)
                    nc.vector.tensor_copy(out, ps[n % 2][:, 0:out.shape[1]]).then_inc(emptied, 1)
                    n += 1
                ve.sem_inc(emptied, 2)
                nc.vector.tensor_scalar(slope[:, :], score[:, :], SLOPE, None, ALU.mult)
                ve.drain()
                nc.vector.tensor_tensor(score[:, :], score[:, :], slope[:, :], ALU.max).then_inc(lin, 1)
                nc.vector.tensor_copy(node_h[:, :].rearrange("p (q h) -> p q h", h=HEADS), e["slot_node"][:, :].unsqueeze(2).to_broadcast([P, QP, HEADS])).then_inc(named, 1)
                for j, lane in enumerate((0, P - 1)):
                    nc.vector.tensor_copy(picks[:, j, :], c["ident"][:, lane:lane + 1].to_broadcast([P, P]))
                for g in range(G):
                    empty(turned[:, g * 512:(g + 1) * 512])
                for g in range(G):
                    empty(forth[:, g * 512:(g + 1) * 512])
                ve.drain()
                nc.vector.tensor_tensor(change[:, 1:W], forth[:, 1:W], forth[:, 0:W - 1], ALU.not_equal)
                ve.drain()
                nc.vector.tensor_scalar(change[:, 1:W], change[:, 1:W], NEG, None, ALU.mult)
                ve.drain()
                nc.vector.memset(change[:, 0:W + 1:P], NEG)
                ve.drain()
                nc.vector.tensor_tensor_scan(forth[:, :], change[:, 0:W], turned[:, :], NEG, ALU.add, ALU.max)
                nc.vector.tensor_tensor_scan(back[:, ::-1], change[:, W:0:-1], turned[:, ::-1], NEG, ALU.add, ALU.max)
                ve.drain()
                nc.vector.tensor_tensor(forth[:, :], forth[:, :], back[:, :], ALU.max).then_inc(scanned, 1)
                for g in range(G):
                    empty(back[:, g * 512:(g + 1) * 512])
                ve.drain().then_inc(topped, 1)
                top = back
                for g in range(G):
                    empty(turned[:, g * 512:(g + 1) * 512])
                for g in range(G):
                    empty(slope[:, g * 512:(g + 1) * 512])
                for j in range(2):
                    empty(ends[:, j, :])
                ve.drain()
                nc.vector.memset(joins[:, :], NEG)
                ve.drain()
                nc.vector.tensor_tensor(joins[:, 1:QP], ends[:, 0, 1:QP], ends[:, 1, 0:QP - 1], ALU.not_equal)
                nc.vector.tensor_tensor(whole[:, :], ends[:, 0, :], ends[:, 1, :], ALU.not_equal)
                for j in range(2):
                    nc.vector.tensor_tensor(apart[:, j, :], e["slot_node"][:, :], ends[:, j, :], ALU.not_equal)
                ve.drain()
                nc.vector.tensor_scalar(joins[:, 1:QP], joins[:, 1:QP], NEG, None, ALU.mult)
                nc.vector.tensor_scalar(whole[:, :], whole[:, :], NEG, None, ALU.mult)
                nc.vector.tensor_scalar(apart[:, :, :], apart[:, :, :], NEG, None, ALU.mult)
                ve.drain()
                nc.vector.tensor_tensor(step[:, 0, :], joins[:, 0:QP], whole[:, :], ALU.min)
                nc.vector.tensor_tensor(step[:, 1, :], joins[:, 1:QP + 1], whole[:, :], ALU.min)
                ve.drain()
                first_v = turned[:, :].rearrange("p (q h) -> p q h", h=HEADS)
                last_v = slope[:, :].rearrange("p (q h) -> p q h", h=HEADS)
                for hd in range(HEADS):
                    nc.vector.tensor_tensor_scan(last_v[:, :, hd], step[:, 0, :], last_v[:, :, hd], NEG, ALU.add, ALU.max)
                    nc.vector.tensor_tensor_scan(first_v[:, ::-1, hd], step[:, 1, ::-1], first_v[:, ::-1, hd], NEG, ALU.add, ALU.max)
                ve.drain()
                wide = [P, QP, HEADS]
                carry = node_h[:, :].rearrange("p (q h) -> p q h", h=HEADS)
                top_v = top[:, :].rearrange("p (q h) -> p q h", h=HEADS)
                nc.vector.memset(carry[:, 0, :], NEG)
                nc.vector.tensor_tensor(carry[:, 1:QP, :], last_v[:, 0:QP - 1, :], joins[:, 1:QP].unsqueeze(2).to_broadcast([P, QP - 1, HEADS]), ALU.add)
                ve.drain()
                nc.vector.tensor_tensor(carry, carry, apart[:, 0, :].unsqueeze(2).to_broadcast(wide), ALU.add)
                ve.drain()
                nc.vector.tensor_tensor(top_v, top_v, carry, ALU.max)
                ve.drain()
                nc.vector.memset(carry[:, QP - 1, :], NEG)
                nc.vector.tensor_tensor(carry[:, 0:QP - 1, :], first_v[:, 1:QP, :], joins[:, 1:QP].unsqueeze(2).to_broadcast([P, QP - 1, HEADS]), ALU.add)
                ve.drain()
                nc.vector.tensor_tensor(carry, carry, apart[:, 1, :].unsqueeze(2).to_broadcast(wide), ALU.add)
                ve.drain()
                nc.vector.tensor_tensor(top_v, top_v, carry, ALU.max)
                ve.drain()
                nc.vector.tensor_tensor(score[:, :], score[:, :], top[:, :], ALU.subtract).then_inc(bounded, 1)
                ve.wait_ge(exped, 1)


def attend(nc, x, acc):
    with Names(nc, "attend") as m:
        per = m.sb("per", [P, NT, HEADS])
        end = m.sem("end")
        acc_v = acc[:, :].rearrange("p (t d) -> p t d", d=HROW)
        with nc.Block() as block:
            @block.vector
            def _(ve):
                nc.vector.tensor_scalar(per[:, :, :], acc_v[:, :, D:HROW], 1e-16, None, ALU.add)
                ve.drain()
                nc.vector.reciprocal(per[:, :, :], per[:, :, :])
                ve.drain()
                for hd in range(HEADS):
                    mine = acc_v[:, :, hd * HD:(hd + 1) * HD]
                    nc.vector.tensor_tensor(mine, mine, per[:, :, hd].unsqueeze(2).to_broadcast([P, NT, HD]), ALU.mult)
                ve.drain()
                nc.vector.tensor_tensor(x[:, :, :], x[:, :, :], acc_v[:, :, 0:D], ALU.add).then_inc(end, 1)
                ve.wait_ge(end, 1)


def feed_forward(nc, layer, c, a, x, dram, out):
    tag, EX, H, NB = layer["name"], layer["experts"], layer["hidden"], layer["blocks"]
    with Names(nc, f"ffn{tag}") as m:
        r = dict(weight=m.sb("weight", [P, TOP, NT]), pos=m.sb("pos", [P, NT, TOP], I32), owner=m.sb("owner", [1, NB], I32))
        xs_d, ys_d = dram(f"xs_{tag}", [NB * P, D]), dram(f"ys_{tag}", [NB * P, D])
        first = tag == "L0"
        z_d = None if first else dram(f"z_{tag}", [NR, D])
        gate, bias = (a["L0_ffn_Wr"], a["L0_ffn_br"]) if first else (a["L1_ffn_gate_w"], a["L1_ffn_gate_b"])
        with Names(nc, f"weights{tag}") as k:
            w = dict(first=k.sb("w1", [P, EX * KD * H]), second=k.sb("w2", [P, EX * H // P * D]), landed=k.sem("landed"))
            route(nc, layer, c, a, x, r, w, gate, bias, z_d, xs_d, first)
            experts(nc, layer, c, a, r, w, xs_d, ys_d)
        if first:
            combine(nc, layer, r, ys_d, x, None)
        else:
            with Names(nc, "last") as k:
                z = k.sb("z", [P, NT, D])
                combine(nc, layer, r, ys_d, z, lambda mm: Finish(nc, mm, a, x, z, z_d, out))


def build(nc, a, out):
    with Names.whole, Names(nc, "all") as keep:
        def dram(name, shape, dt=F32):
            return nc.dram_tensor(name, shape, dt, kind="Internal").ap()

        sb = keep.sb
        c = dict(ident=sb("ident", [P, P]), before=sb("before", [P, P]), ones=sb("ones", [P, P]), before_b=sb("before_b", [P, P], BF16), ones_b=sb("ones_b", [P, P], BF16),
                 count_f=sb("count_f", [P, P]), lane_f=sb("lane_f", [P, 1]), by_head=sb("by_head", [P, 3 * HEADS]))
        e = dict(degree=sb("degree", [P, NT]), tile_i=sb("tile_i", [1, QP], I32),
                 slot_dst=sb("slot_dst", [P, QP], I32), slot_src=sb("slot_src", [P, QP]), slot_node=sb("slot_node", [P, QP]))
        x = sb("x", [P, NT, D])
        slot_d = dram("slot_lanes", [QP, P], FP16)
        with Names(nc, "gnn0") as m:
            c.update(upto=m.sb("upto", [P, P]), count_h=m.sb("count_h", [P, QP], FP16), count_b=m.sb("count_b", [P, P], BF16))
            constants(nc, c)
            z_d = dram("z_gnn0", [NR, D])
            first_norm(nc, a["x"], x, z_d)
            sort_edges(nc, c, e, a["src"], a["dst"], dram("low_lanes", [EC, P], BF16), slot_d)
            acc = m.sb("acc", [P, NT * HROW])
            aggregate(nc, "sum0", c, e, z_d, D, acc)
            mean_layer(nc, c, e, a, x, z_d, acc)
        feed_forward(nc, LAYERS[0], c, a, x, dram, out)
        with Names(nc, "gnn1") as m:
            score = m.sb("score", [P, QP * HEADS])
            h_d = dram("h_gnn1", [NR, HROW])
            with Names(nc, "gnn1a") as k:
                split = k.sb("split", [P, NT, 3, HROW], BF16)
                coef = k.sb("coef", [P, 2, KD])
                heads(nc, c, a, x, split, h_d, coef)
                scores(nc, c, e, split, h_d, slot_d, coef, score)
            edge_softmax(nc, c, e, score)
            acc = m.sb("acc1", [P, NT * HROW])
            aggregate(nc, "sum1", c, e, h_d, HROW, acc, score)
            attend(nc, x, acc)
        feed_forward(nc, LAYERS[1], c, a, x, dram, out)


def kernel(**inputs):
    import numpy as np
    import concourse.bacc as bacc
    from concourse.bass_utils import run_bass_kernel_spmd

    laid = dict(inputs)
    for name in ("L0_gnn_W1", "L0_gnn_W2"):
        laid[name] = np.transpose(laid[name])
    laid["L1_gnn_W"] = np.transpose(laid["L1_gnn_W"], (1, 0, 2)).reshape(D, HEADS * HD)

    def on_partitions(v):
        return np.transpose(np.reshape(v, (v.shape[0], -1, P)), (2, 0, 1))
    for name in ("L0_ffn_b1", "L1_ffn_b1", "L0_ffn_ln_g", "L0_ffn_ln_b"):
        laid[name] = on_partitions(np.asarray(laid[name]))
    nc = bacc.Bacc("TRN2", target_bir_lowering=False, num_devices=1)
    arrays, args = {}, {}
    for name, v in laid.items():
        v = np.ascontiguousarray(v)
        arrays[f"in_{name}"] = v
        args[name] = nc.dram_tensor(f"in_{name}", v.shape, mybir.dt.from_np(v.dtype), kind="ExternalInput").ap()
    out = nc.dram_tensor("out_x", (N, D), F32, kind="ExternalOutput").ap()
    build(nc, args, out)
    return run_bass_kernel_spmd(nc, [arrays], core_ids=[0]).results[0]["out_x"]
```

```python
import concourse.bass as bass
from concourse import mybir
from contextlib import ExitStack

F32 = mybir.dt.float32
BF16 = mybir.dt.bfloat16
FP16 = mybir.dt.float16
I32 = mybir.dt.int32
ALU = mybir.AluOpType
ACT = mybir.ActivationFunctionType
AX = mybir.AxisListType.X

P = 128
N, D, E = 3125, 256, 53125
KD = D // P
NT = -(-N // P)
TAIL = N - (NT - 1) * P
TAGS = 2
XROW = D + TAGS
NR = NT * P
BINS = NT + 1
EC = -(-E // P)
Q = (E + NT * (P - 1)) // P
HALF = 10
SLOTS = 2 * HALF
PAIRS = SLOTS // 2
PACK = HALF // 2
BITS = NT.bit_length()
Q = -(-Q // (2 * SLOTS)) * 2 * SLOTS
QP = -(-Q // 16) * 16
NOWHERE = QP * P
MID = N // 2
HEADS, HD = 8, 32
HPART = HD // KD
HROW = D + HEADS
PLACES = 16
SOME = 4
DEPTH = 4
PIECE = 13
NP = EC // PIECE
NEG = -1.0e38
SLOPE = 0.2
ROWG = EC // 4
TOP = 2
FEW = 4
LAYERS = (dict(name="L0", experts=8, hidden=1024), dict(name="L1", experts=16, hidden=512))
for layer in LAYERS:
    layer["blocks"] = (TOP * N + layer["experts"] * (P - 1)) // P


class Names:

    whole = ExitStack()

    def __init__(self, nc, stage):
        self.nc, self.stage, self.ctx, self.sems = nc, stage, ExitStack(), []

    def __enter__(self):
        return self

    def __exit__(self, *error):
        if self.sems and error[0] is None:
            with self.nc.Block() as block:
                @block.gpsimd
                def _(pool):
                    for one in self.sems:
                        pool.sem_clear(one)
        return self.ctx.__exit__(*error)

    def sb(self, name, shape, dt=F32):
        return self.ctx.enter_context(self.nc.sbuf_tensor(f"{self.stage}_{name}", shape, dt))

    def ps(self, name, dt=F32):
        return self.ctx.enter_context(self.nc.psum_tensor(f"{self.stage}_{name}", [P, 512], dt))

    def gather_sem(self, name):
        return Names.whole.enter_context(self.nc.semaphore(f"{self.stage}_{name}"))

    def sem(self, name):
        self.sems.append(self.ctx.enter_context(self.nc.semaphore(f"{self.stage}_{name}")))
        return self.sems[-1]


def rows(dram, t0, t1):
    return dram[t0 * P:t1 * P, :].rearrange("(t p) d -> p t d", p=P)


def load_nodes(eng, tiles, dram, sem):
    eng.dma_start(tiles[:, 0:NT - 1, :], rows(dram, 0, NT - 1)).then_inc(sem, 16)
    eng.dma_start(tiles[0:TAIL, NT - 1, :], dram[(NT - 1) * P:N, :]).then_inc(sem, 16)


def per_tile(ap, inner):
    return ap.unsqueeze(2).to_broadcast([P, NT, inner])


def tile_of(x, t):
    return x[:, bass.ds(t, 1), :].rearrange("p t d -> p (t d)")


class Norm:
    GROUP = 5
    MINE = 3

    def __init__(self, m, tag):
        self.stats = m.sb(f"{tag}_stats", [P, NT, 6])
        self.mean = m.sb(f"{tag}_mean", [P, NT])
        self.var = m.sb(f"{tag}_var", [P, NT])
        self.raw = m.sb(f"{tag}_raw", [P, NT])
        self.gap = m.sb(f"{tag}_gap", [P, NT])
        self.root = m.sb(f"{tag}_root", [P, NT])
        self.scale = m.sb(f"{tag}_scale", [P, NT])
        self.shift = m.sb(f"{tag}_shift", [P, NT])
        self.var_ready = m.sem(f"{tag}_var_ready")
        self.rooted = m.sem(f"{tag}_rooted")
        self.scaled = m.sem(f"{tag}_scaled")

    def over_tiles(self, eng, first, last, step):
        with eng.Fori(0, NT // self.GROUP) as i:
            for j in range(first, last):
                op = step(self.GROUP * i + j)
        return op

    def count(self, nc, x, t):
        return nc.vector.bn_stats(self.stats[:, bass.ds(t, 1), :].rearrange("p t s -> p (t s)"), tile_of(x, t))

    def moments(self, nc, ve):
        nc.vector.tensor_tensor(self.mean[:, :], self.stats[:, :, 1], self.stats[:, :, 4], ALU.add)
        nc.vector.tensor_tensor(self.gap[:, :], self.stats[:, :, 1], self.stats[:, :, 4], ALU.subtract)
        nc.vector.tensor_tensor(self.raw[:, :], self.stats[:, :, 2], self.stats[:, :, 5], ALU.add)
        ve.drain()
        nc.vector.scalar_tensor_tensor(self.gap[:, :], self.gap[:, :], 0.25, self.gap[:, :], ALU.mult, ALU.mult)
        nc.vector.tensor_scalar(self.mean[:, :], self.mean[:, :], 0.5, None, ALU.mult)
        ve.drain()
        nc.vector.scalar_tensor_tensor(self.raw[:, :], self.raw[:, :], 1.0 / D, self.gap[:, :], ALU.mult, ALU.add)
        ve.drain()
        nc.vector.tensor_scalar(self.var[:, :], self.raw[:, :], 1e-5, None, ALU.add).then_inc(self.var_ready, 1)
        ve.wait_ge(self.rooted, 1)
        nc.vector.reciprocal(self.scale[:, :], self.root[:, :])
        ve.drain()
        nc.vector.scalar_tensor_tensor(self.shift[:, :], self.mean[:, :], -1.0, self.scale[:, :], ALU.mult, ALU.mult).then_inc(self.scaled, 1)

    def vector(self, nc, ve, x, z, done):
        self.over_tiles(ve, 0, self.GROUP, lambda t: self.count(nc, x, t))
        ve.drain()
        self.moments(nc, ve)
        self.over_tiles(ve, 0, self.MINE, lambda t: nc.vector.tensor_scalar(
            tile_of(z, t), tile_of(x, t), self.mean[:, bass.ds(t, 1)], self.scale[:, bass.ds(t, 1)], ALU.subtract, ALU.mult))
        ve.drain().then_inc(done, 1)

    def root_of_var(self, nc, act):
        act.wait_ge(self.var_ready, 1)
        nc.scalar.activation(self.root[:, :], self.var[:, :], ACT.Sqrt).then_inc(self.rooted, 1)
        act.wait_ge(self.scaled, 1)
        act.sem_inc(self.scaled, 1)

    def write(self, nc, x, z, t):
        return nc.scalar.activation(tile_of(z, t), tile_of(x, t), ACT.Identity,
                                    bias=self.shift[:, bass.ds(t, 1)], scale=self.scale[:, bass.ds(t, 1)])

    def scalar(self, nc, act, x, z, done):
        self.root_of_var(nc, act)
        self.over_tiles(act, self.MINE, self.GROUP, lambda t: self.write(nc, x, z, t))
        act.drain().then_inc(done, 1)


def constants(nc, c):
    with Names(nc, "const") as m:
        count = m.sb("count", [P, QP], I32)
        lane = m.sb("lane", [P, 1], I32)
        made = m.sem("made")
        copied = m.sem("copied")
        with nc.Block() as block:
            @block.gpsimd
            def _(pool):
                nc.gpsimd.iota(count[:, :], pattern=[[1, QP]], base=0, channel_multiplier=0).then_inc(made, 1)
                nc.gpsimd.iota(lane[:, :], pattern=[[0, 1]], base=0, channel_multiplier=1).then_inc(made, 1)
                nc.gpsimd.memset(c["ident"][:, :], 0.0).then_inc(made, 1)
                nc.gpsimd.memset(c["before"][:, :], 1.0).then_inc(made, 1)
                nc.gpsimd.memset(c["upto"][:, :], 1.0).then_inc(made, 1)
                nc.gpsimd.memset(c["ones"][:, :], 1.0).then_inc(made, 1)
                pool.wait_ge(made, 6)
                nc.gpsimd.affine_select(out=c["ident"][:, :], in_=c["ident"][:, :], compare_op=ALU.not_equal, fill=1.0,
                                        base=0, pattern=[[-1, P]], channel_multiplier=1).then_inc(made, 1)
                nc.gpsimd.affine_select(out=c["before"][:, :], in_=c["before"][:, :], compare_op=ALU.is_gt, fill=0.0,
                                        base=0, pattern=[[1, P]], channel_multiplier=-1).then_inc(made, 1)
                nc.gpsimd.affine_select(out=c["upto"][:, :], in_=c["upto"][:, :], compare_op=ALU.is_ge, fill=0.0,
                                        base=0, pattern=[[1, P]], channel_multiplier=-1).then_inc(made, 1)
                nc.gpsimd.memset(c["by_head"][:, HEADS:], 0.0)
                nc.gpsimd.memset(c["by_head"][:, 0:HEADS], 1.0).then_inc(made, 1)
                pool.wait_ge(made, 10)
                nc.gpsimd.affine_select(out=c["by_head"][:, 0:HEADS], in_=c["by_head"][:, 0:HEADS], compare_op=ALU.is_ge, fill=0.0,
                                        base=0, pattern=[[-HPART, HEADS]], channel_multiplier=1).then_inc(made, 1)
                pool.wait_ge(made, 11)
                nc.gpsimd.affine_select(out=c["by_head"][:, 0:HEADS], in_=c["by_head"][:, 0:HEADS], compare_op=ALU.is_gt, fill=0.0,
                                        base=HPART, pattern=[[HPART, HEADS]], channel_multiplier=-1).then_inc(made, 1)
                pool.wait_ge(made, 12)

            @block.vector
            def _(ve):
                ve.wait_ge(made, 2)
                nc.vector.tensor_copy(c["count_f"][:, :], count[:, 0:P])
                nc.vector.tensor_copy(c["count_h"][:, :], count[:, :])
                nc.vector.tensor_copy(c["count_b"][:, :], count[:, 0:P])
                nc.vector.tensor_copy(c["lane_f"][:, :], lane[:, :])
                ve.wait_ge(made, 9)
                nc.vector.tensor_copy(c["before_b"][:, :], c["before"][:, :])
                nc.vector.tensor_copy(c["ones_b"][:, :], c["ones"][:, :]).then_inc(copied, 1)
                ve.wait_ge(copied, 1)


def sort_edges(nc, c, e, o, src, dst, low_d):
    tile_f, low_f, dst_f, pos_q, pos_r = o["tile_f"], o["low_f"], o["dst_f"], o["pos_q"], o["pos_r"]
    with Names(nc, "sort") as m:
        src_rows = m.sb("src_rows", [ROWG, 4, P], I32)
        dst_rows = m.sb("dst_rows", [ROWG, 4, P], I32)
        rows_f = m.sb("rows_f", [ROWG, 2, 4, P])
        low_i = m.sb("low_i", [ROWG, 4, P], I32)
        low_rows = m.sb("low_rows", [ROWG, 4, P], BF16)
        col_i = m.sb("col_i", [P, EC], I32)
        part_i = m.sb("part_i", [P, 2, EC], I32)
        low_col = m.sb("low_col", [P, EC], BF16)
        tile_col = m.sb("tile_col", [P, EC], BF16)
        in_tile = m.sb("in_tile", [P, EC, BINS], BF16)
        prior = m.sb("prior", [P, (EC + 1) * BINS])
        pos = m.sb("pos", [P, EC])
        low_b = m.sb("low_b", [P, DEPTH, PIECE * P], BF16)
        lane_hot = m.sb("lane_hot", [P, DEPTH, PIECE * P], BF16)
        same = m.sb("same", [P, DEPTH, PIECE * P], BF16)
        earlier = m.sb("earlier", [P, DEPTH, PIECE * P], BF16)
        high = m.sb("high", [P, DEPTH, PIECE * BINS], BF16)
        rest = m.sb("rest", [P, DEPTH, PIECE * BINS], BF16)
        tiles = m.sb("tiles", [P, DEPTH, PIECE * BINS], BF16)
        chosen = m.sb("chosen", [P, PIECE, BINS])
        start = m.sb("start", [P, BINS])
        counts_i = m.sb("counts_i", [P, BINS], I32)
        chunks_f = m.sb("chunks_f", [P, BINS])
        upto_f = m.sb("upto_f", [P, BINS])
        zeros = m.sb("zeros", [P, EC])
        tcol_i = m.sb("tcol_i", [BINS, 1], I32)
        tcol_f = m.sb("tcol_f", [BINS, 1])
        tcum_f = m.sb("tcum_f", [BINS, 1])
        tile_i = m.sb("tile_i", [1, QP], I32)
        past = m.sb("past", [BINS, QP])
        ps = [m.ps(f"ps{i}") for i in range(4)]
        ps_x = m.ps("ps_x")

        filled, loaded, low_ready, low_out = m.sem("filled"), m.sem("loaded"), m.sem("low_ready"), m.sem("low_out")
        rows_ready, turned, cols_ready = m.sem("rows_ready"), m.sem("turned"), m.sem("cols_ready")
        hot_ready, counted, kept = m.sem("hot_ready"), m.sem("counted"), m.sem("kept")
        sums_ready, sums_done, tcol_ready, tcum_done = m.sem("sums_ready"), m.sem("sums_done"), m.sem("tcol_ready"), m.sem("tcum_done")
        tile_done = m.sem("tile_done")
        past_ready = m.sem("past_ready")
        low_in = [m.sem(f"low_in{s}") for s in range(DEPTH)]
        first_ready, high_ready, rest_ready, tiles_ready = m.sem("first_ready"), m.sem("high_ready"), m.sem("rest_ready"), m.sem("tiles_ready")
        act_ready, apart, tiles_first = m.sem("act_ready"), m.sem("apart"), m.sem("tiles_first")
        lane_ready, same_ready, earlier_ready = m.sem("lane_ready"), m.sem("same_ready"), m.sem("earlier_ready")
        looked, picked = m.sem("looked"), m.sem("picked")
        end, act_same = m.sem("end"), m.sem("act_same")
        tick = m.sem("tick")
        prior_v = prior[:, :].rearrange("p (c t) -> p c t", t=BINS)
        full = E - 3 * ROWG * P

        with nc.Block() as block:
            @block.sync
            def _(sp):
                sp.wait_ge(filled, 1)
                for rows_i, edges in ((src_rows, src), (dst_rows, dst)):
                    for g in range(3):
                        sp.dma_start(rows_i[:, g, :], edges[g * ROWG * P:(g + 1) * ROWG * P].rearrange("(c e) -> c e", e=P)).then_inc(loaded, 16)
                    sp.dma_start(rows_i[0:full // P, 3, :], edges[3 * ROWG * P:3 * ROWG * P + full // P * P].rearrange("(c e) -> c e", e=P)).then_inc(loaded, 16)
                    sp.dma_start(rows_i[full // P:full // P + 1, 3, 0:full % P], edges[E - full % P:E].rearrange("(c e) -> c e", c=1)).then_inc(loaded, 16)
                sp.wait_ge(low_ready, 1)
                for g in range(4):
                    sp.dma_start(low_d[g * ROWG:(g + 1) * ROWG, :], low_rows[:, g, :]).then_inc(low_out, 16)
                sp.wait_ge(low_out, 64)

                def spread(piece, s):
                    sp.dma_start(low_b[:, s, :], low_d[bass.ds(piece * PIECE, PIECE), :].rearrange("c e -> (c e)").partition_broadcast(P)).then_inc(low_in[s], 16)
                for s in range(DEPTH):
                    spread(s, s)
                with sp.Fori(1, NP // DEPTH) as i:
                    for s in range(DEPTH):
                        if s < DEPTH - 1:
                            sp.wait_ge(same_ready, (DEPTH - 1) * (i - 1) + s + 1)
                        else:
                            sp.wait_ge(lane_ready, DEPTH * i)
                            sp.wait_ge(act_same, i)
                        spread(DEPTH * i + s, s)

            @block.gpsimd
            def _(pool):
                pool.wait_ge(cols_ready, 1)
                pool.sem_inc(tick, 1)
                with pool.Fori(0, NP // DEPTH) as i:
                    for s in range(DEPTH):
                        n = DEPTH * i + s
                        pool.wait_ge(counted, n + 1)
                        pool.sem_inc(tick, 1)
                        nc.gpsimd.tensor_copy(tiles[:, s, :], in_tile[:, bass.ds(n * PIECE, PIECE), :].rearrange("p c t -> p (c t)")).then_inc(tiles_first, 1)
                pool.wait_ge(first_ready, 1)
                pool.sem_inc(tick, 1)
                with pool.Fori(0, NP // DEPTH) as i:
                    for s in range(DEPTH):
                        n = DEPTH * i + s
                        pool.wait_ge(high_ready, n + 1)
                        pool.wait_ge(looked, n + 1)
                        pool.sem_inc(tick, 1)
                        nc.gpsimd.tensor_tensor(rest[:, s, :], prior_v[:, bass.ds(n * PIECE, PIECE), :].rearrange("p c t -> p (c t)"),
                                                high[:, s, :], ALU.subtract).then_inc(rest_ready, 1)
                        if s < DEPTH - 1:
                            pool.wait_ge(same_ready, (DEPTH - 1) * i + s + 1)
                        else:
                            pool.wait_ge(act_same, i + 1)
                        pool.sem_inc(tick, 1)
                        nc.gpsimd.affine_select(out=earlier[:, s, :].rearrange("p (c e) -> p c e", e=P),
                                                in_=same[:, s, :].rearrange("p (c e) -> p c e", e=P),
                                                compare_op=ALU.is_gt, fill=0.0, base=0, pattern=[[0, PIECE], [1, P]],
                                                channel_multiplier=-1).then_inc(earlier_ready, 1)

            @block.scalar
            def _(act):
                act.wait_ge(cols_ready, 1)
                act.sem_inc(kept, DEPTH)
                with act.Fori(0, NP // DEPTH) as i:
                    s = DEPTH - 1
                    act.wait_ge(counted, DEPTH * (i + 1))
                    act.sem_inc(tick, 1)
                    for j in range(PIECE):
                        last = nc.scalar.activation(same[:, s, j * P:(j + 1) * P], c["count_b"][:, :], ACT.Abs, scale=-1.0,
                                                    bias=low_f[:, bass.ds((DEPTH * i + s) * PIECE + j, 1)])
                    last.then_inc(apart, 1)
                    act.wait_ge(apart, i + 1)
                    act.sem_inc(tick, 1)
                    nc.scalar.activation(same[:, s, :], same[:, s, :], ACT.Relu, scale=-1.0, bias=c["ones"][:, 0:1]).then_inc(act_ready, 1)
                    for s in range(DEPTH):
                        act.wait_ge(counted, DEPTH + DEPTH * i + s + 1)
                        act.sem_inc(tick, 1)
                        nc.scalar.activation(prior[:, bass.ds(((DEPTH * i + s) * PIECE + 1) * BINS, PIECE * BINS)],
                                             ps[s][:, 0:PIECE * BINS], ACT.Copy).then_inc(kept, 1)
                act.wait_ge(first_ready, 1)
                act.sem_inc(tick, 1)
                with act.Fori(0, NP // DEPTH) as i:
                    for s in range(DEPTH):
                        piece = bass.ds((DEPTH * i + s) * PIECE, PIECE)
                        act.wait_ge(looked, DEPTH * i + s + 1)
                        act.sem_inc(tick, 1)
                        nc.scalar.activation(high[:, s, :], prior_v[:, piece, :].rearrange("p c t -> p (c t)"), ACT.Copy).then_inc(high_ready, 1)
                        nc.scalar.activation(tiles[:, s, :], in_tile[:, piece, :].rearrange("p c t -> p (c t)"), ACT.Copy).then_inc(tiles_ready, 1)
                        if s == 1:
                            other = DEPTH - 1
                            act.wait_ge(low_in[other], 16 * i + 16)
                            act.wait_ge(looked, DEPTH * i + other + 1)
                            act.sem_inc(tick, 1)
                            for j in range(PIECE):
                                last = nc.scalar.activation(same[:, other, j * P:(j + 1) * P], low_b[:, other, j * P:(j + 1) * P], ACT.Abs, scale=-1.0,
                                                            bias=low_f[:, bass.ds((DEPTH * i + other) * PIECE + j, 1)])
                            last.then_inc(apart, 1)
                            act.wait_ge(apart, NP // DEPTH + i + 1)
                            act.sem_inc(tick, 1)
                            nc.scalar.activation(same[:, other, :], same[:, other, :], ACT.Relu, scale=-1.0, bias=c["ones"][:, 0:1]).then_inc(act_same, 1)

            @block.tensor
            def _(pe):
                pe.wait_ge(rows_ready, 1)
                for k in range(2):
                    for g in range(4):
                        last = nc.tensor.transpose(ps[2 + k][:, g * ROWG:(g + 1) * ROWG], rows_f[:, k, g, :], c["ident"][0:ROWG, 0:ROWG])
                last.then_inc(turned, 1)
                pe.sem_inc(counted, DEPTH)
                with pe.Fori(0, NP // DEPTH) as i:
                    for s in range(DEPTH):
                        if s < DEPTH - 1:
                            pe.wait_ge(hot_ready, (DEPTH - 1) * i + s + 1)
                        else:
                            pe.wait_ge(act_ready, i + 1)
                        pe.wait_ge(tiles_first, DEPTH * i + s + 1)
                        pe.wait_ge(kept, DEPTH * i + s + 1)
                        pe.sem_inc(tick, 1)
                        for j in range(PIECE):
                            last = nc.tensor.matmul(ps[s][:, j * BINS:(j + 1) * BINS], same[:, s, j * P:(j + 1) * P],
                                                    tiles[:, s, j * BINS:(j + 1) * BINS], start=True, stop=True)
                        last.then_inc(counted, 1)
                pe.wait_ge(sums_ready, 1)
                total = prior_v[:, EC, :]
                nc.tensor.matmul(ps_x[:, 0:BINS], c["ones"][:, :], total, start=True, stop=True)
                nc.tensor.matmul(ps_x[:, BINS:2 * BINS], c["before"][:, :], total, start=True, stop=True)
                nc.tensor.matmul(ps_x[0:BINS, 2 * BINS:2 * BINS + 1], total, c["ones"][:, 0:1], start=True, stop=True).then_inc(sums_done, 1)
                pe.wait_ge(tcol_ready, 1)
                nc.tensor.matmul(ps[3][0:BINS, 0:1], c["upto"][0:BINS, 0:BINS], tcol_f[:, :], start=True, stop=True).then_inc(tcum_done, 1)
                pe.wait_ge(past_ready, 1)
                nc.tensor.matmul(ps[2][:, 0:QP], c["ones"][0:NT, :], past[0:NT, :], start=True, stop=True).then_inc(tile_done, 1)
                pe.sem_inc(looked, DEPTH)
                with pe.Fori(0, NP // DEPTH) as i:
                    for s in range(DEPTH):
                        n = DEPTH * i + s
                        pe.wait_ge(lane_ready, n + 1)
                        pe.wait_ge(rest_ready, n + 1)
                        pe.wait_ge(earlier_ready, n + 1)
                        pe.wait_ge(tiles_ready, n + 1)
                        pe.wait_ge(picked, n + 1)
                        pe.sem_inc(tick, 1)
                        for j in range(PIECE):
                            bins = slice(j * BINS, (j + 1) * BINS)
                            hot = lane_hot[:, s, j * P:(j + 1) * P]
                            nc.tensor.matmul(ps[s][:, bins], hot, high[:, s, bins], start=True, stop=False)
                            nc.tensor.matmul(ps[s][:, bins], hot, rest[:, s, bins], start=False, stop=False)
                            last = nc.tensor.matmul(ps[s][:, bins], earlier[:, s, j * P:(j + 1) * P], tiles[:, s, bins], start=False, stop=True)
                        last.then_inc(looked, 1)

            @block.vector
            def _(ve):
                nc.vector.memset(src_rows[:, :, :], NT * P)
                nc.vector.memset(dst_rows[:, :, :], 0).then_inc(filled, 1)
                nc.vector.memset(zeros[:, :], 0.0)
                nc.vector.memset(prior[:, 0:BINS], 0.0)
                ve.wait_ge(loaded, 160)
                nc.vector.tensor_copy(rows_f[:, 0, :, :], src_rows[:, :, :])
                nc.vector.tensor_copy(rows_f[:, 1, :, :], dst_rows[:, :, :]).then_inc(rows_ready, 1)
                nc.vector.tensor_scalar(low_i[:, :, :], src_rows[:, :, :], P - 1, None, ALU.bitwise_and)
                ve.drain()
                nc.vector.tensor_copy(low_rows[:, :, :], low_i[:, :, :]).then_inc(low_ready, 1)
                ve.wait_ge(turned, 1)
                nc.vector.tensor_copy(col_i[:, :], ps[2][:, 0:EC])
                nc.vector.tensor_scalar(dst_f[:, :], ps[3][:, 0:EC], -float(MID), None, ALU.add)
                ve.drain()
                nc.vector.tensor_scalar(part_i[:, 0, :], col_i[:, :], P - 1, None, ALU.bitwise_and)
                nc.vector.tensor_scalar(part_i[:, 1, :], col_i[:, :], 7, None, ALU.arith_shift_right)
                ve.drain()
                nc.vector.tensor_copy(low_col[:, :], part_i[:, 0, :])
                nc.vector.tensor_copy(low_f[:, :], part_i[:, 0, :])
                nc.vector.tensor_copy(tile_col[:, :], part_i[:, 1, :])
                ve.drain()
                nc.vector.tensor_tensor(in_tile[:, :, :], tile_col[:, :].unsqueeze(2).to_broadcast([P, EC, BINS]),
                                        c["count_b"][:, 0:BINS].unsqueeze(1).to_broadcast([P, EC, BINS]), ALU.is_equal)
                ve.drain()
                ve.sem_inc(cols_ready, 1)
                with ve.Fori(0, NP // DEPTH) as i:
                    for s in range(DEPTH - 1):
                        ve.wait_ge(counted, DEPTH * i + s + 1)
                        nc.vector.tensor_tensor(same[:, s, :].rearrange("p (c e) -> p c e", e=P),
                                                low_col[:, bass.ds((DEPTH * i + s) * PIECE, PIECE)].unsqueeze(2).to_broadcast([P, PIECE, P]),
                                                c["count_b"][:, :].unsqueeze(1).to_broadcast([P, PIECE, P]), ALU.is_equal).then_inc(hot_ready, 1)
                ve.wait_ge(kept, DEPTH + NP)
                with ve.Fori(0, BINS) as t:
                    sl = prior_v[:, 1:EC + 1, bass.ds(t, 1)].rearrange("p c t -> p (c t)")
                    nc.vector.tensor_tensor_scan(sl, zeros[:, :], sl, 0.0, ALU.add, ALU.add)
                ve.drain()
                nc.vector.tensor_copy(e["degree"][:, :], prior_v[:, EC, 0:NT]).then_inc(sums_ready, 1)
                ve.wait_ge(sums_done, 1)
                nc.vector.tensor_scalar(counts_i[:, :], ps_x[:, 0:BINS], float(P - 1), None, ALU.add)
                nc.vector.tensor_scalar(tcol_i[:, :], ps_x[0:BINS, 2 * BINS:2 * BINS + 1], float(P - 1), None, ALU.add)
                ve.drain()
                nc.vector.tensor_scalar(counts_i[:, :], counts_i[:, :], 7, None, ALU.arith_shift_right)
                nc.vector.tensor_scalar(tcol_i[:, :], tcol_i[:, :], 7, None, ALU.arith_shift_right)
                ve.drain()
                nc.vector.tensor_copy(tcol_f[:, :], tcol_i[:, :]).then_inc(tcol_ready, 1)
                nc.vector.tensor_copy(chunks_f[:, :], counts_i[:, :])
                ve.drain()
                nc.vector.tensor_tensor_scan(upto_f[:, :], zeros[:, 0:BINS], chunks_f[:, :], 0.0, ALU.add, ALU.add)
                ve.drain()
                nc.vector.tensor_tensor(start[:, :], upto_f[:, :], chunks_f[:, :], ALU.subtract)
                ve.drain()
                nc.vector.scalar_tensor_tensor(start[:, :], start[:, :], float(P), ps_x[:, BINS:2 * BINS], ALU.mult, ALU.add)
                ve.drain()
                nc.vector.memset(start[:, NT:BINS], float(NOWHERE))
                ve.drain()
                nc.vector.tensor_tensor(prior_v[:, 0:EC, :], prior_v[:, 0:EC, :], start[:, :].unsqueeze(1).to_broadcast([P, EC, BINS]),
                                        ALU.add).then_inc(first_ready, 1)
                ve.wait_ge(tcum_done, 1)
                nc.vector.tensor_copy(tcum_f[:, :], ps[3][0:BINS, 0:1])
                ve.drain()
                nc.vector.tensor_scalar(past[:, :], c["count_h"][0:BINS, :], tcum_f[:, 0:1], None, ALU.is_ge).then_inc(past_ready, 1)
                ve.wait_ge(tile_done, 1)
                nc.vector.tensor_scalar(tile_f[:, :], ps[2][:, 0:QP], 1.0, None, ALU.mult)
                nc.vector.tensor_scalar(tile_i[:, :], ps[2][0:1, 0:QP], float(NT - 1), None, ALU.min)
                ve.drain()
                nc.vector.tensor_copy(e["tiles"][:, :], tile_i[:, 0:Q:PACK])
                for j in range(1, PACK):
                    nc.vector.tensor_scalar(tile_i[:, j:Q:PACK], tile_i[:, j:Q:PACK], BITS * j, None, ALU.logical_shift_left)
                ve.drain()
                for j in range(1, PACK):
                    nc.vector.tensor_tensor(e["tiles"][:, :], e["tiles"][:, :], tile_i[:, j:Q:PACK], ALU.bitwise_or)
                    ve.drain()
                def compare(piece, s):
                    nc.vector.tensor_scalar(lane_hot[:, s, :], low_b[:, s, :], c["lane_f"][:, 0:1], None, ALU.is_equal).then_inc(lane_ready, 1)
                    if s == DEPTH - 1:
                        return
                    nc.vector.tensor_tensor(same[:, s, :].rearrange("p (c e) -> p c e", e=P),
                                            low_b[:, s, :].rearrange("p (c e) -> p c e", e=P),
                                            low_col[:, bass.ds(piece * PIECE, PIECE)].unsqueeze(2).to_broadcast([P, PIECE, P]),
                                            ALU.is_equal).then_inc(same_ready, 1)

                def pick(piece, s):
                    ve.wait_ge(looked, DEPTH + piece + 1)
                    ve.sem_inc(tick, 1)
                    nc.vector.tensor_tensor(chosen[:, :, :], ps[s][:, 0:PIECE * BINS].rearrange("p (c t) -> p c t", t=BINS),
                                            in_tile[:, bass.ds(piece * PIECE, PIECE), :], ALU.mult).then_inc(picked, 1)
                    ve.drain()
                    nc.vector.tensor_reduce(pos[:, bass.ds(piece * PIECE, PIECE)], chosen[:, :, :], AX, ALU.add)
                    ve.drain()

                def look(piece, s, turn):
                    ve.wait_ge(low_in[s], turn)
                    ve.sem_inc(tick, 1)
                    compare(piece, s)

                lag = DEPTH - 1
                ve.sem_inc(picked, DEPTH)
                for s in range(DEPTH):
                    if s >= lag:
                        pick(s - lag, s - lag)
                    look(s, s, 16)
                with ve.Fori(1, NP // DEPTH) as i:
                    for s in range(DEPTH):
                        pick(DEPTH * i + s - lag, (s - lag) % DEPTH)
                        look(DEPTH * i + s, s, 16 * i + 16)
                for n in range(NP - lag, NP):
                    pick(n, n % DEPTH)
                ve.drain()
                nc.vector.tensor_copy(col_i[:, :], pos[:, :])
                ve.drain()
                nc.vector.tensor_scalar(part_i[:, 0, :], col_i[:, :], P - 1, None, ALU.bitwise_and)
                nc.vector.tensor_scalar(part_i[:, 1, :], col_i[:, :], 7, None, ALU.arith_shift_right)
                ve.drain()
                nc.vector.tensor_scalar(low_f[:, :], low_f[:, :], 1.0, None, ALU.add)
                nc.vector.tensor_copy(pos_r[:, :], part_i[:, 0, :])
                nc.vector.tensor_copy(pos_q[:, :], part_i[:, 1, :]).then_inc(end, 1)
                ve.wait_ge(end, 1)


def place_edges(nc, c, e, o, slot_d):
    tile_f, low_f, dst_f, pos_q, pos_r = o["tile_f"], o["low_f"], o["dst_f"], o["pos_q"], o["pos_r"]
    with Names(nc, "place") as m:
        nothing = m.sb("nothing", [P, QP], FP16)
        slot_rows = m.sb("slot_rows", [P, -(-QP // P), P], FP16)
        chunk_hot = m.sb("chunk_hot", [P, PLACES, QP], FP16)
        lane_of = m.sb("lane_of", [P, PLACES, P], FP16)
        dst_hot = m.sb("dst_hot", [P, PLACES, P], FP16)
        src_hot = m.sb("src_hot", [P, PLACES, P], FP16)
        ps_dst, ps_src, ps_x = m.ps("ps_dst"), m.ps("ps_src"), m.ps("ps_x")
        empty_ready, place_ready, dst_ready, src_ready, placed, all_placed = (
            m.sem(n) for n in ("empty_ready", "place_ready", "dst_ready", "src_ready", "placed", "all_placed"))
        slots_ready, slots_turned, rows_kept, rows_out, end, tick = (
            m.sem(n) for n in ("slots_ready", "slots_turned", "rows_kept", "rows_out", "end", "tick"))
        groups = [(g, min(P, QP - g * P)) for g in range(-(-QP // P))]
        with nc.Block() as block:
            @block.sync
            def _(sp):
                sp.wait_ge(rows_kept, 1)
                for g, n in groups:
                    sp.dma_start(slot_d[g * P:g * P + n, :], slot_rows[0:n, g, :]).then_inc(rows_out, 16)
                sp.wait_ge(rows_out, 16 * len(groups))

            @block.vector
            def _(ve):
                nc.vector.memset(nothing[:, :], 0.0).then_inc(empty_ready, 1)
                with ve.Fori(0, EC // PLACES) as i:
                    for s in range(PLACES):
                        k = PLACES * i + s
                        if s % SOME == 0:
                            ve.wait_ge(placed, k + SOME)
                            ve.sem_inc(tick, 1)
                        nc.vector.tensor_scalar(lane_of[:, s, :], c["count_h"][:, 0:P], pos_r[:, bass.ds(k, 1)], None, ALU.is_equal)
                        nc.vector.tensor_scalar(chunk_hot[:, s, :], c["count_h"][:, :], pos_q[:, bass.ds(k, 1)], None, ALU.is_equal).then_inc(place_ready, 1)
                ve.wait_ge(all_placed, 1)
                nc.vector.tensor_scalar(e["slot_src"][:, :], ps_src[:, 0:QP], -1.0, None, ALU.add).then_inc(slots_ready, 1)
                nc.vector.tensor_scalar(e["slot_dst"][:, :], ps_dst[:, 0:QP], float(MID), None, ALU.add)
                ve.wait_ge(slots_turned, 1)
                for g, n in groups:
                    last = nc.vector.tensor_copy(slot_rows[0:n, g, :], ps_x[0:n, g * P:(g + 1) * P])
                last.then_inc(rows_kept, 1)
                nc.vector.scalar_tensor_tensor(e["slot_node"][:, :], tile_f[:, :], float(P), e["slot_src"][:, :], ALU.mult, ALU.add).then_inc(end, 1)
                ve.wait_ge(end, 1)

            @block.gpsimd
            def _(pool):
                with pool.Fori(0, EC // PLACES) as i:
                    for g in range(PLACES // SOME):
                        mine = slice(g * SOME, (g + 1) * SOME)
                        pool.wait_ge(place_ready, PLACES * i + SOME * (g + 1))
                        pool.wait_ge(placed, PLACES * i + SOME * (g + 1))
                        pool.sem_inc(tick, 1)
                        nc.gpsimd.tensor_tensor(src_hot[:, mine, :], lane_of[:, mine, :],
                                                low_f[:, bass.ds(PLACES * i + SOME * g, SOME)].unsqueeze(2).to_broadcast([P, SOME, P]),
                                                ALU.mult).then_inc(src_ready, 1)

            @block.scalar
            def _(act):
                with act.Fori(0, EC // PLACES) as i:
                    for s in range(PLACES):
                        k = PLACES * i + s
                        act.wait_ge(place_ready, k + 1)
                        act.wait_ge(placed, k + 1)
                        act.sem_inc(tick, 1)
                        nc.scalar.activation(dst_hot[:, s, :], lane_of[:, s, :], ACT.Copy, scale=dst_f[:, bass.ds(k, 1)]).then_inc(dst_ready, 1)

            @block.tensor
            def _(pe):
                pe.wait_ge(empty_ready, 1)
                nc.tensor.matmul(ps_dst[:, 0:QP], nothing[:, 0:P], nothing[:, :], start=True, stop=False)
                nc.tensor.matmul(ps_src[:, 0:QP], nothing[:, 0:P], nothing[:, :], start=True, stop=False)
                pe.sem_inc(placed, PLACES)
                with pe.Fori(0, EC // PLACES) as i:
                    for s in range(PLACES):
                        k = PLACES * i + s
                        pe.wait_ge(dst_ready, k + 1)
                        if s % SOME == 0:
                            pe.wait_ge(src_ready, PLACES // SOME * i + s // SOME + 1)
                        pe.sem_inc(tick, 1)
                        nc.tensor.matmul(ps_dst[:, 0:QP], dst_hot[:, s, :], chunk_hot[:, s, :], start=False, stop=False)
                        nc.tensor.matmul(ps_src[:, 0:QP], src_hot[:, s, :], chunk_hot[:, s, :], start=False, stop=False).then_inc(placed, 1)
                nc.tensor.matmul(ps_dst[:, 0:QP], nothing[:, 0:P], nothing[:, :], start=False, stop=True)
                nc.tensor.matmul(ps_src[:, 0:QP], nothing[:, 0:P], nothing[:, :], start=False, stop=True).then_inc(all_placed, 1)
                pe.wait_ge(slots_ready, 1)
                for g, n in groups:
                    last = nc.tensor.transpose(ps_x[0:n, g * P:(g + 1) * P], e["slot_src"][:, g * P:g * P + n], c["ident"][:, :])
                last.then_inc(slots_turned, 1)


class Project:

    def __init__(self, m, chunks, width, staged=None):
        self.chunks, self.width = chunks, width
        self.turned_ps = [m.ps(f"turned_ps{s}") for s in range(2)]
        self.out_ps = [m.ps(f"out_ps{s}") for s in range(2)]
        self.turned = m.sb("turned", [P, 2, chunks * P])
        self.staged = m.sb("staged", [P, 2, chunks * P]) if staged is None else staged
        self.brought = m.sem("brought")
        self.turn_done, self.copied = m.sem("turn_done"), m.sem("copied")
        self.product, self.used = m.sem("product"), m.sem("used")
        self.tick = m.sem("project_tick")

    def over_tiles(self, eng, step, tiles=NT):
        with eng.Fori(0, tiles // 2) as i:
            for s in range(2):
                step(2 * i + s, s)
        for t in range(tiles // 2 * 2, tiles):
            step(t, t % 2)

    def tensor(self, nc, pe, ident, weight):
        pe.sem_inc(self.product, 2)
        pe.sem_inc(self.turn_done, 2)

        def turn(t, s):
            pe.wait_ge(self.brought, t + 1)
            pe.wait_ge(self.copied, t + 1)
            pe.sem_inc(self.tick, 1)
            for j in range(self.chunks):
                last = nc.tensor.transpose(self.turned_ps[s][:, j * P:(j + 1) * P], self.staged[:, s, j * P:(j + 1) * P], ident)
            last.then_inc(self.turn_done, 1)

        def multiply(t, s):
            pe.wait_ge(self.copied, 2 + t + 1)
            pe.wait_ge(self.used, t + 1)
            pe.sem_inc(self.tick, 1)
            for j in range(self.chunks):
                last = nc.tensor.matmul(self.out_ps[s][:, 0:self.width], self.turned[:, s, j * P:(j + 1) * P], weight(j),
                                        start=(j == 0), stop=(j == self.chunks - 1))
            last.then_inc(self.product, 1)

        def step(t, s):
            turn(t + 1, 1 - s)
            multiply(t, s)
        turn(0, 0)
        self.over_tiles(pe, step, NT - 1)
        multiply(NT - 1, (NT - 1) % 2)

    def scalar(self, nc, act, keep=None):
        act.sem_inc(self.copied, 2)

        def copy(t, s):
            act.wait_ge(self.turn_done, 2 + t + 1)
            act.wait_ge(self.product, t + 1)
            act.sem_inc(self.tick, 1)
            nc.scalar.activation(self.turned[:, s, :], self.turned_ps[s][:, 0:self.chunks * P], ACT.Copy).then_inc(self.copied, 1)

        def store(t, s):
            act.wait_ge(self.product, 2 + t + 1)
            act.sem_inc(self.tick, 1)
            nc.scalar.activation(keep(t), self.out_ps[s][:, 0:self.width], ACT.Copy).then_inc(self.used, 1)

        if keep is None:
            self.over_tiles(act, copy)
            return
        act.sem_inc(self.used, 2)

        def step(t, s):
            copy(t + 1, 1 - s)
            store(t, s)
        copy(0, 0)
        self.over_tiles(act, step, NT - 1)
        store(NT - 1, (NT - 1) % 2)

    def fetch(self, eng, bring, t, s):
        eng.wait_ge(self.turn_done, t + 1)
        eng.sem_inc(self.tick, 1)
        bring(t, self.staged[:, s, 0:self.chunks * P]).then_inc(self.brought, 1)

    def pool(self, pool, bring):
        self.over_tiles(pool, lambda t, s: self.fetch(pool, bring, t, s))

    def vector(self, ve, bring, use):
        def fetch(t, s):
            self.fetch(ve, bring, t, s)

        ve.sem_inc(self.used, 2)

        def finish(t, s):
            ve.wait_ge(self.product, 2 + t + 1)
            ve.sem_inc(self.tick, 1)
            use(t, self.out_ps[s][:, 0:self.width]).then_inc(self.used, 1)

        def step(t, s):
            fetch(t + 2, s)
            finish(t, s)
        if bring is None:
            self.over_tiles(ve, finish)
            return
        for t in range(2):
            fetch(t, t)
        self.over_tiles(ve, step, NT - 2)
        for t in range(NT - 2, NT):
            finish(t, t % 2)


def first_norm(nc, x_in, x, z_d):
    with Names(nc, "norm0") as m:
        z = m.sb("z", [P, NT, D])
        norm = Norm(m, "ln")
        cleared, loaded, normed, stored = m.sem("cleared"), m.sem("loaded"), m.sem("normed"), m.sem("stored")
        with nc.Block() as block:
            @block.sync
            def _(sp):
                sp.wait_ge(cleared, 1)
                load_nodes(sp, x, x_in, loaded)
                sp.wait_ge(normed, 2)
                sp.dma_start(rows(z_d, 0, NT), z[:, :, :]).then_inc(stored, 16)
                sp.wait_ge(stored, 16)

            @block.vector
            def _(ve):
                nc.vector.memset(x[:, NT - 1, :], 0.0).then_inc(cleared, 1)
                ve.wait_ge(loaded, 32)
                norm.vector(nc, ve, x, z, normed)
                ve.wait_ge(stored, 16)

            @block.scalar
            def _(act):
                norm.scalar(nc, act, x, z, normed)


class Gather:

    def __init__(self, m, width, ordered=False):
        self.rows = m.sb("rows", [P, SLOTS, width])
        self.index = m.sb("index", [P, 2, SLOTS], I32)
        self.index_ready = m.sem("index_ready")
        self.width = width
        self.landed = [(m.sem if ordered else m.gather_sem)(f"landed{p}") for p in range(PAIRS)]
        self.freed = m.sem("freed")
        self.tick = m.sem("gather_tick")

    def pool(self, nc, pool, e, table):
        turns = Q // SLOTS

        def bring(turn, b):
            nc.gpsimd.tensor_copy(self.index[:, b, :], e["slot_dst"][:, bass.ds(SLOTS * turn, SLOTS)]).then_inc(self.index_ready, 1)

        def gather(turn, b, last):
            for h in range(2):
                pool.wait_ge(self.freed, 2 * turn + h + 1)
                if h == 0:
                    pool.wait_ge(self.index_ready, turn + 1)
                pool.sem_inc(self.tick, 1)
                for s in range(h * HALF, (h + 1) * HALF):
                    if s == SLOTS - 1 and not last:
                        bring(turn + 1, 1 - b)
                    pool.indirect_dma_start(out=self.rows[:, s, :], out_offset=None, in_=table[:, :],
                                            in_offset=bass.IndirectOffsetOnAxis(ap=self.index[:, b, s:s + 1], axis=0)).then_inc(self.landed[s // 2], 16)
        bring(0, 0)
        with pool.Fori(0, turns // 2 - 1) as i:
            for b in range(2):
                gather(2 * i + b, b, False)
        for turn in range(turns - 2, turns):
            gather(turn, turn % 2, turn == turns - 1)

    def load(self, sp, saved_d, i):
        for h in range(2):
            sp.wait_ge(self.freed, 2 * i + h + 1)
            for p in range(h * HALF // 2, (h + 1) * HALF // 2):
                mine = slice(2 * p % HALF * self.width, (2 * p % HALF + 2) * self.width)
                sp.dma_start(self.rows[:, 2 * p:2 * p + 2, :].rearrange("p s w -> p (s w)"),
                             saved_d[bass.ds(2 * i + h, 1), :, mine].rearrange("o p w -> p (o w)")).then_inc(self.landed[p], 16)


def tiles_of(nc, engine, e, part, count):
    per = count // PACK
    packed = nc.values_load_multi_w_load_instructions(e["tiles"][0:1, bass.ds(part * per, per)], engines=[engine],
                                                      min_val=0, max_val=2 ** (BITS * PACK) - 1)[1]
    return [((v >> BITS * j) & 2 ** BITS - 1).with_bounds(min_val=0, max_val=NT - 1) for v in packed for j in range(PACK)]


def aggregate(nc, stage, c, e, table, width, acc, slots, weight=None, saved_d=None, ahead=None):
    blocks = slots.shape[0] // P
    out_width = HROW if weight is not None else D
    banks = HALF // 2
    turns = Q // SLOTS
    with Names(nc, stage) as m:
        g = Gather(m, width, weight is not None)
        pick = m.sb("pick", [P, 2, HALF, P])
        scaled = m.sb("scaled", [P, SLOTS, HROW]) if weight is not None else None
        sums = [acc] if weight is None else [acc, m.sb("odd", [P, NT * HROW])]
        blank = m.sb("blank", [P, XROW])
        cleared, zeroed = m.sem("cleared"), m.sem("zeroed")
        ps = [m.ps(f"ps{i}") for i in range(banks)]
        apart, pick_ready, scaled_ready, summed, added, joined, weighed, tick = (
            m.sem(n) for n in ("apart", "pick_ready", "scaled_ready", "summed", "added", "joined", "weighed", "tick"))
        with nc.Block() as block:
            def scale(pool):
                with pool.Fori(0, turns) as i:
                    for p in range(PAIRS):
                        pool.wait_ge(g.landed[p], 16 * i + 16)
                        pool.sem_inc(tick, 1)
                        nc.gpsimd.tensor_tensor(scaled[:, 2 * p:2 * p + 2, 0:D].rearrange("p s (h d) -> p s h d", d=HD),
                                                g.rows[:, 2 * p:2 * p + 2, 0:D].rearrange("p s (h d) -> p s h d", d=HD),
                                                weight[:, bass.ds((PAIRS * i + p) * 2 * HEADS, 2 * HEADS)].rearrange("p (s h) -> p s h", h=HEADS).unsqueeze(3).to_broadcast([P, 2, HEADS, HD]),
                                                ALU.mult).then_inc(scaled_ready, 1)

            @block.sync
            def _(sp):
                def fill(block):
                    sp.dma_start(slots[bass.ds(block * P, P), :], blank[:, :]).then_inc(zeroed, 16)

                if ahead:
                    ahead.load(sp)
                sp.wait_ge(cleared, 1)
                with sp.Fori(0, turns) as i:
                    if weight is not None:
                        g.load(sp, saved_d, i)
                    for b in range(blocks // turns):
                        fill(i * (blocks // turns) + b)
                for b in range(blocks // turns * turns, blocks):
                    fill(b)
                sp.wait_ge(zeroed, 16 * blocks)

            @block.gpsimd
            def _(pool):
                if weight is None:
                    g.pool(nc, pool, e, table)
                else:
                    scale(pool)

            @block.scalar
            def _(act):
                with act.Fori(0, turns) as i:
                    for h in range(2):
                        act.wait_ge(g.freed, 2 * i + h + 1)
                        act.sem_inc(tick, 1)
                        for s in range(HALF):
                            last = nc.scalar.activation(pick[:, h, s, :], c["count_f"][:, 0:P], ACT.Abs, scale=-1.0,
                                                        bias=e["slot_src"][:, bass.ds((2 * i + h) * HALF + s, 1)])
                        last.then_inc(apart, 1)
                        act.wait_ge(apart, 2 * i + h + 1)
                        act.sem_inc(tick, 1)
                        nc.scalar.activation(pick[:, h, :, :], pick[:, h, :, :], ACT.Relu, scale=-1.0, bias=c["ones"][:, 0:1]).then_inc(pick_ready, 1)
                        if weight is None:
                            continue
                        nc.scalar.activation(scaled[:, h * HALF:(h + 1) * HALF, D:HROW],
                                             weight[:, bass.ds((2 * i + h) * HALF * HEADS, HALF * HEADS)].rearrange("p (s h) -> p s h", h=HEADS),
                                             ACT.Copy).then_inc(weighed, 1)

            @block.tensor
            def _(pe):
                pe.sem_inc(g.freed, 2)
                with pe.Fori(0, turns) as i:
                    for s in range(SLOTS):
                        k, h = SLOTS * i + s, s // HALF
                        if s % HALF == 0:
                            pe.wait_ge(pick_ready, 2 * i + h + 1)
                            if weight is not None:
                                pe.wait_ge(weighed, 2 * i + h + 1)
                        if s % 2 == 0 and weight is None:
                            pe.wait_ge(g.landed[s // 2], 32 * i + 32)
                        elif s % 2 == 0:
                            pe.wait_ge(scaled_ready, PAIRS * i + s // 2 + 1)
                        pe.wait_ge(added, k + 1)
                        pe.sem_inc(tick, 1)
                        rhs = g.rows[:, s, 0:D] if weight is None else scaled[:, s, :]
                        last = nc.tensor.matmul(ps[s % banks][:, 0:out_width], pick[:, h, s % HALF, :], rhs, start=True, stop=True)
                        last.then_inc(summed, 1)
                        if s % HALF == HALF - 1:
                            pe.wait_ge(summed, k + 1)
                            pe.sem_inc(g.freed, 1)

            @block.vector
            def _(ve):
                def add_pair(k, s, pair):
                    columns = [nc.snap(tile * HROW, engines=[nc.vector.engine], min_val=0, max_val=(NT - 1) * HROW) for tile in pair]
                    ve.wait_ge(summed, k + 2)
                    ve.wait_ge(added, banks + k)
                    ve.sem_inc(tick, 1)
                    for j, column in enumerate(columns):
                        mine = sums[j % len(sums)][:, bass.ds(column, out_width)]
                        if j and len(sums) == 1:
                            ve.wait_ge(added, banks + k + 1)
                            ve.sem_inc(tick, 1)
                        nc.vector.tensor_tensor(mine, mine, ps[(s + j) % banks][:, 0:out_width], ALU.add).then_inc(added, 1)

                nc.vector.memset(blank[:, :], 0.0).then_inc(cleared, 1)
                for part in sums:
                    nc.vector.memset(part[:, :], 0.0)
                if ahead:
                    ahead.add_biases(ve)
                ve.drain()
                ve.sem_inc(added, banks)
                with ve.Fori(0, turns) as i:
                    tiles = tiles_of(nc, nc.vector.engine, e, i, SLOTS)
                    for s in range(0, SLOTS, 2):
                        add_pair(SLOTS * i + s, s, tiles[s:s + 2])
                for part in sums[1:]:
                    ve.wait_ge(added, banks + Q)
                    nc.vector.tensor_tensor(acc[:, :], acc[:, :], part[:, :], ALU.add).then_inc(joined, 1)
                    ve.wait_ge(joined, 1)


class MeanInputs:

    def __init__(self, nc, m, a, x, z_d):
        self.nc, self.a, self.x, self.z_d = nc, a, x, z_d
        self.z = m.sb("z", [P, NT, D])
        self.w = m.sb("w", [P, 2 * KD, D])
        self.bias = m.sb("bias", [P, 2, D])
        self.biases_in, self.loaded = m.sem("biases_in"), m.sem("loaded")

    def load(self, sp):
        for j, name in enumerate(("L0_gnn_b1", "L0_gnn_b2")):
            sp.dma_start(self.bias[:, j, :], self.a[name].partition_broadcast(P)).then_inc(self.biases_in, 16)
        for j, name in enumerate(("L0_gnn_W1", "L0_gnn_W2")):
            sp.dma_start(self.w[:, j * KD:(j + 1) * KD, :], self.a[name].rearrange("(k p) o -> p k o", p=P)).then_inc(self.loaded, 16)
        sp.dma_start(self.z[:, :, :], rows(self.z_d, 0, NT)).then_inc(self.loaded, 16)

    def add_biases(self, ve):
        nc, x = self.nc, self.x
        ve.wait_ge(self.biases_in, 32)
        nc.vector.tensor_tensor(self.bias[:, 0, :], self.bias[:, 0, :], self.bias[:, 1, :], ALU.add)
        ve.drain()
        nc.vector.tensor_tensor(x[:, :, :], x[:, :, :], self.bias[:, 0, :].unsqueeze(1).to_broadcast([P, NT, D]), ALU.add)


def mean_layer(nc, c, e, x, inputs, acc):
    with Names(nc, "mean") as m:
        per = m.sb("per", [P, NT])
        project = Project(m, 2 * KD, D)
        end = m.sem("end")
        with nc.Block() as block:
            @block.vector
            def _(ve):
                nc.vector.tensor_scalar(per[:, :], e["degree"][:, :], 1.0, None, ALU.max)
                ve.drain()
                nc.vector.reciprocal(per[:, :], per[:, :])
                ve.drain()

                def use(t, out):
                    mine = x[:, bass.ds(t, 1), :].rearrange("p t d -> p (t d)")
                    return nc.vector.tensor_tensor(mine, mine, out, ALU.add)
                def bring(t, place):
                    nc.vector.tensor_copy(place[:, 0:D], tile_of(inputs.z, t))
                    return nc.vector.tensor_scalar(place[:, D:2 * D], acc[:, bass.ds(t * HROW, D)], per[:, bass.ds(t, 1)], None, ALU.mult)
                ve.wait_ge(inputs.loaded, 48)
                ve.sem_inc(end, 1)
                project.vector(ve, bring, use)
                ve.drain().then_inc(end, 1)

            @block.scalar
            def _(act):
                project.scalar(nc, act)

            @block.tensor
            def _(pe):
                pe.wait_ge(inputs.loaded, 48)
                project.tensor(nc, pe, c["ident"][:, :], lambda j: inputs.w[:, j, :])


def route(nc, layer, c, a, x, r, w, gate, gate_bias, z_d, xs_d, again):
    EX, NB, H, tag = layer["experts"], layer["blocks"], layer["hidden"], layer["name"]
    low = f"{tag}_ffn_W" if tag == "L0" else f"{tag}_ffn_w"
    with Names(nc, f"route{tag}") as m:
        z = m.sb("z", [P, NT, D])
        norm = Norm(m, "ln")
        again_scale = m.sb("again_scale", [P, NT])
        again_root = m.sb("again_root", [P, NT])
        places = m.sb("places", [P, FEW, XROW])
        tags = m.sb("tags", [P, NT, TAGS])
        pos = m.sb("pos", [P, NT, TOP], I32)
        gate_w = m.sb("gate_w", [P, KD, EX])
        gate_b = m.sb("gate_b", [P, EX])
        logits = m.sb("logits", [P, NT, EX])
        rank = m.sb("rank", [P, EX])
        valid = m.sb("valid", [P, NT])
        best = m.sb("best", [P, TOP, NT])
        first = m.sb("first", [P, NT])
        taken = m.sb("taken", [P, NT, EX])
        hot = m.sb("hot", [P, TOP, NT, EX], BF16)
        before = m.sb("before", [P, TOP, NT, EX], BF16)
        column = m.sb("column", [P, 1 + TOP * NT, EX])
        size_i = m.sb("size_i", [P, EX], I32)
        size_f = m.sb("size_f", [P, EX])
        ends = m.sb("ends", [P, EX])
        base = m.sb("base", [P, EX])
        zeros = m.sb("zeros", [P, TOP * NT])
        owner_f = m.sb("owner_f", [1, NB])
        pos_f = m.sb("pos_f", [P, TOP, NT])
        index = m.sb("index", [P, FEW, TOP], I32)
        project = Project(m, KD, EX, places)
        before_ps = [m.ps(f"before_ps{k}") for k in range(2)]
        total_ps = [m.ps(f"total_ps{k}") for k in range(2)]
        loaded, normed, var_again, rooted_again = (m.sem(n) for n in ("loaded", "normed", "var_again", "rooted_again"))
        tables, hot_ready, summed, spread, away, pos_ready = m.sem("tables"), m.sem("hot_ready"), m.sem("summed"), m.sem("spread"), m.sem("away"), m.sem("pos_ready")
        place_ready, sent = m.sem("place_ready"), [m.gather_sem(f"sent{s}") for s in range(FEW)]
        kept, tick = m.sem("kept"), m.sem("tick")
        with nc.Block() as block:
            @block.sync
            def _(sp):
                sp.dma_start(gate_w[:, :, :], gate.rearrange("(k p) e -> p k e", p=P)).then_inc(loaded, 16)
                sp.dma_start(gate_b[:, :], gate_bias.partition_broadcast(P)).then_inc(loaded, 16)
                for ex in range(EX):
                    sp.dma_start(w["first"][:, ex * KD * H:(ex + 1) * KD * H].rearrange("p (k h) -> p k h", h=H),
                                 a[low + "1"][ex].rearrange("(k p) h -> p k h", p=P)).then_inc(w["landed"], 16)
                    sp.dma_start(w["second"][:, ex * H // P * D:(ex + 1) * H // P * D].rearrange("p (k d) -> p k d", d=D),
                                 a[low + "2"][ex].rearrange("(k p) d -> p k d", p=P)).then_inc(w["landed"], 16)
                if z_d is not None:
                    sp.wait_ge(normed, 2)
                    sp.dma_start(rows(z_d, 0, NT), z[:, :, :]).then_inc(kept, 16)
                    sp.wait_ge(kept, 16)

            @block.scalar
            def _(act):
                norm.scalar(nc, act, x, z, normed)
                project.scalar(nc, act)
                if again:
                    act.wait_ge(var_again, 1)
                    nc.scalar.activation(again_root[:, :], again_scale[:, :], ACT.Sqrt).then_inc(rooted_again, 1)
                act.wait_ge(spread, 1)
                nc.scalar.activation(r["weight"][:, 1, :], first[:, :], ACT.Exp).then_inc(away, 1)

            @block.tensor
            def _(pe):
                pe.wait_ge(loaded, 32)
                project.tensor(nc, pe, c["ident"][:, :], lambda j: gate_w[:, j, :])
                pe.wait_ge(hot_ready, 1)
                for k in range(TOP):
                    chosen = hot[:, k, :, :].rearrange("p t e -> p (t e)")
                    nc.tensor.matmul(before_ps[k][:, 0:NT * EX], c["before_b"][:, :], chosen, start=True, stop=True)
                    last = nc.tensor.matmul(total_ps[k][:, 0:NT * EX], c["ones_b"][:, :], chosen, start=True, stop=True)
                last.then_inc(summed, 1)

            @block.vector
            def _(ve):
                nc.vector.memset(zeros[:, :], 0.0)
                norm.vector(nc, ve, x, z, normed)
                if again:
                    nc.vector.tensor_tensor(again_scale[:, :], norm.raw[:, :], norm.scale[:, :], ALU.mult)
                    ve.drain()
                    nc.vector.tensor_tensor(again_scale[:, :], again_scale[:, :], norm.scale[:, :], ALU.mult)
                    ve.drain()
                    nc.vector.tensor_scalar(again_scale[:, :], again_scale[:, :], 1e-5, None, ALU.add).then_inc(var_again, 1)

                def use(t, out):
                    return nc.vector.tensor_tensor(logits[:, bass.ds(t, 1), :].rearrange("p t e -> p (t e)"), out, gate_b[:, :], ALU.add)
                project.vector(ve, None, use)
                ve.wait_ge(tables, 2)
                nc.vector.tensor_scalar(rank[:, :], c["count_f"][:, 0:EX], -1.0, float(EX), ALU.mult, ALU.add)
                ve.drain()
                for k in range(TOP):
                    shape = [P, NT, EX]
                    mine = hot[:, k, :, :]
                    nc.vector.tensor_reduce(best[:, k, :], logits[:, :, :], AX, ALU.max)
                    ve.drain()
                    nc.vector.tensor_tensor(taken[:, :, :], logits[:, :, :], best[:, k, :].unsqueeze(2).to_broadcast(shape), ALU.is_equal)
                    ve.drain()
                    nc.vector.tensor_tensor(taken[:, :, :], taken[:, :, :], rank[:, :].unsqueeze(1).to_broadcast(shape), ALU.mult)
                    ve.drain()
                    nc.vector.tensor_reduce(first[:, :], taken[:, :, :], AX, ALU.max)
                    ve.drain()
                    nc.vector.tensor_tensor(mine, rank[:, :].unsqueeze(1).to_broadcast(shape), first[:, :].unsqueeze(2).to_broadcast(shape), ALU.is_equal)
                    ve.drain()
                    nc.vector.scalar_tensor_tensor(logits[:, :, :], mine, NEG, logits[:, :, :], ALU.mult, ALU.add)
                    ve.drain()
                    nc.vector.tensor_tensor(mine, mine, valid[:, :].unsqueeze(2).to_broadcast(shape), ALU.mult)
                    ve.drain()
                nc.vector.tensor_tensor(first[:, :], best[:, 1, :], best[:, 0, :], ALU.subtract).then_inc(spread, 1)
                nc.vector.memset(column[:, 0, :], 0.0).then_inc(hot_ready, 1)
                ve.wait_ge(away, 1)
                nc.vector.tensor_scalar(first[:, :], r["weight"][:, 1, :], 1.0, None, ALU.add)
                ve.drain()
                nc.vector.reciprocal(r["weight"][:, 0, :], first[:, :])
                ve.drain()
                nc.vector.tensor_tensor(r["weight"][:, 1, :], r["weight"][:, 1, :], r["weight"][:, 0, :], ALU.mult)
                ve.wait_ge(summed, 1)
                for k in range(TOP):
                    nc.vector.tensor_copy(before[:, k, :, :].rearrange("p t e -> p (t e)"), before_ps[k][:, 0:NT * EX])
                    nc.vector.tensor_copy(column[:, 1 + k * NT:1 + (k + 1) * NT, :].rearrange("p t e -> p (t e)"), total_ps[k][:, 0:NT * EX])
                ve.drain()
                for ex in range(EX):
                    totals = column[:, 1:, ex]
                    nc.vector.tensor_tensor_scan(totals, zeros[:, :], totals, 0.0, ALU.add, ALU.add)
                ve.drain()
                prior = column[:, 0:TOP * NT, :]
                nc.vector.tensor_scalar(size_i[:, :], column[:, TOP * NT, :], float(P - 1), None, ALU.add)
                ve.drain()
                nc.vector.tensor_scalar(size_i[:, :], size_i[:, :], 7, None, ALU.arith_shift_right)
                ve.drain()
                nc.vector.tensor_copy(size_f[:, :], size_i[:, :])
                ve.drain()
                nc.vector.tensor_tensor_scan(ends[:, :], zeros[:, 0:EX], size_f[:, :], 0.0, ALU.add, ALU.add)
                ve.drain()
                nc.vector.tensor_tensor(base[:, :], ends[:, :], size_f[:, :], ALU.subtract)
                ve.drain()
                nc.vector.tensor_scalar(base[:, :], base[:, :], float(P), None, ALU.mult)
                ve.drain()
                flat = [P, TOP * NT, EX]
                before_v = before[:, :, :, :].rearrange("p k t e -> p (k t) e")
                nc.vector.tensor_tensor(prior, prior, before_v, ALU.add)
                ve.drain()
                nc.vector.tensor_tensor(prior, prior, base[:, :].unsqueeze(1).to_broadcast(flat), ALU.add)
                ve.drain()
                nc.vector.tensor_tensor(prior, prior, hot[:, :, :, :].rearrange("p k t e -> p (k t) e"), ALU.mult)
                ve.drain()
                nc.vector.tensor_reduce(pos_f[:, :, :].rearrange("p k t -> p (k t)"), prior, AX, ALU.add)
                ve.drain()
                nc.vector.tensor_copy(tags[:, :, 1], pos_f[:, 1, :])
                nc.vector.tensor_scalar(tags[:, :, 0], c["count_f"][:, 0:NT], float(P), c["lane_f"][:, 0:1], ALU.mult, ALU.add)
                ve.drain()
                nc.vector.tensor_scalar(tags[:, :, 0], tags[:, :, 0], float(TOP), float(TOP), ALU.mult, ALU.add)
                nc.vector.tensor_copy(pos[:, :, :], pos_f[:, :, :].rearrange("p k t -> p t k")).then_inc(pos_ready, 1)
                if again:
                    ve.wait_ge(rooted_again, 1)
                    nc.vector.reciprocal(again_scale[:, :], again_root[:, :])
                ve.wait_ge(pos_ready, 1)
                ve.drain()

                def bring(t, s):
                    nc.vector.tensor_copy(index[:, s, :], pos[:, bass.ds(t, 1), :].rearrange("p t k -> p (t k)"))
                    nc.vector.tensor_copy(places[:, s, D:XROW], tags[:, bass.ds(t, 1), :].rearrange("p t k -> p (t k)"))
                    if again:
                        op = nc.vector.tensor_scalar(places[:, s, 0:D], tile_of(z, t), again_scale[:, bass.ds(t, 1)], None, ALU.mult)
                    else:
                        op = nc.vector.tensor_copy(places[:, s, 0:D], tile_of(z, t))
                    op.then_inc(place_ready, 1)
                for s in range(FEW):
                    bring(s, s)
                nc.vector.memset(owner_f[:, :], 0.0)
                ve.drain()
                for ex in range(EX):
                    nc.vector.scalar_tensor_tensor(owner_f[:, :], c["count_f"][0:1, 0:NB], ends[0:1, ex:ex + 1], owner_f[:, :], ALU.is_ge, ALU.add)
                    ve.drain()
                nc.vector.tensor_scalar(r["owner"][:, 0:NB], owner_f[:, :], float(EX - 1), None, ALU.min)
                with ve.Fori(1, NT // FEW) as i:
                    for s in range(FEW):
                        ve.wait_ge(sent[s], 32 * i)
                        ve.sem_inc(tick, 1)
                        bring(FEW * i + s, s)
                ve.wait_ge(sent[0], 32 * (NT // FEW))
                bring(NT - 1, 0)
                ve.wait_ge(place_ready, NT)

            @block.gpsimd
            def _(pool):
                nc.gpsimd.memset(valid[:, :], 1.0).then_inc(tables, 1)
                pool.wait_ge(tables, 1)
                nc.gpsimd.affine_select(out=valid[:, :], in_=valid[:, :], compare_op=ALU.is_gt, fill=0.0, base=N,
                                        pattern=[[-P, NT]], channel_multiplier=-1).then_inc(tables, 1)
                pool.wait_ge(normed, 2)
                pool.sem_inc(tick, 1)
                project.pool(pool, lambda t, place: nc.gpsimd.tensor_copy(place, tile_of(z, t)))

                def send(s, n):
                    for k in range(TOP):
                        pool.indirect_dma_start(out=xs_d[:, :], out_offset=bass.IndirectOffsetOnAxis(ap=index[0:n, s, k:k + 1], axis=0),
                                                in_=places[0:n, s, :], in_offset=None).then_inc(sent[s], 16)
                with pool.Fori(0, NT // FEW) as i:
                    for s in range(FEW):
                        pool.wait_ge(place_ready, FEW * i + s + 1)
                        pool.sem_inc(tick, 1)
                        send(s, P)
                pool.wait_ge(place_ready, NT)
                pool.sem_inc(tick, 1)
                send(0, TAIL)
                for s in range(FEW):
                    pool.wait_ge(sent[s], 32 * (NT // FEW + (1 if s == 0 else 0)))


def experts(nc, layer, c, a, r, w, xs_d, ys_d):
    EX, NB, H, tag = layer["experts"], layer["blocks"], layer["hidden"], layer["name"]
    HC = H // P
    scaled = tag == "L0"
    func = ACT.Gelu if scaled else ACT.Relu
    w1_all, w2_sb, b1, b2 = w["first"], w["second"], a[f"{tag}_ffn_b1"], a[f"{tag}_ffn_b2"]
    with Names(nc, f"experts{tag}") as m:
        w1_sb = m.sb("w1", [P, 2, KD * H])
        b1_sb = m.sb("b1", [P, EX * HC])
        b2_sb = m.sb("b2", [P, EX * D])
        ln = m.sb("ln", [P, 2, EX * KD]) if scaled else None
        xb = m.sb("xb", [P, 2, XROW])
        slot = m.sb("slot", [P, NB])
        result = m.sb("result", [P, NB], I32)
        index = m.sb("index", [P, 2], I32)
        xT = m.sb("xT", [P, 2, KD, P])
        hT = m.sb("hT", [P, 2, HC, P])
        yb = m.sb("yb", [P, 2, D])
        banks = HC // 4
        turn_ps = [m.ps(f"turn_ps{s}") for s in range(2)]
        hid_ps = [[m.ps(f"hid_ps{s}{q}") for q in range(banks)] for s in range(2)]
        out_ps = [m.ps(f"out_ps{s}") for s in range(2)]
        w_in = m.sem("w_in")
        w1_ready = m.sem("w1_ready")
        x_in = [m.sem(f"x_in{s}") for s in range(2)]
        y_out = [m.gather_sem(f"y_out{s}") for s in range(2)]
        turned, addressed, ready, hidden, acted, product, done = (m.sem(n) for n in ("turned", "addressed", "ready", "hidden", "acted", "product", "done"))
        placed, tick = m.sem("placed"), m.sem("tick")
        loads = 16 * (2 + (2 if scaled else 0))
        with nc.Block() as block:
            @block.sync
            def _(sp):
                sp.dma_start(b1_sb[:, :], b1.rearrange("p e c -> p (e c)")).then_inc(w_in, 16)
                sp.dma_start(b2_sb[:, :], b2.rearrange("e d -> (e d)").partition_broadcast(P)).then_inc(w_in, 16)
                if scaled:
                    for j, name in enumerate(("L0_ffn_ln_g", "L0_ffn_ln_b")):
                        sp.dma_start(ln[:, j, :], a[name].rearrange("p e k -> p (e k)")).then_inc(w_in, 16)
                sp.sem_inc(turned, 2)
                sp.sem_inc(addressed, 2)
                with sp.Fori(0, NB // 2) as i:
                    for s in range(2):
                        b = 2 * i + s
                        sp.wait_ge(turned, b + 1)
                        sp.wait_ge(addressed, b + 1)
                        sp.dma_start(xb[:, s, :], xs_d[bass.ds(b * P, P), :]).then_inc(x_in[s], 16)

            @block.gpsimd
            def _(pool):
                def send(b, s, count):
                    pool.wait_ge(placed, b + 1)
                    pool.wait_ge(done, 2 + b + 1)
                    if count is not None:
                        pool.wait_ge(y_out[1 - s], 16 * count)
                    pool.sem_inc(tick, 1)
                    pool.indirect_dma_start(out=ys_d[:, :], out_offset=bass.IndirectOffsetOnAxis(ap=index[:, s:s + 1], axis=0),
                                            in_=yb[:, s, :], in_offset=None).then_inc(y_out[s], 16)
                send(0, 0, None)
                send(1, 1, 1)
                with pool.Fori(1, NB // 2) as i:
                    for s in range(2):
                        send(2 * i + s, s, i + s)
                for s in range(2):
                    pool.wait_ge(y_out[s], 16 * (NB // 2))

            @block.tensor
            def _(pe):
                def turn(b, s, count):
                    pe.wait_ge(x_in[s], 16 * count)
                    pe.wait_ge(ready, b + 1)
                    pe.sem_inc(tick, 1)
                    for k in range(KD):
                        last = nc.tensor.transpose(turn_ps[s][:, k * P:(k + 1) * P], xb[:, s, k * P:(k + 1) * P], c["ident"][:, :])
                    last.then_inc(turned, 1)

                def hide(b, s):
                    pe.wait_ge(w1_ready, b + 1)
                    pe.wait_ge(ready, 2 + b + 1)
                    pe.wait_ge(acted, (b + 1) * banks)
                    pe.sem_inc(tick, 1)
                    for hc in range(HC):
                        for k in range(KD):
                            last = nc.tensor.matmul(hid_ps[s][hc // 4][:, hc % 4 * P:(hc % 4 + 1) * P],
                                                    w1_sb[:, s, k * H + hc * P:k * H + (hc + 1) * P],
                                                    xT[:, s, k, :], start=(k == 0), stop=(k == KD - 1))
                        if hc % 4 == 3:
                            last.then_inc(hidden, 1)

                def finish(b, s):
                    ex = pe.value_load(r["owner"][0:1, bass.ds(b, 1)], min_val=0, max_val=EX - 1)
                    pe.wait_ge(acted, (2 + b + 1) * banks)
                    pe.wait_ge(done, b + 1)
                    pe.sem_inc(tick, 1)
                    for hc in range(HC):
                        last = nc.tensor.matmul(out_ps[s][:, 0:D], hT[:, s, hc, :], w2_sb[:, bass.ds(ex * (HC * D) + hc * D, D)],
                                                start=(hc == 0), stop=(hc == HC - 1))
                    last.then_inc(product, 1)

                pe.sem_inc(product, 2)
                pe.wait_ge(w["landed"], 16 * 2 * EX)
                turn(0, 0, 1)
                turn(1, 1, 1)
                hide(0, 0)
                with pe.Fori(0, (NB - 2) // 2) as i:
                    for s in range(2):
                        b = 2 * i + s + 1
                        turn(b + 1, s, i + 2)
                        hide(b, 1 - s)
                        finish(b - 1, s)
                hide(NB - 1, 1)
                finish(NB - 2, 0)
                finish(NB - 1, 1)

            @block.scalar
            def _(act):
                act.sem_inc(acted, 2 * banks)
                act.wait_ge(w_in, loads)
                with act.Fori(0, NB // 2) as i:
                    for s in range(2):
                        b = 2 * i + s
                        ex = act.value_load(r["owner"][0:1, bass.ds(b, 1)], min_val=0, max_val=EX - 1)
                        act.wait_ge(product, b + 1)
                        act.sem_inc(tick, 1)
                        for q in range(banks):
                            act.wait_ge(hidden, b * banks + q + 1)
                            act.sem_inc(tick, 1)
                            for j in range(4):
                                hc = 4 * q + j
                                last = nc.scalar.activation(hT[:, s, hc, :], hid_ps[s][q][:, j * P:(j + 1) * P], func,
                                                            bias=b1_sb[:, bass.ds(ex * HC + hc, 1)])
                            last.then_inc(acted, 1)

            @block.vector
            def _(ve):
                def scale(b, s, lagging):
                    ve.wait_ge(turned, 2 + b + 1)
                    if lagging:
                        ve.wait_ge(hidden, (b - 1) * banks)
                    ve.sem_inc(tick, 1)
                    ex = ve.value_load(r["owner"][0:1, bass.ds(b, 1)], min_val=0, max_val=EX - 1)
                    nc.vector.scalar_tensor_tensor(result[:, bass.ds(b, 1)], xb[:, s, D + 1:D + 2], slot[:, bass.ds(b, 1)], xb[:, s, D:D + 1],
                                                   ALU.is_equal, ALU.add).then_inc(addressed, 1)
                    nc.vector.tensor_copy(w1_sb[:, s, :], w1_all[:, bass.ds(ex * (KD * H), KD * H)]).then_inc(w1_ready, 1)
                    if not scaled:
                        nc.vector.tensor_copy(xT[:, s, :, :].rearrange("p k t -> p (k t)"), turn_ps[s][:, 0:D]).then_inc(ready, 1)
                        return
                    for k in range(KD):
                        last = nc.vector.tensor_scalar(xT[:, s, k, :], turn_ps[s][:, k * P:(k + 1) * P], ln[:, 0, bass.ds(ex * KD + k, 1)],
                                                       ln[:, 1, bass.ds(ex * KD + k, 1)], ALU.mult, ALU.add)
                    last.then_inc(ready, 1)

                def shift(b, s, count):
                    ex = ve.value_load(r["owner"][0:1, bass.ds(b, 1)], min_val=0, max_val=EX - 1)
                    ve.wait_ge(product, 2 + b + 1)
                    ve.wait_ge(addressed, 2 + b + 1)
                    if count is not None:
                        ve.wait_ge(y_out[s], 16 * count)
                    ve.sem_inc(tick, 1)
                    nc.vector.tensor_copy(index[:, s:s + 1], result[:, bass.ds(b, 1)]).then_inc(placed, 1)
                    nc.vector.tensor_tensor(yb[:, s, :], out_ps[s][:, 0:D], b2_sb[:, bass.ds(ex * D, D)], ALU.add).then_inc(done, 1)

                nc.vector.tensor_scalar(slot[:, :], c["count_f"][:, 0:NB], float(P), c["lane_f"][:, 0:1], ALU.mult, ALU.add)
                ve.drain()
                ve.sem_inc(ready, 2)
                ve.sem_inc(done, 2)
                ve.wait_ge(w_in, loads)
                ve.wait_ge(w["landed"], 16 * 2 * EX)
                scale(0, 0, False)
                scale(1, 1, False)
                scale(2, 0, True)
                shift(0, 0, None)
                scale(3, 1, True)
                shift(1, 1, None)
                with ve.Fori(1, NB // 2 - 1) as i:
                    for s in range(2):
                        scale(2 * i + s + 2, s, True)
                        shift(2 * i + s, s, i)
                for s in range(2):
                    shift(NB - 2 + s, s, NB // 2 - 1)


def combine(nc, layer, r, ys_d, target, after):
    tag = layer["name"]
    with Names(nc, f"combine{tag}") as m:
        ys = m.sb("ys", [P, FEW, TOP, D])
        first, used, end, tick = m.sem("first"), m.sem("used"), m.sem("end"), m.sem("tick")
        landed = [m.sem(f"landed{s}") for s in range(FEW)]
        extra = after(m) if after else None
        with nc.Block() as block:
            @block.sync
            def _(sp):
                if extra:
                    extra.load(sp)

                def fetch(t, s, n):
                    sp.wait_ge(used, t + 1)
                    sp.dma_start(ys[0:n, s, :, :].rearrange("p k d -> p (k d)"),
                                 ys_d[bass.ds(TOP * (P * t + 1), TOP * n), :].rearrange("(p k) d -> p (k d)", k=TOP)).then_inc(landed[s], 16)
                with sp.Fori(0, NT // FEW) as i:
                    for s in range(FEW):
                        fetch(FEW * i + s, s, P)
                fetch(NT - 1, 0, TAIL)
                if extra:
                    extra.store(sp)

            @block.vector
            def _(ve):
                ve.sem_inc(used, FEW)
                if extra:
                    extra.before(ve)

                def add(k, t, s, n, signal):
                    mine = target[0:n, bass.ds(t, 1), :].rearrange("p t d -> p (t d)")
                    nc.vector.scalar_tensor_tensor(mine, ys[0:n, s, k, :], r["weight"][0:n, k, bass.ds(t, 1)], mine, ALU.mult, ALU.add).then_inc(signal, 1)

                def some(t, places, n, turn):
                    tiles = [(t + j, s) for j, s in enumerate(places)]
                    for mine, s in tiles:
                        ve.wait_ge(landed[s], turn)
                        ve.sem_inc(tick, 1)
                        add(0, mine, s, n, first)
                    for mine, s in tiles:
                        ve.wait_ge(first, mine + 1)
                        ve.sem_inc(tick, 1)
                        add(1, mine, s, n, used)
                    if extra:
                        for mine, s in tiles:
                            ve.wait_ge(used, FEW + mine + 1)
                            ve.sem_inc(tick, 1)
                            extra.each(mine)
                with ve.Fori(0, NT // FEW) as i:
                    for s in range(0, FEW, 2):
                        some(FEW * i + s, (s, s + 1), P, 16 * i + 16)
                some(NT - 1, (0,), TAIL, 16 * (NT // FEW) + 16)
                ve.drain()
                if extra:
                    extra.vector(ve)
                ve.drain().then_inc(end, 1)

            if extra:
                extra.rest(block)


class Finish:
    GROUP = 5

    def __init__(self, nc, m, a, x, z, z_d, out):
        self.nc, self.a, self.x, self.z, self.z_d, self.out = nc, a, x, z, z_d, out
        self.affine = m.sb("affine", [P, 2, D])
        self.norm = Norm(m, "ln")
        self.affine_in, self.started = m.sem("affine_in"), m.sem("started")
        self.loaded, self.normed, self.total, self.stored = m.sem("loaded"), m.sem("normed"), m.sem("total"), m.sem("stored")
        self.groups = [slice(g, g + self.GROUP) for g in range(0, NT, self.GROUP)]

    def before(self, ve):
        nc, x = self.nc, self.x
        ve.wait_ge(self.affine_in, 32)
        nc.vector.tensor_tensor(x[:, :, :], x[:, :, :], self.affine[:, 1, :].unsqueeze(1).to_broadcast([P, NT, D]), ALU.add)
        ve.wait_ge(self.loaded, 16)
        ve.sem_inc(self.started, 1)

    def each(self, t):
        self.norm.count(self.nc, self.z, t)

    def vector(self, ve):
        nc, x, z = self.nc, self.x, self.z
        self.norm.moments(nc, ve)
        for n, tiles in enumerate(self.groups):
            ve.wait_ge(self.normed, n + 1)
            nc.vector.tensor_tensor(z[:, tiles, :], z[:, tiles, :], self.affine[:, 0, :].unsqueeze(1).to_broadcast([P, self.GROUP, D]), ALU.mult)
            ve.drain()
            nc.vector.tensor_tensor(x[:, tiles, :], x[:, tiles, :], z[:, tiles, :], ALU.add).then_inc(self.total, 1)

    def rest(self, block):
        nc, z = self.nc, self.z

        @block.scalar
        def _(act):
            self.norm.root_of_var(nc, act)
            for tiles in self.groups:
                for t in range(tiles.start, tiles.stop):
                    last = self.norm.write(nc, z, z, t)
                last.then_inc(self.normed, 1)

    def load(self, sp):
        for j, name in enumerate(("L1_ffn_gamma", "L1_ffn_beta")):
            sp.dma_start(self.affine[:, j, :], self.a[name].partition_broadcast(P)).then_inc(self.affine_in, 16)
        sp.dma_start(self.z[:, :, :], rows(self.z_d, 0, NT)).then_inc(self.loaded, 16)

    def store(self, sp):
        for n, tiles in enumerate(self.groups):
            sp.wait_ge(self.total, n + 1)
            full = min(tiles.stop, NT - 1)
            sp.dma_start(rows(self.out, tiles.start, full), self.x[:, tiles.start:full, :]).then_inc(self.stored, 16)
        sp.dma_start(self.out[(NT - 1) * P:N, :], self.x[0:TAIL, NT - 1, :]).then_inc(self.stored, 16)
        sp.wait_ge(self.stored, 16 * (len(self.groups) + 1))


def heads(nc, c, a, x, split, h_d, coef):
    G = 5
    WIDTH = HROW + HEADS
    with Names(nc, "heads") as m:
        z = m.sb("z", [P, NT, D])
        norm = Norm(m, "ln")
        w = m.sb("w", [P, KD, WIDTH])
        scaled = m.sb("scaled", [P, 2, KD, D])
        att = m.sb("att", [P, HEADS, 5, HD])
        ends = m.sb("ends", [P, 3, D])
        line = m.sb("line", [1, 2, KD, HEADS, HPART])
        row = m.sb("row", [P, NT, WIDTH])
        rest = m.sb("rest", [P, 2, G, D])
        work = m.sb("work", [P, 2, G, D])
        square = m.sb("square", [P, NT, HEADS])
        term = m.sb("term", [P, 3, NT, HEADS])
        coef_ps = m.ps("coef_ps")
        project = Project(m, KD, WIDTH)
        line_ready, turned = m.sem("line_ready"), m.sem("turned")
        loaded, normed, tick, w_ready, rounded, left, row_ready, stored = (
            m.sem(n) for n in ("loaded", "normed", "tick", "w_ready", "rounded", "left", "row_ready", "stored"))
        groups = [slice(g, g + G) for g in range(0, NT, G)]
        ALONE = 3

        def by_head(ap):
            return ap.rearrange("p (h d) -> p h d", d=HD)

        with nc.Block() as block:
            @block.sync
            def _(sp):
                sp.dma_start(w[:, :, 0:D], a["L1_gnn_W"].rearrange("(k p) o -> p k o", p=P)).then_inc(loaded, 16)
                sp.dma_start(att[:, :, :, :].rearrange("p h f d -> p (h f d)"), a["L1_gnn_a"].rearrange("h f -> (h f)").partition_broadcast(P)).then_inc(loaded, 16)
                for n, tiles in enumerate(groups):
                    sp.wait_ge(row_ready, n + 1)
                    sp.dma_start(rows(h_d, tiles.start, tiles.stop), row[:, tiles, 0:HROW]).then_inc(stored, 16)
                sp.wait_ge(stored, 16 * len(groups))

            @block.gpsimd
            def _(pool):
                pool.wait_ge(normed, 2)
                pool.sem_inc(tick, 1)
                project.pool(pool, lambda t, place: nc.gpsimd.tensor_copy(place, tile_of(z, t)))

            @block.scalar
            def _(act):
                norm.scalar(nc, act, x, z, normed)
                project.scalar(nc, act, lambda t: tile_of(row, t))
                for n, tiles in enumerate(groups[ALONE:]):
                    act.wait_ge(project.used, 2 + tiles.stop)
                    nc.scalar.activation(split[:, tiles, 0, 0:D], row[:, tiles, 0:D], ACT.Copy).then_inc(rounded, 1)
                    for part in range(2):
                        act.wait_ge(left, 2 * n + part + 1)
                        nc.scalar.activation(split[:, tiles, 1 + part, 0:D], rest[:, part, :, :], ACT.Copy).then_inc(rounded, 1)

            @block.tensor
            def _(pe):
                pe.wait_ge(line_ready, 1)
                flat = line[:, :, :, :, :].rearrange("p j f h d -> p (j f h d)")
                for j in range(2 * KD):
                    last = nc.tensor.transpose(coef_ps[:, j:j + 1], flat[:, j * P:(j + 1) * P], c["ident"][0:1, 0:1])
                last.then_inc(turned, 1)
                pe.wait_ge(w_ready, 1)
                project.tensor(nc, pe, c["ident"][:, :], lambda j: w[:, j, :])

            @block.vector
            def _(ve):
                norm.vector(nc, ve, x, z, normed)
                ve.wait_ge(loaded, 32)
                nc.vector.tensor_tensor(by_head(ends[:, 0, :]), att[:, :, 1, :], att[:, :, 2, :], ALU.add)
                nc.vector.tensor_tensor(by_head(ends[:, 1, :]), att[:, :, 0, :], att[:, :, 2, :], ALU.subtract)
                nc.vector.tensor_scalar(by_head(ends[:, 2, :]), att[:, :, 4, :], 0.5, None, ALU.mult)
                for j, scale in enumerate((1.0, -0.5)):
                    for f in range(KD):
                        last = nc.vector.tensor_scalar(line[:, j, f, :, :], att[0:1, :, 3 + j, f:HD:KD], scale, None, ALU.mult)
                last.then_inc(line_ready, 1)
                ve.drain()
                for j in range(2):
                    nc.vector.tensor_tensor(scaled[:, j, :, :], w[:, :, 0:D], ends[:, j, :].unsqueeze(1).to_broadcast([P, KD, D]), ALU.mult)
                ve.drain()
                for j in range(2):
                    last = nc.vector.tensor_reduce(w[:, :, D + j * HEADS:D + (j + 1) * HEADS], scaled[:, j, :, :].rearrange("p k (h d) -> p k h d", d=HD), AX, ALU.add)
                last.then_inc(w_ready, 1)
                ve.wait_ge(turned, 1)
                nc.vector.tensor_copy(coef[:, :, :].rearrange("p j f -> p (j f)"), coef_ps[:, 0:2 * KD])
                half = ends[:, 2, :].unsqueeze(1).to_broadcast([P, G, D])
                def rounded_part(n, tiles, part):
                    if n >= ALONE:
                        ve.wait_ge(rounded, 3 * (n - ALONE) + part + 1)
                        return
                    source = row[:, tiles, 0:D] if part == 0 else rest[:, part - 1, :, :]
                    nc.vector.tensor_copy(split[:, tiles, part, 0:D], source)
                    ve.drain()

                for n, tiles in enumerate(groups):
                    mine = row[:, tiles, 0:D]
                    ve.wait_ge(project.used, 2 + tiles.stop)
                    nc.vector.tensor_tensor(work[:, 0, :, :], mine, half, ALU.mult)
                    rounded_part(n, tiles, 0)
                    op = nc.vector.tensor_tensor(rest[:, 0, :, :], mine, split[:, tiles, 0, 0:D], ALU.subtract)
                    if n >= ALONE:
                        op.then_inc(left, 1)
                    ve.drain()
                    nc.vector.tensor_tensor(work[:, 1, :, :], work[:, 0, :, :], mine, ALU.mult)
                    rounded_part(n, tiles, 1)
                    op = nc.vector.tensor_tensor(rest[:, 1, :, :], rest[:, 0, :, :], split[:, tiles, 1, 0:D], ALU.subtract)
                    if n >= ALONE:
                        op.then_inc(left, 1)
                    ve.drain()
                    nc.vector.tensor_reduce(square[:, tiles, :], work[:, 1, :, :].rearrange("p t (h d) -> p t h d", d=HD), AX, ALU.add)
                    ve.drain()
                    nc.vector.tensor_tensor(row[:, tiles, D:HROW], row[:, tiles, D:HROW], square[:, tiles, :], ALU.add).then_inc(row_ready, 1)
                    rounded_part(n, tiles, 2)
                nc.vector.scalar_tensor_tensor(term[:, 0, :, :], row[:, :, HROW:WIDTH], -1.0, square[:, :, :], ALU.mult, ALU.subtract)
                ve.drain()
                for part in range(3):
                    nc.vector.tensor_copy(split[:, :, part, D:HROW], term[:, part, :, :])
                    ve.drain()
                    if part < 2:
                        nc.vector.tensor_tensor(term[:, part + 1, :, :], term[:, part, :, :], split[:, :, part, D:HROW], ALU.subtract)
                        ve.drain()


def scores(nc, c, e, split, h_d, saved_d, slot_d, coef, score):
    turns = Q // SLOTS
    HP = HALF // 2
    PARTS = 3
    W = PARTS * HEADS
    with Names(nc, "scores") as m:
        g = Gather(m, HROW)
        lanes = m.sb("lanes", [P, 2, HALF * P], FP16)
        minus = m.sb("minus", [P, 2, HALF * P], BF16)
        node = m.sb("node", [P, PAIRS, 2, PARTS, HROW], BF16)
        size = m.sb("size", [P, HP, 2, KD, P])
        slope = m.sb("slope", [P, HP, 2, KD, P])
        joint = m.sb("joint", [P, HP, 2, P])
        ends = m.sb("ends", [P, 2, HALF, HEADS])
        total = m.sb("total", [P, HALF, HEADS])
        diff_ps = [m.ps(f"diff_ps{s}") for s in range(HP)]
        sum_ps = [m.ps(f"sum_ps{s}") for s in range(2)]
        lanes_in = [m.sem(f"lanes_in{s}") for s in range(2)]
        saved = [m.sem(f"saved{s}") for s in range(2)]
        minus_ready, staged, diffed, absed, sized, joined, multiplied, reduced, kept, summed, tick = (
            m.sem(n) for n in ("minus_ready", "staged", "diffed", "absed", "sized", "joined", "multiplied", "reduced", "kept", "summed", "tick"))

        def chunk(row, f):
            return row[:, f:D:KD]

        with nc.Block() as block:
            @block.sync
            def _(sp):
                with sp.Fori(0, turns) as i:
                    for f in range(2):
                        sp.wait_ge(minus_ready, 2 * i + f + 1)
                        sp.dma_start(lanes[:, f, :], slot_d[bass.ds((2 * i + f) * HALF, HALF), :].rearrange("c e -> (c e)").partition_broadcast(P)).then_inc(lanes_in[f], 16)
                        for p in range(f * HP, (f + 1) * HP):
                            mine = slice(2 * p % HALF * HROW, (2 * p % HALF + 2) * HROW)
                            sp.wait_ge(g.landed[p], 32 * i + 32)
                            sp.dma_start(saved_d[bass.ds(2 * i + f, 1), :, mine].rearrange("o p w -> p (o w)"),
                                         g.rows[:, 2 * p:2 * p + 2, :].rearrange("p s w -> p (s w)")).then_inc(saved[f], 16)
                for f in range(2):
                    sp.wait_ge(saved[f], 16 * HP * turns)

            @block.gpsimd
            def _(pool):
                g.pool(nc, pool, e, h_d)

            @block.tensor
            def _(pe):
                def differ(i, p):
                    if p % HP == 0:
                        pe.wait_ge(minus_ready, 2 + 2 * i + p // HP + 1)
                    pe.wait_ge(g.landed[p], 32 * i + 32)
                    pe.wait_ge(staged, PAIRS * i + p + 1)
                    pe.wait_ge(absed, PAIRS * i + p + 1)
                    pe.sem_inc(tick, 1)
                    for j in range(2):
                        s = 2 * p + j
                        for f in range(KD):
                            out = diff_ps[p % HP][:, (KD * j + f) * P:(KD * j + f + 1) * P]
                            nc.tensor.matmul(out, chunk(g.rows[:, s, :], f), c["ident"][:, :], start=True, stop=False)
                            for part in range(PARTS):
                                last = nc.tensor.matmul(out, chunk(node[:, p, j, part, :], f), minus[:, s // HALF, s % HALF * P:(s % HALF + 1) * P],
                                                        start=False, stop=(part == PARTS - 1))
                    last.then_inc(diffed, 1)

                def reduce(i, p):
                    if p % HP == 0:
                        pe.wait_ge(kept, 2 * i + p // HP + 1)
                    pe.wait_ge(joined, HP + PAIRS * i + p + 1)
                    pe.sem_inc(tick, 1)
                    for j in range(2):
                        s, half = 2 * p + j, p // HP
                        out = sum_ps[half][:, s % HALF * W:(s % HALF + 1) * W]
                        nc.tensor.matmul(out, minus[:, half, s % HALF * P:(s % HALF + 1) * P], node[:, p, j, :, D:HROW], start=True, stop=False)
                        last = nc.tensor.matmul(out, joint[:, p % HP, j, :], c["by_head"][:, :], start=False, stop=True)
                    last.then_inc(reduced, 1)

                lead = 3
                pe.sem_inc(reduced, PAIRS)
                for p in range(lead):
                    differ(0, p)
                with pe.Fori(0, turns - 1) as i:
                    for p in range(PAIRS):
                        differ(*((i, p + lead) if p + lead < PAIRS else (i + 1, p + lead - PAIRS)))
                        reduce(i, p)
                for p in range(PAIRS):
                    if p + lead < PAIRS:
                        differ(turns - 1, p + lead)
                    reduce(turns - 1, p)

            @block.scalar
            def _(act):
                act.sem_inc(absed, HP)
                with act.Fori(0, turns) as i:
                    for p in range(PAIRS):
                        act.wait_ge(diffed, PAIRS * i + p + 1)
                        act.wait_ge(joined, PAIRS * i + p + 1)
                        act.sem_inc(tick, 1)
                        nc.scalar.activation(size[:, p % HP, :, :, :].rearrange("p j f e -> p (j f e)"), diff_ps[p % HP][:, :], ACT.Abs).then_inc(absed, 1)
                        if p % HP == HP - 1:
                            half = p // HP
                            act.wait_ge(kept, 2 * i + half + 1)
                            act.wait_ge(saved[half], 16 * HP * i + 16 * HP)
                            act.sem_inc(tick, 1)
                            nc.scalar.activation(ends[:, half, :, :], g.rows[:, half * HALF:(half + 1) * HALF, D:HROW], ACT.Copy).then_inc(g.freed, 1)
                        act.wait_ge(absed, HP + PAIRS * i + p + 1)
                        act.sem_inc(tick, 1)
                        for f in range(KD):
                            last = nc.scalar.activation(slope[:, p % HP, :, f, :], size[:, p % HP, :, f, :], ACT.Identity,
                                                        bias=coef[:, 0, f:f + 1], scale=coef[:, 1, f:f + 1])
                        last.then_inc(sized, 1)

            @block.vector
            def _(ve):
                def keep(half, f):
                    ve.wait_ge(reduced, PAIRS + half * HP + HP)
                    ve.sem_inc(tick, 1)
                    nc.vector.tensor_reduce(total[:, :, :], sum_ps[f][:, 0:HALF * W].rearrange("p (s k h) -> p s h k", h=HEADS, k=PARTS), AX, ALU.add).then_inc(summed, 1)
                    ve.wait_ge(summed, half + 1)
                    ve.wait_ge(g.freed, 2 + half + 1)
                    ve.sem_inc(tick, 1)
                    nc.vector.tensor_tensor(score[:, bass.ds(half * (HALF * HEADS), HALF * HEADS)].rearrange("p (s h) -> p s h", h=HEADS),
                                            total[:, :, :], ends[:, f, :, :], ALU.add).then_inc(kept, 1)

                def choose(i, f):
                    ve.wait_ge(lanes_in[f], 16 * i + 16)
                    ve.sem_inc(tick, 1)
                    nc.vector.tensor_scalar(minus[:, f, :], lanes[:, f, :], c["lane_f"][:, 0:1], -1.0, ALU.is_equal, ALU.mult).then_inc(minus_ready, 1)

                def stage(i, p, tiles):
                    ve.wait_ge(reduced, PAIRS * i + p + 1)
                    ve.sem_inc(tick, 1)
                    for j in range(2):
                        last = nc.vector.tensor_copy(node[:, p, j, :, :].rearrange("p k d -> p (k d)"),
                                                     split[:, bass.ds(tiles[2 * (p % HP) + j], 1), :, :].rearrange("p t k d -> p (t k d)"))
                    last.then_inc(staged, 1)

                def multiply(i, p):
                    ve.wait_ge(sized, PAIRS * i + p + 1)
                    ve.sem_inc(tick, 1)
                    mine = size[:, p % HP, :, :, :]
                    nc.vector.tensor_tensor(mine, mine, slope[:, p % HP, :, :, :], ALU.mult).then_inc(multiplied, 1)

                def join(i, p):
                    ve.wait_ge(multiplied, PAIRS * i + p + 1)
                    ve.wait_ge(reduced, PAIRS - HP + PAIRS * i + p + 1)
                    ve.sem_inc(tick, 1)
                    nc.vector.tensor_tensor(joint[:, p % HP, :, :], size[:, p % HP, :, 0, :], size[:, p % HP, :, 1, :], ALU.add).then_inc(joined, 1)

                def half(i, f, first=False, last=False):
                    more = not (last and f)
                    nxt, other = i + f, 1 - f
                    ahead = {1: (0,), 2: (1, 2), 3: (3,), 4: (4,)}
                    for p in range(HP):
                        multiply(i, f * HP + p)
                        if p == 1:
                            if not (first and f == 0):
                                keep(2 * i + f - 1, other)
                            if more:
                                choose(nxt, other)
                                tiles = tiles_of(nc, nc.vector.engine, e, 2 * i + f + 1, HALF)
                        if more:
                            for q in ahead.get(p, ()):
                                stage(nxt, other * HP + q, tiles)
                        join(i, f * HP + p)

                nc.vector.memset(score[:, Q * HEADS:], 0.0)
                ve.sem_inc(g.freed, 2)
                ve.sem_inc(kept, 2)
                ve.sem_inc(minus_ready, 2)
                ve.sem_inc(joined, HP)
                tiles = tiles_of(nc, nc.vector.engine, e, 0, HALF)
                choose(0, 0)
                for p in range(HP):
                    stage(0, p, tiles)
                for f in range(2):
                    half(0, f, first=True)
                with ve.Fori(1, turns - 1) as i:
                    for f in range(2):
                        half(i, f)
                for f in range(2):
                    half(turns - 1, f, last=True)
                keep(2 * turns - 1, 1)
                ve.drain().then_inc(tick, 1)


def edge_softmax(nc, c, e, score):
    W = QP * HEADS
    BLK = W // P
    with Names(nc, "softmax") as m:
        slope = m.sb("slope", [P, W])
        node_h = m.sb("node_h", [P, W])
        turned = m.sb("turned", [P, W])
        change = m.sb("change", [P, W + 1])
        forth = m.sb("forth", [P, W])
        back = m.sb("back", [P, W])
        picks = m.sb("picks", [P, 2, P])
        ends = m.sb("ends", [P, 2, QP])
        joins = m.sb("joins", [P, QP + 1])
        whole = m.sb("whole", [P, QP])
        step = m.sb("step", [P, 2, QP])
        apart = m.sb("apart", [P, 2, QP])
        BANKS = 8
        ps = [m.ps(f"ps{s}") for s in range(BANKS)]
        lin, named, moved, scanned, topped, run, foreseen, bounded, exped = (
            m.sem(n) for n in ("lin", "named", "moved", "scanned", "topped", "run", "foreseen", "bounded", "exped"))
        G = BLK // 4
        emptied = [m.sem(f"emptied{s}") for s in range(2)]
        blocks = [slice(g * 512, (g + 1) * 512) for g in range(G)]
        copies = ([turned[:, b] for b in blocks] + [forth[:, b] for b in blocks] + [back[:, b] for b in blocks]
                  + [turned[:, b] for b in blocks] + [slope[:, b] for b in blocks] + [ends[:, j, :] for j in range(2)])

        def by_chunk(buffer):
            return buffer[:, :].rearrange("p (q h) -> p q h", h=HEADS)

        def wide(mask):
            return mask.unsqueeze(2).to_broadcast([P, QP - 1, HEADS])
        first_v, last_v = by_chunk(turned), by_chunk(slope)
        with nc.Block() as block:
            @block.gpsimd
            def _(pool):
                pool.wait_ge(run, HEADS)
                nc.gpsimd.memset(by_chunk(forth)[:, QP - 1, :], NEG).then_inc(foreseen, 1)
                nc.gpsimd.tensor_tensor(by_chunk(forth)[:, 0:QP - 1, :], first_v[:, 1:QP, :], wide(apart[:, 1, 0:QP - 1]), ALU.add).then_inc(foreseen, 1)

            @block.tensor
            def _(pe):
                n = 0

                def four(source, g):
                    nonlocal n
                    pe.wait_ge(emptied[n % 2], n // 2 + 1)
                    for j in range(4):
                        b = 4 * g + j
                        last = nc.tensor.transpose(ps[n % BANKS][:, j * P:(j + 1) * P], source[:, b * P:(b + 1) * P], c["ident"][:, :])
                    last.then_inc(moved, 1)
                    n += 1
                for g in range(G):
                    pe.wait_ge(lin, g + 1)
                    four(score, g)
                pe.wait_ge(named, 1)
                for g in range(G):
                    four(node_h, g)
                pe.wait_ge(scanned, 1)
                for g in range(G):
                    four(forth, g)
                pe.wait_ge(topped, 1)
                for j in range(2):
                    for g in range(G):
                        pe.wait_ge(emptied[n % 2], n // 2 + 1)
                        nc.tensor.matmul(ps[n % BANKS][:, :], picks[:, j, :], back[:, g * 512:(g + 1) * 512], start=True, stop=True).then_inc(moved, 1)
                        n += 1
                for j in range(2):
                    pe.wait_ge(emptied[n % 2], n // 2 + 1)
                    nc.tensor.matmul(ps[n % BANKS][:, 0:QP], picks[:, j, :], e["slot_node"][:, :], start=True, stop=True).then_inc(moved, 1)
                    n += 1

            @block.scalar
            def _(act):
                nc.scalar.activation(node_h[:, :].rearrange("p (q h) -> p q h", h=HEADS), e["slot_node"][:, :].unsqueeze(2).to_broadcast([P, QP, HEADS]), ACT.Copy).then_inc(named, 1)
                act.sem_inc(emptied[1], BANKS // 2)
                for n in range(1, len(copies), 2):
                    act.wait_ge(moved, n + 1)
                    nc.scalar.activation(copies[n], ps[n % BANKS][:, 0:copies[n].shape[1]], ACT.Copy).then_inc(emptied[1], 1)
                act.wait_ge(bounded, 1)
                nc.scalar.activation(score[:, :], score[:, :], ACT.Exp).then_inc(exped, 1)

            @block.vector
            def _(ve):
                def empty(first, last):
                    for n in range(first + first % 2, last, 2):
                        ve.wait_ge(moved, n + 1)
                        nc.vector.tensor_copy(copies[n], ps[n % BANKS][:, 0:copies[n].shape[1]]).then_inc(emptied[0], 1)
                    ve.wait_ge(emptied[1], BANKS // 2 + last // 2)
                    ve.drain()
                ve.sem_inc(emptied[0], BANKS // 2)
                for b in blocks:
                    nc.vector.scalar_tensor_tensor(score[:, b], score[:, b], SLOPE, score[:, b], ALU.mult, ALU.max).then_inc(lin, 1)
                for j, lane in enumerate((0, P - 1)):
                    nc.vector.tensor_copy(picks[:, j, :], c["ident"][:, lane:lane + 1].to_broadcast([P, P]))
                empty(0, 2 * G)
                nc.vector.tensor_tensor(change[:, 1:W], forth[:, 1:W], forth[:, 0:W - 1], ALU.not_equal)
                ve.drain()
                nc.vector.tensor_scalar(change[:, 1:W], change[:, 1:W], NEG, None, ALU.mult)
                ve.drain()
                nc.vector.memset(change[:, 0:W + 1:P], NEG)
                ve.drain()
                nc.vector.tensor_tensor_scan(forth[:, :], change[:, 0:W], turned[:, :], NEG, ALU.add, ALU.max)
                nc.vector.tensor_tensor_scan(back[:, ::-1], change[:, W:0:-1], turned[:, ::-1], NEG, ALU.add, ALU.max)
                ve.drain()
                nc.vector.tensor_tensor(forth[:, :], forth[:, :], back[:, :], ALU.max).then_inc(scanned, 1)
                empty(2 * G, 3 * G)
                ve.drain().then_inc(topped, 1)
                top = back
                empty(3 * G, len(copies))
                nc.vector.memset(joins[:, :], NEG)
                ve.drain()
                nc.vector.tensor_tensor(joins[:, 1:QP], ends[:, 0, 1:QP], ends[:, 1, 0:QP - 1], ALU.not_equal)
                nc.vector.tensor_tensor(whole[:, :], ends[:, 0, :], ends[:, 1, :], ALU.not_equal)
                for j in range(2):
                    nc.vector.tensor_tensor(apart[:, j, :], e["slot_node"][:, :], ends[:, j, :], ALU.not_equal)
                ve.drain()
                nc.vector.tensor_scalar(joins[:, 1:QP], joins[:, 1:QP], NEG, None, ALU.mult)
                nc.vector.tensor_scalar(whole[:, :], whole[:, :], NEG, None, ALU.mult)
                nc.vector.tensor_scalar(apart[:, :, :], apart[:, :, :], NEG, None, ALU.mult)
                ve.drain()
                nc.vector.tensor_tensor(step[:, 0, :], joins[:, 0:QP], whole[:, :], ALU.min)
                nc.vector.tensor_tensor(step[:, 1, :], joins[:, 1:QP + 1], whole[:, :], ALU.min)
                nc.vector.tensor_tensor(apart[:, 0, 1:QP], apart[:, 0, 1:QP], joins[:, 1:QP], ALU.min)
                nc.vector.tensor_tensor(apart[:, 1, 0:QP - 1], apart[:, 1, 0:QP - 1], joins[:, 1:QP], ALU.min)
                ve.drain()
                for hd in range(HEADS):
                    nc.vector.tensor_tensor_scan(first_v[:, ::-1, hd], step[:, 1, ::-1], first_v[:, ::-1, hd], NEG, ALU.add, ALU.max).then_inc(run, 1)
                for hd in range(HEADS):
                    nc.vector.tensor_tensor_scan(last_v[:, :, hd], step[:, 0, :], last_v[:, :, hd], NEG, ALU.add, ALU.max)
                ve.drain()
                carry = by_chunk(node_h)
                nc.vector.memset(carry[:, 0, :], NEG)
                nc.vector.tensor_tensor(carry[:, 1:QP, :], last_v[:, 0:QP - 1, :], wide(apart[:, 0, 1:QP]), ALU.add)
                ve.drain()
                nc.vector.tensor_tensor(top[:, :], top[:, :], node_h[:, :], ALU.max)
                ve.drain()
                ve.wait_ge(foreseen, 2)
                nc.vector.tensor_tensor(top[:, :], top[:, :], forth[:, :], ALU.max)
                ve.drain()
                nc.vector.tensor_tensor(score[:, :], score[:, :], top[:, :], ALU.subtract).then_inc(bounded, 1)
                ve.wait_ge(exped, 1)


def attend(nc, x, acc):
    with Names(nc, "attend") as m:
        per = m.sb("per", [P, NT, HEADS])
        end = m.sem("end")
        acc_v = acc[:, :].rearrange("p (t d) -> p t d", d=HROW)
        with nc.Block() as block:
            @block.vector
            def _(ve):
                nc.vector.tensor_scalar(per[:, :, :], acc_v[:, :, D:HROW], 1e-16, None, ALU.add)
                ve.drain()
                nc.vector.reciprocal(per[:, :, :], per[:, :, :])
                ve.drain()
                for hd in range(HEADS):
                    mine = acc_v[:, :, hd * HD:(hd + 1) * HD]
                    nc.vector.tensor_tensor(mine, mine, per[:, :, hd].unsqueeze(2).to_broadcast([P, NT, HD]), ALU.mult)
                ve.drain()
                nc.vector.tensor_tensor(x[:, :, :], x[:, :, :], acc_v[:, :, 0:D], ALU.add).then_inc(end, 1)
                ve.wait_ge(end, 1)


def feed_forward(nc, layer, c, a, x, xs_d, dram, out):
    tag, EX, H, NB = layer["name"], layer["experts"], layer["hidden"], layer["blocks"]
    with Names(nc, f"ffn{tag}") as m:
        r = dict(weight=m.sb("weight", [P, TOP, NT]), owner=m.sb("owner", [1, NB], I32))
        ys_d = dram(f"ys_{tag}", [TOP * (N + 1), D])
        first = tag == "L0"
        z_d = None if first else dram(f"z_{tag}", [NR, D])
        gate, bias = (a["L0_ffn_Wr"], a["L0_ffn_br"]) if first else (a["L1_ffn_gate_w"], a["L1_ffn_gate_b"])
        with Names(nc, f"weights{tag}") as k:
            w = dict(first=k.sb("w1", [P, EX * KD * H]), second=k.sb("w2", [P, EX * H // P * D]), landed=k.sem("landed"))
            route(nc, layer, c, a, x, r, w, gate, bias, z_d, xs_d, first)
            experts(nc, layer, c, a, r, w, xs_d, ys_d)
        if first:
            combine(nc, layer, r, ys_d, x, None)
        else:
            with Names(nc, "last") as k:
                z = k.sb("z", [P, NT, D])
                combine(nc, layer, r, ys_d, z, lambda mm: Finish(nc, mm, a, x, z, z_d, out))


def build(nc, a, out):
    with Names.whole, Names(nc, "all") as keep:
        def dram(name, shape, dt=F32):
            return nc.dram_tensor(name, shape, dt, kind="Internal").ap()

        sb = keep.sb
        c = dict(ident=sb("ident", [P, P]), before=sb("before", [P, P]), ones=sb("ones", [P, P]), before_b=sb("before_b", [P, P], BF16), ones_b=sb("ones_b", [P, P], BF16),
                 count_f=sb("count_f", [P, P]), lane_f=sb("lane_f", [P, 1]), by_head=sb("by_head", [P, 3 * HEADS]))
        e = dict(degree=sb("degree", [P, NT]), tiles=sb("tiles", [1, Q // PACK], I32),
                 slot_dst=sb("slot_dst", [P, QP], I32), slot_src=sb("slot_src", [P, QP]), slot_node=sb("slot_node", [P, QP]))
        x = sb("x", [P, NT, D])
        slot_d = dram("slot_lanes", [QP, P], FP16)
        slots = {layer["name"]: dram(f"xs_{layer['name']}", [layer["blocks"] * P, XROW]) for layer in LAYERS}
        with Names(nc, "gnn0") as m:
            c.update(upto=m.sb("upto", [P, P]), count_h=m.sb("count_h", [P, QP], FP16), count_b=m.sb("count_b", [P, P], BF16))
            constants(nc, c)
            z_d = dram("z_gnn0", [NR, D])
            first_norm(nc, a["x"], x, z_d)
            with Names(nc, "edges") as k:
                o = dict(low_f=k.sb("low_f", [P, EC]), dst_f=k.sb("dst_f", [P, EC]), pos_q=k.sb("pos_q", [P, EC]),
                         pos_r=k.sb("pos_r", [P, EC]), tile_f=k.sb("tile_f", [P, QP]))
                sort_edges(nc, c, e, o, a["src"], a["dst"], dram("low_lanes", [EC, P], BF16))
                place_edges(nc, c, e, o, slot_d)
            acc = m.sb("acc", [P, NT * HROW])
            with Names(nc, "mean_in") as k:
                inputs = MeanInputs(nc, k, a, x, z_d)
                aggregate(nc, "sum0", c, e, z_d, D, acc, slots["L0"], ahead=inputs)
                mean_layer(nc, c, e, x, inputs, acc)
        feed_forward(nc, LAYERS[0], c, a, x, slots["L0"], dram, out)
        with Names(nc, "gnn1") as m:
            score = m.sb("score", [P, QP * HEADS])
            h_d = dram("h_gnn1", [NR, HROW])
            saved_d = dram("saved_gnn1", [Q // HALF, P, HALF * HROW])
            with Names(nc, "gnn1a") as k:
                split = k.sb("split", [P, NT, 3, HROW], BF16)
                coef = k.sb("coef", [P, 2, KD])
                heads(nc, c, a, x, split, h_d, coef)
                scores(nc, c, e, split, h_d, saved_d, slot_d, coef, score)
            edge_softmax(nc, c, e, score)
            acc = m.sb("acc1", [P, NT * HROW])
            aggregate(nc, "sum1", c, e, None, HROW, acc, slots["L1"], score, saved_d)
            attend(nc, x, acc)
        feed_forward(nc, LAYERS[1], c, a, x, slots["L1"], dram, out)


def kernel(**inputs):
    import numpy as np
    import concourse.bacc as bacc
    from concourse.bass_utils import run_bass_kernel_spmd

    laid = dict(inputs)
    for name in ("L0_gnn_W1", "L0_gnn_W2"):
        laid[name] = np.transpose(laid[name])
    laid["L1_gnn_W"] = np.transpose(laid["L1_gnn_W"], (1, 0, 2)).reshape(D, HEADS * HD)

    def on_partitions(v):
        return np.transpose(np.reshape(v, (v.shape[0], -1, P)), (2, 0, 1))
    for name in ("L0_ffn_b1", "L1_ffn_b1", "L0_ffn_ln_g", "L0_ffn_ln_b"):
        laid[name] = on_partitions(np.asarray(laid[name]))
    nc = bacc.Bacc("TRN2", target_bir_lowering=False, num_devices=1)
    arrays, args = {}, {}
    for name, v in laid.items():
        v = np.ascontiguousarray(v)
        arrays[f"in_{name}"] = v
        args[name] = nc.dram_tensor(f"in_{name}", v.shape, mybir.dt.from_np(v.dtype), kind="ExternalInput").ap()
    out = nc.dram_tensor("out_x", (N, D), F32, kind="ExternalOutput").ap()
    build(nc, args, out)
    return run_bass_kernel_spmd(nc, [arrays], core_ids=[0]).results[0]["out_x"]
```
